# Optimizing a Trainium2 kernel written in Bass

```python
import numpy as np
import jax
import jax.numpy as jnp

def _softmax(x, axis=-1):
    return jax.nn.softmax(x, axis=axis)

def _gelu(x):
    return jax.nn.gelu(x, approximate=True)

def _silu(x):
    return jax.nn.silu(x)

def _sigmoid(x):
    return jax.nn.sigmoid(x)

def _layernorm(x, axis=-1, eps=1e-05):
    m = jnp.mean(x, axis=axis, keepdims=True)
    v = jnp.var(x, axis=axis, keepdims=True)
    return (x - m) / jnp.sqrt(v + eps)

def _scatter_add(tgt, idx, src, axis=0):
    return tgt.at[idx].add(src)

def _segment_sum(src, seg, n):
    return jax.ops.segment_sum(src, seg, n)
kernel_name = 'mk_gnn_ffn_d2_gnn_r32_12fd2e'

def setup_inputs(seed: int=0):
    np.random.seed(seed)
    _w = jnp.asarray

    def _rec_inputs():
        import jax
        import jax.numpy as jnp
        _gk = jax.random.key(seed)
        x = -0.0003713 + 1 * jax.random.normal(jax.random.fold_in(_gk, 1), (3125, 256), jnp.float32)
        src = jax.random.randint(jax.random.fold_in(_gk, 2), (50000,), 0, 3125, jnp.int32)
        dst = jax.random.randint(jax.random.fold_in(_gk, 3), (50000,), 0, 3125, jnp.int32)
        _o = jnp.argsort(dst, stable=True)
        src = src[_o]
        dst = dst[_o]
        return (x, src, dst)
    x, src, dst = _rec_inputs()

    def _L0_gnn_setup():
        import jax, jax.numpy as jnp
        import numpy as np
        N, E, D_IN, D_OUT = (50000, 50000, 256, 256)
        key = jax.random.key(seed)
        k1, k2, k3, k4, k5, k6 = jax.random.split(key, 6)
        x = jax.random.normal(k1, (N, D_IN), dtype=jnp.float32)
        edge_index = jax.random.randint(k2, (2, E), 0, N, dtype=jnp.int64)
        s = 1.0 / np.sqrt(D_IN)
        W1 = jax.random.uniform(k3, (D_OUT, D_IN), minval=-s, maxval=s, dtype=jnp.float32)
        b1 = jax.random.uniform(k4, (D_OUT,), minval=-s, maxval=s, dtype=jnp.float32)
        W2 = jax.random.uniform(k5, (D_OUT, D_IN), minval=-s, maxval=s, dtype=jnp.float32)
        b2 = jax.random.uniform(k6, (D_OUT,), minval=-s, maxval=s, dtype=jnp.float32)
        return {'x': x, 'W1': W1, 'b1': b1, 'W2': W2, 'b2': b2, 'edge_index': edge_index}
    _L0_gnn_all = _L0_gnn_setup()
    _L0_gnn_in = {k: v for k, v in _L0_gnn_all.items() if k in ('W1', 'b1', 'W2', 'b2')}
    del _L0_gnn_all

    def _L0_ffn_setup():
        import jax, jax.numpy as jnp
        import numpy as np
        DIM = 256
        H = 8
        D = 64
        G = 64
        INNER = H * D
        SCALE = D ** (-0.5)
        key = jax.random.key(seed)
        ks = jax.random.split(key, 12)
        B, N = (4, 512)
        x = jax.random.normal(ks[0], (B, N, DIM), dtype=jnp.float32)
        s = lambda fan_in: 1.0 / np.sqrt(fan_in)
        W_fx = jax.random.normal(ks[1], (DIM, INNER), dtype=jnp.float32) * s(DIM)
        b_fx = jnp.zeros((INNER,), dtype=jnp.float32)
        W_x = jax.random.normal(ks[2], (DIM, INNER), dtype=jnp.float32) * s(DIM)
        b_x = jnp.zeros((INNER,), dtype=jnp.float32)
        A = jax.random.normal(ks[3], (G, D), dtype=jnp.float32)
        Q, _ = jnp.linalg.qr(A.T)
        W_slice = Q[:, :G].astype(jnp.float32)
        b_slice = jnp.zeros((G,), dtype=jnp.float32)
        W_q = jax.random.normal(ks[4], (D, D), dtype=jnp.float32) * s(D)
        W_k = jax.random.normal(ks[5], (D, D), dtype=jnp.float32) * s(D)
        W_v = jax.random.normal(ks[6], (D, D), dtype=jnp.float32) * s(D)
        W_out = jax.random.normal(ks[7], (INNER, DIM), dtype=jnp.float32) * s(INNER)
        b_out = jnp.zeros((DIM,), dtype=jnp.float32)
        temperature = jnp.ones((1, H, 1, 1), dtype=jnp.float32) * 0.5
        return {'x': x, 'W_fx': W_fx, 'b_fx': b_fx, 'W_x': W_x, 'b_x': b_x, 'W_slice': W_slice, 'b_slice': b_slice, 'W_q': W_q, 'W_k': W_k, 'W_v': W_v, 'W_out': W_out, 'b_out': b_out, 'temperature': temperature}
    _L0_ffn_all = _L0_ffn_setup()
    _L0_ffn_in = {k: v for k, v in _L0_ffn_all.items() if k in ('W_fx', 'b_fx', 'W_x', 'b_x', 'W_slice', 'b_slice', 'W_q', 'W_k', 'W_v', 'W_out', 'b_out', 'temperature')}
    del _L0_ffn_all

    def _L1_gnn_setup():
        import jax, jax.numpy as jnp
        import numpy as np
        import math
        N_NODES = 50000
        N_EDGES = 50000
        C = 256
        H = 8
        HD = C // H

        def _layernorm(x, g, b, eps=1e-05):
            mu = jnp.mean(x, axis=-1, keepdims=True)
            var = jnp.mean(jnp.square(x - mu), axis=-1, keepdims=True)
            return (x - mu) * jax.lax.rsqrt(var + eps) * g + b
        key = jax.random.key(seed)
        ks = jax.random.split(key, 16)
        s = 0.02
        d = {'feat': jax.random.normal(ks[0], (N_NODES, C), jnp.float32), 'edge_src': jax.random.randint(ks[1], (N_EDGES,), 0, N_NODES), 'edge_dst': jax.random.randint(ks[2], (N_EDGES,), 0, N_NODES), 'Wq': jax.random.normal(ks[3], (C, C), jnp.float32) * s, 'bq': jnp.zeros((C,), jnp.float32), 'Wk': jax.random.normal(ks[4], (C, C), jnp.float32) * s, 'bk': jnp.zeros((C,), jnp.float32), 'Wv': jax.random.normal(ks[5], (C, C), jnp.float32) * s, 'bv': jnp.zeros((C,), jnp.float32), 'Wp': jax.random.normal(ks[6], (C, C), jnp.float32) * s, 'bp': jnp.zeros((C,), jnp.float32), 'ln_g': jnp.ones((C,), jnp.float32), 'ln_b': jnp.zeros((C,), jnp.float32), 'W1': jax.random.normal(ks[7], (4 * C, C), jnp.float32) * s, 'b1': jnp.zeros((4 * C,), jnp.float32), 'W2': jax.random.normal(ks[8], (C, 4 * C), jnp.float32) * s, 'b2': jnp.zeros((C,), jnp.float32)}
        return d
    _L1_gnn_all = _L1_gnn_setup()
    _L1_gnn_in = {k: v for k, v in _L1_gnn_all.items() if k in ('Wq', 'bq', 'Wk', 'bk', 'Wv', 'bv', 'Wp', 'bp', 'ln_g', 'ln_b', 'W1', 'b1', 'W2', 'b2')}
    del _L1_gnn_all

    def _L1_ffn_setup():
        import jax, jax.numpy as jnp
        import numpy as np
        B, K, D = (512, 16, 256)
        E = 32
        H = int(D * 0.25)
        key = jax.random.key(seed)
        ks = jax.random.split(key, 7)
        d_rs = D ** (-0.5)
        h_rs = H ** (-0.5)
        x = jax.random.normal(ks[0], (B, K, D), dtype=jnp.float32)
        router_w = jax.random.uniform(ks[1], (E, D), jnp.float32, -d_rs, d_rs)
        router_b = jax.random.uniform(ks[2], (E,), jnp.float32, -d_rs, d_rs)
        W1 = jax.random.uniform(ks[3], (E, D, H), jnp.float32, -h_rs, h_rs)
        b1 = jax.random.uniform(ks[4], (E, H), jnp.float32, -h_rs, h_rs)
        W2 = jax.random.uniform(ks[5], (E, H, D), jnp.float32, -d_rs, d_rs)
        b2 = jax.random.uniform(ks[6], (E, D), jnp.float32, -d_rs, d_rs)
        return {'x': x, 'router_w': router_w, 'router_b': router_b, 'W1': W1, 'b1': b1, 'W2': W2, 'b2': b2}
    _L1_ffn_all = _L1_ffn_setup()
    _L1_ffn_in = {k: v for k, v in _L1_ffn_all.items() if k in ('router_w', 'router_b', 'W1', 'b1', 'W2', 'b2')}
    del _L1_ffn_all
    return {'x': x, 'src': src, 'dst': dst, 'L0_gnn_W1': _L0_gnn_in['W1'], 'L0_gnn_b1': _L0_gnn_in['b1'], 'L0_gnn_W2': _L0_gnn_in['W2'], 'L0_gnn_b2': _L0_gnn_in['b2'], 'L0_ffn_W_fx': _L0_ffn_in['W_fx'], 'L0_ffn_b_fx': _L0_ffn_in['b_fx'], 'L0_ffn_W_x': _L0_ffn_in['W_x'], 'L0_ffn_b_x': _L0_ffn_in['b_x'], 'L0_ffn_W_slice': _L0_ffn_in['W_slice'], 'L0_ffn_b_slice': _L0_ffn_in['b_slice'], 'L0_ffn_W_q': _L0_ffn_in['W_q'], 'L0_ffn_W_k': _L0_ffn_in['W_k'], 'L0_ffn_W_v': _L0_ffn_in['W_v'], 'L0_ffn_W_out': _L0_ffn_in['W_out'], 'L0_ffn_b_out': _L0_ffn_in['b_out'], 'L0_ffn_temperature': _L0_ffn_in['temperature'], 'L1_gnn_Wq': _L1_gnn_in['Wq'], 'L1_gnn_bq': _L1_gnn_in['bq'], 'L1_gnn_Wk': _L1_gnn_in['Wk'], 'L1_gnn_bk': _L1_gnn_in['bk'], 'L1_gnn_Wv': _L1_gnn_in['Wv'], 'L1_gnn_bv': _L1_gnn_in['bv'], 'L1_gnn_Wp': _L1_gnn_in['Wp'], 'L1_gnn_bp': _L1_gnn_in['bp'], 'L1_gnn_ln_g': _L1_gnn_in['ln_g'], 'L1_gnn_ln_b': _L1_gnn_in['ln_b'], 'L1_gnn_W1': _L1_gnn_in['W1'], 'L1_gnn_b1': _L1_gnn_in['b1'], 'L1_gnn_W2': _L1_gnn_in['W2'], 'L1_gnn_b2': _L1_gnn_in['b2'], 'L1_ffn_router_w': _L1_ffn_in['router_w'], 'L1_ffn_router_b': _L1_ffn_in['router_b'], 'L1_ffn_W1': _L1_ffn_in['W1'], 'L1_ffn_b1': _L1_ffn_in['b1'], 'L1_ffn_W2': _L1_ffn_in['W2'], 'L1_ffn_b2': _L1_ffn_in['b2']}

def reference(x, src, dst, L0_gnn_W1, L0_gnn_b1, L0_gnn_W2, L0_gnn_b2, L0_ffn_W_fx, L0_ffn_b_fx, L0_ffn_W_x, L0_ffn_b_x, L0_ffn_W_slice, L0_ffn_b_slice, L0_ffn_W_q, L0_ffn_W_k, L0_ffn_W_v, L0_ffn_W_out, L0_ffn_b_out, L0_ffn_temperature, L1_gnn_Wq, L1_gnn_bq, L1_gnn_Wk, L1_gnn_bk, L1_gnn_Wv, L1_gnn_bv, L1_gnn_Wp, L1_gnn_bp, L1_gnn_ln_g, L1_gnn_ln_b, L1_gnn_W1, L1_gnn_b1, L1_gnn_W2, L1_gnn_b2, L1_ffn_router_w, L1_ffn_router_b, L1_ffn_W1, L1_ffn_b1, L1_ffn_W2, L1_ffn_b2):
    import jax
    import jax.numpy as jnp

    def _L0_gnn_ref(x, W1, b1, W2, b2, edge_index):
        import jax, jax.numpy as jnp
        import numpy as np
        N, E, D_IN, D_OUT = (50000, 50000, 256, 256)
        dst = edge_index[0]
        nbr = edge_index[1]
        n = x.shape[0]
        agg = jax.ops.segment_sum(x[nbr], dst, num_segments=n)
        cnt = jax.ops.segment_sum(jnp.ones((nbr.shape[0],), x.dtype), dst, num_segments=n)
        mean = agg / jnp.maximum(cnt, 1.0)[:, None]
        return x @ W1.T + b1 + mean @ W2.T + b2

    def _L0_ffn_ref(x, W_fx, b_fx, W_x, b_x, W_slice, b_slice, W_q, W_k, W_v, W_out, b_out, temperature):
        import jax, jax.numpy as jnp
        import numpy as np
        DIM = 256
        H = 8
        D = 64
        G = 64
        INNER = H * D
        SCALE = D ** (-0.5)
        B, N, _ = x.shape
        fx_mid = (x @ W_fx + b_fx).reshape(B, N, H, D).transpose(0, 2, 1, 3)
        x_mid = (x @ W_x + b_x).reshape(B, N, H, D).transpose(0, 2, 1, 3)
        temp = jnp.clip(temperature, 0.1, 5.0)
        slice_weights = jax.nn.softmax((x_mid @ W_slice + b_slice) / temp, axis=-1)
        slice_norm = slice_weights.sum(axis=2)
        slice_token = jnp.einsum('bhnc,bhng->bhgc', fx_mid, slice_weights)
        slice_token = slice_token / (slice_norm[..., None] + 1e-05)
        q = slice_token @ W_q
        k = slice_token @ W_k
        v = slice_token @ W_v
        attn = jax.nn.softmax(jnp.einsum('bhgc,bhkc->bhgk', q, k) * SCALE, axis=-1)
        out_slice = jnp.einsum('bhgk,bhkc->bhgc', attn, v)
        out_x = jnp.einsum('bhgc,bhng->bhnc', out_slice, slice_weights)
        out_x = out_x.transpose(0, 2, 1, 3).reshape(B, N, INNER)
        return out_x @ W_out + b_out

    def _L1_gnn_ref(feat, edge_src, edge_dst, Wq, bq, Wk, bk, Wv, bv, Wp, bp, ln_g, ln_b, W1, b1, W2, b2):
        import jax, jax.numpy as jnp
        import numpy as np
        import math
        N_NODES = 50000
        N_EDGES = 50000
        C = 256
        H = 8
        HD = C // H

        def _layernorm(x, g, b, eps=1e-05):
            mu = jnp.mean(x, axis=-1, keepdims=True)
            var = jnp.mean(jnp.square(x - mu), axis=-1, keepdims=True)
            return (x - mu) * jax.lax.rsqrt(var + eps) * g + b
        n = feat.shape[0]
        q = (feat @ Wq.T + bq).reshape(n, H, HD)
        k = (feat @ Wk.T + bk).reshape(n, H, HD)
        v = (feat @ Wv.T + bv).reshape(n, H, HD)
        score = jnp.einsum('ehd,ehd->eh', q[edge_dst], k[edge_src])
        score = jnp.clip(score / math.sqrt(HD), -10.0, 10.0)
        smax = jax.ops.segment_max(score, edge_dst, num_segments=n)
        smax = jnp.where(jnp.isfinite(smax), smax, 0.0)
        ex = jnp.exp(score - smax[edge_dst])
        den = jax.ops.segment_sum(ex, edge_dst, num_segments=n)
        alpha = ex / den[edge_dst]
        wv = jax.ops.segment_sum(alpha[:, :, None] * v[edge_src], edge_dst, num_segments=n).reshape(n, C)
        y = wv @ Wp.T + bp
        x = feat + y
        h = _layernorm(x, ln_g, ln_b)
        h = jax.nn.gelu(h @ W1.T + b1, approximate=False) @ W2.T + b2
        return x + h

    def _L1_ffn_ref(x, router_w, router_b, W1, b1, W2, b2):
        import jax, jax.numpy as jnp
        import numpy as np
        B, K, D = (512, 16, 256)
        E = 32
        H = int(D * 0.25)
        xf = x.reshape(-1, D)
        logits = xf @ router_w.T + router_b
        idx = jnp.argmax(logits, axis=-1)
        w1t = jnp.take(W1, idx, axis=0)
        h = jnp.einsum('nd,ndh->nh', xf, w1t) + jnp.take(b1, idx, axis=0)
        h = jax.nn.relu(h)
        w2t = jnp.take(W2, idx, axis=0)
        out = jnp.einsum('nh,nhd->nd', h, w2t) + jnp.take(b2, idx, axis=0)
        out = jax.nn.relu(out)
        return out.reshape(x.shape)
    edge_index = jnp.stack([src, dst])
    x = x + _L0_gnn_ref(_layernorm(x, axis=-1), L0_gnn_W1, L0_gnn_b1, L0_gnn_W2, L0_gnn_b2, edge_index)
    x = x + _L0_ffn_ref(_layernorm(x, axis=-1)[None], L0_ffn_W_fx, L0_ffn_b_fx, L0_ffn_W_x, L0_ffn_b_x, L0_ffn_W_slice, L0_ffn_b_slice, L0_ffn_W_q, L0_ffn_W_k, L0_ffn_W_v, L0_ffn_W_out, L0_ffn_b_out, L0_ffn_temperature)[0]
    x = x + _L1_gnn_ref(_layernorm(x, axis=-1), src, dst, L1_gnn_Wq, L1_gnn_bq, L1_gnn_Wk, L1_gnn_bk, L1_gnn_Wv, L1_gnn_bv, L1_gnn_Wp, L1_gnn_bp, L1_gnn_ln_g, L1_gnn_ln_b, L1_gnn_W1, L1_gnn_b1, L1_gnn_W2, L1_gnn_b2)
    x = x + _L1_ffn_ref(_layernorm(x, axis=-1)[None], L1_ffn_router_w, L1_ffn_router_b, L1_ffn_W1, L1_ffn_b1, L1_ffn_W2, L1_ffn_b2)[0]
    return x

_drawn_inputs = setup_inputs


def setup_inputs(seed=0):
    import zlib

    import numpy as np

    out = dict(_drawn_inputs(seed))
    spreads = {'L0_ffn_b_fx': (0.0, 0.1),
     'L0_ffn_b_x': (0.0, 0.8),
     'L0_ffn_b_slice': (0.0, 0.8),
     'L0_ffn_b_out': (0.0, 0.1),
     'L0_ffn_temperature': (0.5, 0.6),
     'L1_gnn_bq': (0.0, 0.8),
     'L1_gnn_bk': (0.0, 0.8),
     'L1_gnn_bv': (0.0, 0.484),
     'L1_gnn_bp': (0.0, 0.1),
     'L1_gnn_ln_g': (1.0, 0.6),
     'L1_gnn_ln_b': (0.0, 0.8),
     'L1_gnn_b1': (0.0, 0.407),
     'L1_gnn_b2': (0.0, 0.1)}
    factors = {'L0_ffn_W_x': 8.0,
     'L0_ffn_W_slice': 8.0,
     'L0_ffn_W_q': 8.0,
     'L0_ffn_W_k': 8.0,
     'L1_gnn_Wq': 8.0,
     'L1_gnn_Wk': 8.0,
     'L1_gnn_Wv': 3.452,
     'L1_ffn_router_b': 2.669,
     'L1_ffn_b1': 8.0,
     'L1_ffn_b2': 4.993}
    for name, (base, spread) in spreads.items():
        noise = np.random.default_rng([zlib.crc32(name.encode()), seed]).standard_normal(out[name].shape)
        drawn = base * np.exp(spread * noise) if base else spread * noise
        out[name] = jnp.asarray(drawn.astype(out[name].dtype))
    for name, factor in factors.items():
        out[name] = (out[name] * factor).astype(out[name].dtype)
    return out
```

```python
from contextlib import ExitStack

import numpy as np

import concourse.bass as bass
from concourse import mybir

F32 = mybir.dt.float32
BF16 = mybir.dt.bfloat16
I32 = mybir.dt.int32
U32 = mybir.dt.uint32
ALU = mybir.AluOpType
ACT = mybir.ActivationFunctionType
AX = mybir.AxisListType.X

P = 128
NODES = 3125
EDGES = 50000
C = 256
KC = C // P
TILES = -(-NODES // P)
ROWS = TILES * P
CHUNKS = -(-EDGES // P)
STEPS = CHUNKS + TILES - 1
STEP_UNROLL = 4
STEPS_RUN = -(-STEPS // STEP_UNROLL) * STEP_UNROLL
STEP_GROUPS = -(-(STEPS_RUN + 1) // P)
STEP_TABLE = STEP_GROUPS * P
PAD_DST = ROWS
U = STEP_UNROLL
MEAN_CHUNKS = -(-CHUNKS // U) * U
SUMW = C + 1
H0, D0, G0 = 8, 64, 64
INNER = H0 * D0
H1, D1 = 8, 32
ACCW = C + H1
MLP = 4 * C
MC = MLP // P
EXPERTS, HID = 32, C // 4
EC = EXPERTS * HID // P
EPS = 1e-5


def early(t, n):
    return isinstance(t, int) and t < n


def pipeline(eng, count, unroll, stages):
    depth = max(lag for lag, _ in stages)

    def turn(i, v):
        for lag, body in stages:
            if isinstance(i, int) and not 0 <= i - lag < count:
                continue
            body(i - lag, (v - lag) % unroll)

    head = -(-(depth + unroll) // unroll)
    last = count // unroll
    for i in range(head * unroll):
        turn(i, i % unroll)
    with eng.Fori(head, last) as g:
        for v in range(unroll):
            turn(g * unroll + v, v)
    for i in range(last * unroll, count + depth):
        turn(i, i % unroll)


def landed(t, slot, unroll):
    return (t - slot) * (16 // unroll) + 16


class Chain:

    def __init__(self, eng, sem, start, length):
        self.eng, self.sem, self.start, self.length, self.n = eng, sem, start, length, 0

    def __call__(self, ins):
        ins.then_inc(self.sem, 1)
        self.n += 1
        assert self.n <= self.length
        self.eng.wait_ge(self.sem, self.start + self.n)


def chain(eng, sem, length, at=0):
    return lambda t: Chain(eng, sem, length * t + at, length)



WEIGHTS = ["l0_w1t", "l0_w2t", "l0_fx", "l0_slice_out", "l1_qt", "l1_kvt", "l1_pt", "l1_w1t", "l1_w2t",
           "router_t", "moe_w1", "moe_b1", "moe_w2", "moe_b2", "w_slice", "w_q", "w_k", "w_v", "b_fx_row",
           "l1_b1", "ln_g", "ln_b"]
BIASES = ["b1", "b2", "b_slice", "b_out", "bq", "bkv", "bp", "b2m", "router_b", "temperature"]


def layer_norm(dve, carry_waits, link, row, stats, mean_var, rstd, out, stats_ready, rstd_ready, count, out_ready):
    carry_waits(dve)
    link(dve.bn_stats(stats, row))
    carry_waits(dve)
    dve.bn_aggr(mean_var, stats).then_inc(stats_ready, 1)
    dve.wait_ge(stats_ready, count)
    dve.wait_ge(rstd_ready, count)
    dve.tensor_scalar(out, row, mean_var[:, 0:1], rstd, ALU.subtract, ALU.mult).then_inc(out_ready, 1)


def build(nc, a, out):
    with ExitStack() as ctx:
        def sem(name):
            return ctx.enter_context(nc.semaphore(name))

        def sb(name, shape, dt=F32):
            return ctx.enter_context(nc.sbuf_tensor(name, shape, dt))

        def dram(name, shape):
            return nc.dram_tensor(name, shape, F32, kind="Internal").ap()

        xn_dram = dram("xn_rows", (ROWS, C))
        kv_dram = dram("kv_rows", (ROWS, 2 * C))
        sums_dram = [dram(f"first_end_sums{u}", (ROWS + P, SUMW)) for u in range(U)]
        wt_dram = dram("slice_weights_t", (TILES, P, INNER))
        xn_rows = xn_dram.rearrange("(t p) c -> p t c", p=P)
        kv_rows = kv_dram.rearrange("(t p) c -> p t c", p=P)
        wt_rows = wt_dram.rearrange("t p n -> p t n")
        out_rows = out.rearrange("(t p) c -> p t c", p=P)

        s_fence = sem("fence")

        def carry_waits(eng):
            eng.sem_inc(s_fence, 1)

        def fence(eng, signal, value):
            eng.wait_ge(signal, value)
            carry_waits(eng)

        bank = [ctx.enter_context(nc.psum_tensor(f"bank{i}", [P, 512], F32)) for i in range(8)]

        x = sb("x", [P, TILES, C])
        acc = sb("acc", [P, TILES * ACCW])
        q_tab = sb("q_tab", [P, TILES * C])
        ident = sb("ident", [P, P])
        iota_row = sb("iota_row", [P, P])
        ones = sb("ones", [P, P])
        neg_half = sb("neg_half", [P, 1])
        valid = sb("valid", [P, TILES])
        src_step = sb("src_step", [P, STEP_TABLE])
        dst_step = sb("dst_step", [P, STEP_TABLE])
        acc_off = sb("acc_off", [1, STEP_TABLE], I32)
        q_off = sb("q_off", [1, STEP_TABLE], I32)
        w = {name: sb("w_" + name, list(a[name].shape)) for name in WEIGHTS}
        bias = {name: sb("b_" + name, [P, a[name].shape[1]]) for name in BIASES}
        slice_out = sb("slice_out", [P, INNER // P, C])
        b1_mlp = sb("b1_mlp", [P, MC])
        w_logits = sb("w_logits", [P, KC, INNER])
        b_logits = sb("b_logits", [P, INNER])
        moe_mask = sb("moe_mask", [EXPERTS, EXPERTS * HID], BF16)
        countdown = sb("countdown", [P, EXPERTS])
        stats = sb("stats", [P, 3, 6])
        mean_var = sb("mean_var", [P, 3, 2])
        rstd = sb("rstd", [P, 3])

        norm_sems = [(sem(f"stats_ready{i}"), sem(f"rstd_ready{i}"), sem(f"var_eps{i}")) for i in range(3)]
        norms_before = [0, 0, 0]

        def normalize_stages(i):
            stats_ready, rstd_ready, pool_chain = norm_sems[i]
            base = norms_before[i]
            norms_before[i] += TILES
            st, mv, rs = stats[:, i, :], mean_var[:, i, :], rstd[:, i:i + 1]

            def pool_stage(pool):
                def body(t, u):
                    fence(pool, stats_ready, base + t + 1)
                    pool.tensor_scalar(rs, mv[:, 1:2], EPS, None, ALU.add).then_inc(pool_chain, 1)
                    pool.wait_ge(pool_chain, base + t + 1)
                    pool.tensor_tensor(rs, rs, neg_half[:], ALU.pow).then_inc(rstd_ready, 1)
                return body

            def dve_norm(dve, link, row, out, t, out_ready):
                layer_norm(dve, carry_waits, link, row, st, mv, rs, out, stats_ready, rstd_ready, base + t + 1, out_ready)
            return pool_stage, dve_norm

        s_x, s_w, s_rows = sem("x_in"), sem("weights_in"), sem("dst_rows_in")
        s_gathered = sem("step_rows_gathered")
        s_const, s_acc0 = sem("constants_ready"), sem("acc_zeroed")
        s_dchain, s_pchain = sem("table_chain_dve"), sem("table_chain_pool")
        s_below, s_bound = sem("chunk_ends_compared"), sem("tile_ends_counted")
        s_chunk, s_rel = sem("step_chunk_ready"), sem("step_rows_float")
        s_tr, s_tab = sem("step_rows_transposed"), sem("step_tables_ready")
        n_loads = 1 + len(WEIGHTS) + len(BIASES)
        JR = STEP_GROUPS

        with ExitStack() as scope:
            def sc(name, shape, dt=F32):
                return scope.enter_context(nc.sbuf_tensor(name, shape, dt))
            dst_i = sc("dst_i", [P, JR, P], I32)
            last_dst = sc("last_dst", [P, JR])
            iota_i = sc("iota_i", [P, P], I32)
            tile_no_i = sc("tile_no_i", [P, TILES - 1], I32)
            step_no_i = sc("step_no_i", [P, JR], I32)
            tile_end, tile_no = sc("tile_end", [P, TILES - 1]), sc("tile_no", [P, TILES - 1])
            step_no = sc("step_no", [P, JR])
            below = sc("below", [P, JR, TILES - 1])
            bound = sc("bound", [P, TILES - 1])
            passed = sc("passed", [P, TILES - 1])
            step_tile, tile_row0 = sc("step_tile", [P, JR]), sc("tile_row0", [P, JR])
            step_chunk = sc("step_chunk", [P, JR], U32)
            edges_i = sc("edges_i", [P, JR, 2 * P], I32)
            edges_f = sc("edges_f", [P, JR, 2 * P])
            block = scope.enter_context(nc.Block())

            @block.sync
            def _(sp):
                sp.dma_start(dst_i[:], a["edge_rows"].rearrange("(j p) e -> p j e", p=P)[:, :, P:2 * P]).then_inc(s_rows, 16)
                sp.dma_start(x[:], a["x"].rearrange("(t p) c -> p t c", p=P)).then_inc(s_x, 16)
                for name in WEIGHTS:
                    sp.dma_start(w[name][:], a[name]).then_inc(s_w, 16)
                for name in BIASES:
                    sp.dma_start(bias[name][:], a[name].broadcast_to((P, a[name].shape[1]))).then_inc(s_w, 16)
                sp.dma_start(moe_mask[:], a["moe_mask"]).then_inc(s_w, 16)
                sp.wait_ge(s_x, 16)
                sp.wait_ge(s_w, 16 * n_loads)

            @block.gpsimd
            def _(pool):
                link = Chain(pool, s_pchain, 0, 2)
                pool.iota(iota_i[:], pattern=[[1, P]], base=0, channel_multiplier=0).then_inc(s_const, 1)
                pool.iota(tile_no_i[:], pattern=[[1, TILES - 1]], base=0, channel_multiplier=0).then_inc(s_const, 1)
                pool.iota(step_no_i[:], pattern=[[P, JR]], base=0, channel_multiplier=1).then_inc(s_const, 1)
                pool.memset(ones[:], 1.0).then_inc(s_const, 1)
                pool.memset(neg_half[:], -0.5).then_inc(s_const, 1)
                link(pool.memset(ident[:], 0.0))
                pool.affine_select(out=ident[:], in_=ident[:], compare_op=ALU.not_equal, fill=1.0, base=0,
                                   pattern=[[-1, P]], channel_multiplier=1).then_inc(s_const, 1)
                link(pool.memset(valid[:], 1.0))
                pool.affine_select(out=valid[:], in_=valid[:], compare_op=ALU.is_ge, fill=0.0, base=NODES - 1,
                                   pattern=[[-P, TILES]], channel_multiplier=-1).then_inc(s_const, 1)
                for j in range(JR):
                    pool.wait_ge(s_chunk, j + 1)
                    pool.indirect_dma_start(out=edges_i[:, j, :], out_offset=None, in_=a["edge_rows"],
                                            in_offset=bass.IndirectOffsetOnAxis(ap=step_chunk[:, j:j + 1], axis=0)
                                            ).then_inc(s_gathered, 16)
                pool.wait_ge(s_gathered, 16 * JR)

            @block.vector
            def _(dve):
                link = Chain(dve, s_dchain, 0, 6 + 3 * JR)
                dve.memset(acc[:], 0.0).then_inc(s_acc0, 1)
                dve.wait_ge(s_const, 7)
                dve.tensor_copy(iota_row[:], iota_i[:]).then_inc(s_acc0, 1)
                link(dve.tensor_scalar(tile_end[:], tile_no_i[:], float(P), float(P), ALU.mult, ALU.add))
                link(dve.tensor_copy(tile_no[:], tile_no_i[:]))
                link(dve.tensor_copy(step_no[:], step_no_i[:]))
                dve.wait_ge(s_rows, 16)
                link(dve.tensor_copy(last_dst[:], dst_i[:, :, P - 1]))
                for j in range(JR):
                    dve.tensor_scalar(below[:, j, :], tile_end[:], last_dst[:, j:j + 1], None, ALU.is_gt
                                      ).then_inc(s_below, 1)
                dve.wait_ge(s_bound, 1)
                link(dve.tensor_tensor(bound[:], bank[0][:, 0:TILES - 1], tile_no[:], ALU.add))
                for j in range(JR):
                    link(dve.tensor_scalar(passed[:], bound[:], step_no[:, j:j + 1], None, ALU.is_lt))
                    link(dve.tensor_reduce(step_tile[:, j:j + 1], passed[:], AX, ALU.add))
                    dve.tensor_tensor(step_chunk[:, j:j + 1], step_no[:, j:j + 1], step_tile[:, j:j + 1],
                                      ALU.subtract).then_inc(s_chunk, 1)
                link(dve.tensor_scalar(tile_row0[:], step_tile[:], float(P), None, ALU.mult))
                dve.wait_ge(s_gathered, 16 * JR)
                for j in range(JR):
                    dve.tensor_copy(edges_f[:, j, 0:P], edges_i[:, j, 0:P]).then_inc(s_rel, 1)
                    dve.tensor_scalar(edges_f[:, j, P:2 * P], edges_i[:, j, P:2 * P], tile_row0[:, j:j + 1], None,
                                      ALU.subtract).then_inc(s_rel, 1)
                dve.wait_ge(s_tr, 3 * JR)
                dve.tensor_copy(src_step[:], bank[1][:]).then_inc(s_tab, 1)
                dve.tensor_copy(dst_step[:], bank[2][:]).then_inc(s_tab, 1)
                dve.tensor_scalar(acc_off[:], bank[3][0:1, :], float(ACCW), None, ALU.mult).then_inc(s_tab, 1)
                dve.tensor_scalar(q_off[:], bank[3][0:1, :], float(C), None, ALU.mult).then_inc(s_tab, 1)
                dve.wait_ge(s_tab, 4)

            @block.tensor
            def _(pe):
                pe.wait_ge(s_const, 7)
                pe.wait_ge(s_below, JR)
                for j in range(JR):
                    mm = pe.matmul(bank[0][:, 0:TILES - 1], ones[:], below[:, j, :], start=(j == 0), stop=(j == JR - 1))
                mm.then_inc(s_bound, 1)
                for j in range(JR):
                    cols = slice(j * P, (j + 1) * P)
                    pe.wait_ge(s_rel, 2 * j + 2)
                    pe.transpose(bank[1][:, cols], edges_f[:, j, 0:P], ident[:]).then_inc(s_tr, 1)
                    pe.transpose(bank[2][:, cols], edges_f[:, j, P:2 * P], ident[:]).then_inc(s_tr, 1)
                    pe.transpose(bank[3][0:1, cols], step_tile[:, j:j + 1], ident[:]).then_inc(s_tr, 1)

        pool_norm, dve_norm = normalize_stages(0)
        s_fold_mm, s_fold, s_bcol = sem("fold_products"), sem("folded"), sem("bias_columns")
        s_fchain = sem("fold_chain")
        s_xn, s_xt, s_xtc = sem("a_xn_ready"), sem("a_xn_transposed"), sem("a_xnt_copied")
        s_mm, s_added = sem("a_product_ready"), sem("a_added")
        s_nchain, s_addchain = sem("a_norm_chain"), sem("a_add_chain")
        s_store = [sem(f"a_xn_stored{u}") for u in range(2)]
        with ExitStack() as scope:
            def sc(name, shape, dt=F32):
                return scope.enter_context(nc.sbuf_tensor(name, shape, dt))
            xn = sc("a_xn", [P, 2, C])
            xnt = sc("a_xnt", [P, 2, C])
            w_xt = sc("w_xt", [D0, H0, C])
            bx_cols = sc("bx_cols", [D0, H0, P])
            b_x = sc("b_x", [D0, H0])
            inv_temp = sc("inv_temp", [P, H0])
            s_wx = sem("w_x_in")
            block = scope.enter_context(nc.Block())
            per_head = "p (h g) -> p h g"

            @block.sync
            def _(sp):
                sp.dma_start(w_xt[:], a["w_xt"]).then_inc(s_wx, 16)
                sp.dma_start(b_x[:], a["b_x"]).then_inc(s_wx, 16)

                def store(t, u):
                    sp.wait_ge(s_xn, t + 1)
                    sp.dma_start(xn_rows[:, bass.ds(t, 1), :], xn[:, u:u + 1, :]).then_inc(s_store[u], 16)
                pipeline(sp, TILES, 2, [(0, store)])
                for u in range(2):
                    sp.wait_ge(s_store[u], 16 * len(range(u, TILES, 2)))

            @block.gpsimd
            def _(pool):
                pipeline(pool, TILES, 2, [(0, pool_norm(pool))])

            @block.vector
            def _(dve):
                link = Chain(dve, s_fchain, 0, 4)
                link(dve.tensor_scalar(inv_temp[:], bias["temperature"][:], 0.1, 5.0, ALU.max, ALU.min))
                link(dve.reciprocal(inv_temp[:], inv_temp[:]))
                dve.wait_ge(s_wx, 32)
                for h in range(H0):
                    dve.tensor_scalar(bx_cols[:, h, :], ones[0:D0, :], b_x[:, h:h + 1], None, ALU.mult).then_inc(s_bcol, 1)
                dve.wait_ge(s_fold_mm, 1)
                scale = inv_temp[:].unsqueeze(2).broadcast_to((P, H0, G0))
                for k in range(KC):
                    dve.tensor_tensor(w_logits[:, k, :].rearrange(per_head, h=H0), bank[k][:].rearrange(per_head, h=H0),
                                      scale, ALU.mult).then_inc(s_fold, 1)
                link(dve.tensor_tensor(b_logits[:].rearrange(per_head, h=H0), bank[2][:].rearrange(per_head, h=H0),
                                       bias["b_slice"][:].unsqueeze(1).broadcast_to((P, H0, G0)), ALU.add))
                dve.tensor_tensor(b_logits[:].rearrange(per_head, h=H0), b_logits[:].rearrange(per_head, h=H0),
                                  scale, ALU.mult).then_inc(s_fold, 1)
                dve.tensor_tensor(b1_mlp[:], bank[3][:, 0:MC], w["l1_b1"][:], ALU.add).then_inc(s_fold, 1)
                for k in range(KC):
                    dve.tensor_scalar(w["l1_w1t"][:, k, :], w["l1_w1t"][:, k, :], w["ln_g"][:, k:k + 1], None,
                                      ALU.mult).then_inc(s_fold, 1)
                link(dve.tensor_tensor(bias["b1"][:], bias["b1"][:], bias["b2"][:], ALU.add))
                dve.wait_ge(s_fold, 2 * KC + 2)

                def norm(t, u):
                    if not early(t, 2):
                        dve.wait_ge(s_xt, t - 1)
                        dve.wait_ge(s_store[u], landed(t, u, 2) - 16)
                    link = Chain(dve, s_nchain, t, 1)
                    dve_norm(dve, link, x[:, bass.ds(t, 1), :].rearrange("p a c -> p (a c)"), xn[:, u, :], t, s_xn)

                def add(t, u):
                    dve.wait_ge(s_mm, t + 1)
                    row = x[:, bass.ds(t, 1), :].rearrange("p a c -> p (a c)")
                    link = Chain(dve, s_addchain, t, 1)
                    link(dve.tensor_tensor(row, row, bank[6 + u][:, 0:C], ALU.add))
                    dve.tensor_tensor(row, row, bias["b1"][:], ALU.add).then_inc(s_added, 1)
                pipeline(dve, TILES, 2, [(0, norm), (1, add)])
                dve.wait_ge(s_added, TILES)

            @block.scalar
            def _(act):
                def copy(t, u):
                    act.wait_ge(s_xt, t + 1)
                    if not early(t, 2):
                        act.wait_ge(s_mm, t - 1)
                    act.copy(xnt[:, u, :], bank[4 + u][:, 0:C]).then_inc(s_xtc, 1)
                pipeline(act, TILES, 2, [(0, copy)])

            @block.tensor
            def _(pe):
                pe.wait_ge(s_wx, 32)
                pe.wait_ge(s_bcol, H0)
                for h in range(H0):
                    cols = slice(h * G0, (h + 1) * G0)
                    for k in range(KC):
                        pe.matmul(bank[k][:, cols], w_xt[:, h, k * P:(k + 1) * P], w["w_slice"][:], start=True, stop=True)
                    pe.matmul(bank[2][:, cols], bx_cols[:, h, :], w["w_slice"][:], start=True, stop=True)
                for m in range(MC):
                    for k in range(KC):
                        mm = pe.matmul(bank[3][:, m:m + 1], w["l1_w1t"][:, k, m * P:(m + 1) * P], w["ln_b"][:, k:k + 1],
                                       start=(k == 0), stop=(k == KC - 1))
                mm.then_inc(s_fold_mm, 1)

                def turn_rows(t, u):
                    pe.wait_ge(s_xn, t + 1)
                    if not early(t, 2):
                        pe.wait_ge(s_xtc, t - 1)
                    for k in range(KC):
                        mm = pe.transpose(bank[4 + u][:, k * P:(k + 1) * P], xn[:, u, k * P:(k + 1) * P], ident[:])
                    mm.then_inc(s_xt, 1)

                def product(t, u):
                    pe.wait_ge(s_xtc, t + 1)
                    if not early(t, 2):
                        pe.wait_ge(s_added, t - 1)
                    for k in range(KC):
                        mm = pe.matmul(bank[6 + u][:, 0:C], xnt[:, u, k * P:(k + 1) * P], w["l0_w1t"][:, k, :],
                                       start=(k == 0), stop=(k == KC - 1))
                    mm.then_inc(s_mm, 1)
                pipeline(pe, TILES, 2, [(0, turn_rows), (1, product)])

        s_idx, s_eq, s_dup = sem("m_index_ready"), sem("m_equal_ready"), sem("m_index_chain")
        s_target, s_sum, s_total, s_one = sem("m_target_ready"), sem("m_sum_ready"), sem("m_total_copied"), sem("m_constants_ready")
        s_seg, s_zeroed = [sem(f"m_first_ends_landed{u}") for u in range(U)], sem("m_tables_zeroed")
        s_land = [sem(f"m_rows_landed{u}") for u in range(U)]
        s_add = [sem(f"m_rows_added{u}") for u in range(U)]
        s_cols, s_first = sem("m_edge_columns_in"), sem("m_first_ends_ready")
        with ExitStack() as scope:
            def sc(name, shape, dt=F32):
                return scope.enter_context(nc.sbuf_tensor(name, shape, dt))
            first_cols, second_cols = sc("m_first_cols", [P, MEAN_CHUNKS], I32), sc("m_second_cols", [P, MEAN_CHUNKS], I32)
            first = sc("m_first", [P, MEAN_CHUNKS])
            index, target = sc("m_index", [P, U], U32), sc("m_target", [P, U], U32)
            first_row = sc("m_first_row", [P, U, P], I32)
            rows = sc("m_rows", [P, U, SUMW])
            equal = sc("m_equal", [P, U, P])
            before, scratch = sc("m_before", [P, P]), sc("m_scratch", [P, P])
            dup, spare, spare_i = sc("m_dup", [P, 1]), sc("m_spare", [P, 1]), sc("m_spare_i", [P, 1], I32)
            total = sc("m_total", [P, U, SUMW])
            block = scope.enter_context(nc.Block())

            @block.sync
            def _(sp):
                sp.dma_start(first_cols[:], a["first_cols"]).then_inc(s_cols, 16)
                sp.dma_start(second_cols[:], a["second_cols"]).then_inc(s_cols, 16)
                for table in sums_dram:
                    sp.dma_start(table.rearrange("(t p) w -> p t w", p=P),
                                 acc[:, 0:SUMW].unsqueeze(1).broadcast_to((P, TILES + 1, SUMW))).then_inc(s_zeroed, 16)

                def load_first(c, u):
                    if not early(c, U):
                        sp.wait_ge(s_eq, c - (U - 1))
                    sp.dma_start(first_row[:, u, :], a["first_rows"][bass.ds(c, 1), :].broadcast_to((P, P))
                                 ).then_inc(s_seg[u], 16)
                pipeline(sp, MEAN_CHUNKS, U, [(0, load_first)])

            @block.scalar
            def _(act):
                act.wait_ge(s_cols, 32)

                def copy_total(c, u):
                    act.wait_ge(s_sum, c + 1)
                    if not early(c, U):
                        act.wait_ge(s_add[u], landed(c, u, U) - 16)
                    act.copy(total[:, u, :], bank[u][:, 0:SUMW]).then_inc(s_total, 1)

                def fetch_index(c, u):
                    if not early(c, U):
                        act.wait_ge(s_land[u], landed(c, u, U) - 16)
                    act.copy(index[:, u:u + 1], second_cols[:, bass.ds(c, 1)]).then_inc(s_idx, 1)
                pipeline(act, MEAN_CHUNKS, U, [(0, fetch_index), (2, copy_total)])

            @block.gpsimd
            def _(pool):
                pool.memset(rows[:, :, C:SUMW], 1.0).then_inc(s_one, 1)
                pool.memset(before[:], 1.0).then_inc(s_one, 1)
                pool.iota(spare_i[:], pattern=[[0, 1]], base=ROWS, channel_multiplier=1).then_inc(s_one, 1)
                pool.wait_ge(s_one, 3)
                pool.affine_select(out=before[:], in_=before[:], compare_op=ALU.is_gt, fill=0.0, base=0,
                                   pattern=[[-1, P]], channel_multiplier=1).then_inc(s_one, 1)
                pool.wait_ge(s_zeroed, 16 * U)

                def gather(c, u):
                    if not early(c, U):
                        pool.wait_ge(s_sum, c - (U - 1))
                    fence(pool, s_idx, c + 1)
                    pool.indirect_dma_start(out=rows[:, u, 0:C], out_offset=None, in_=xn_dram,
                                            in_offset=bass.IndirectOffsetOnAxis(ap=index[:, u:u + 1], axis=0)
                                            ).then_inc(s_land[u], 16)

                def add(c, u):
                    if not early(c, U):
                        pool.wait_ge(s_add[u], landed(c, u, U) - 16)
                    pool.wait_ge(s_target, c + 1)
                    fence(pool, s_total, c + 1)
                    pool.indirect_dma_start(out=sums_dram[u], in_=total[:, u, :], in_offset=None,
                                            out_offset=bass.IndirectOffsetOnAxis(ap=target[:, u:u + 1], axis=0),
                                            compute_op=ALU.add).then_inc(s_add[u], 16)
                pipeline(pool, MEAN_CHUNKS, U, [(0, gather), (2, add)])
                for u in range(U):
                    pool.wait_ge(s_add[u], 16 * (MEAN_CHUNKS // U))

            @block.vector
            def _(dve):
                dve.wait_ge(s_cols, 32)
                dve.tensor_copy(first[:], first_cols[:]).then_inc(s_first, 1)
                dve.wait_ge(s_one, 4)
                dve.tensor_copy(spare[:], spare_i[:]).then_inc(s_first, 1)
                dve.wait_ge(s_first, 2)

                def compare(c, u):
                    dve.wait_ge(s_seg[u], landed(c, u, U))
                    if not early(c, U):
                        dve.wait_ge(s_sum, c - (U - 1))
                        dve.wait_ge(s_add[u], landed(c, u, U) - 16)
                    own = first[:, bass.ds(c, 1)]
                    dve.tensor_scalar(equal[:, u, :], first_row[:, u, :], own, None, ALU.is_equal).then_inc(s_eq, 1)
                    dve.wait_ge(s_eq, c + 1)
                    link = Chain(dve, s_dup, 4 * c, 4)
                    link(dve.tensor_tensor(scratch[:], equal[:, u, :], before[:], ALU.mult))
                    link(dve.tensor_reduce(dup[:], scratch[:], AX, ALU.max))
                    link(dve.tensor_tensor(scratch[:, 0:1], spare[:], own, ALU.subtract))
                    link(dve.tensor_tensor(dup[:], dup[:], scratch[:, 0:1], ALU.mult))
                    dve.tensor_tensor(target[:, u:u + 1], dup[:], own, ALU.add).then_inc(s_target, 1)
                pipeline(dve, MEAN_CHUNKS, U, [(0, compare)])

            @block.tensor
            def _(pe):
                pe.wait_ge(s_one, 1)

                def sum_equal(c, u):
                    pe.wait_ge(s_eq, c + 1)
                    pe.wait_ge(s_land[u], landed(c, u, U))
                    if not early(c, U):
                        pe.wait_ge(s_total, c - (U - 1))
                    pe.matmul(bank[u][:, 0:SUMW], equal[:, u, :], rows[:, u, :], start=True, stop=True).then_inc(s_sum, 1)
                pipeline(pe, MEAN_CHUNKS, U, [(1, sum_equal)])


        pool_norm, dve_norm = normalize_stages(0)
        s_mean, s_meant, s_meantc = sem("b_mean_ready"), sem("b_mean_transposed"), sem("b_meant_copied")
        s_mm2 = sem("b_product_ready")
        s_xn, s_xt, s_xtc = sem("b_xn_ready"), sem("b_xn_transposed"), sem("b_xnt_copied")
        s_log, s_shift, s_exp, s_wgt = sem("b_logits_ready"), sem("b_shifted"), sem("b_exp_ready"), sem("b_weights_ready")
        s_wsum, s_u, s_wt, s_wtc = sem("b_weights_summed"), sem("b_sliced"), sem("b_weights_transposed"), sem("b_wt_copied")
        s_c0, s_c1, s_c2, s_c3 = sem("b_mean_chain"), sem("b_norm_chain"), sem("b_shift_chain"), sem("b_weigh_chain")
        s_init = sem("b_zeroed")
        s_store = [sem(f"b_wt_stored{u}") for u in range(2)]
        s_load = [sem(f"b_sums_landed{u}") for u in range(2)]
        wsum = sb("wsum", [P, INNER])
        with ExitStack() as scope:
            def sc(name, shape, dt=F32):
                return scope.enter_context(nc.sbuf_tensor(name, shape, dt))
            mean, meant = sc("b_mean", [P, 2, C]), sc("b_meant", [P, 2, C])
            xn, xnt = sc("b_xn", [P, 2, C]), sc("b_xnt", [P, 2, C])
            soft = sc("b_soft", [P, 2, H0, G0])
            soft_flat = soft[:].rearrange("p u h g -> p u (h g)")
            cnt, hmax, hsum = sc("b_cnt", [P, 1]), sc("b_hmax", [P, H0]), sc("b_hsum", [P, H0])
            wt = sc("b_wt", [P, 2, INNER])
            sums = q_tab[:, 0:2 * U * SUMW].rearrange("p (u k w) -> p u k w", u=2, k=U)
            sums_of = sc("b_sums_of", [P, SUMW])
            block = scope.enter_context(nc.Block())

            @block.sync
            def _(sp):
                def load(t, u):
                    if not early(t, 2):
                        sp.wait_ge(s_mean, t - 1)
                    for i, table in enumerate(sums_dram):
                        sp.dma_start(sums[:, u, i, :], table.rearrange("(t p) w -> p t w", p=P)[:, bass.ds(t, 1), :]
                                     ).then_inc(s_load[u], 16)

                def store(t, u):
                    sp.wait_ge(s_wtc, t + 1)
                    sp.dma_start(wt_rows[:, bass.ds(t, 1), :], wt[:, u:u + 1, :]).then_inc(s_store[u], 16)
                pipeline(sp, TILES, 2, [(0, load), (4, store)])
                for u in range(2):
                    sp.wait_ge(s_store[u], 16 * len(range(u, TILES, 2)))

            @block.gpsimd
            def _(pool):
                pool.memset(wsum[:], 0.0).then_inc(s_init, 1)
                pool.wait_ge(s_init, 1)

                def sum_weights(t, u):
                    if not early(t, 1):
                        pool.wait_ge(s_wsum, t)
                    fence(pool, s_wgt, t + 1)
                    pool.tensor_tensor(wsum[:], wsum[:], soft_flat[:, u, :], ALU.add).then_inc(s_wsum, 1)
                pipeline(pool, TILES, 2, [(3, sum_weights), (1, pool_norm(pool))])
                pool.wait_ge(s_wsum, TILES)

            @block.vector
            def _(dve):
                def node_mean(t, u):
                    if not early(t, 2):
                        dve.wait_ge(s_meant, t - 1)
                    dve.wait_ge(s_load[u], U * landed(t, u, 2))
                    link = Chain(dve, s_c0, 3 * t, 3)
                    link(dve.tensor_reduce(sums_of[:], sums[:, u, :, :].rearrange("p k w -> p w k"), AX, ALU.add))
                    link(dve.tensor_scalar(cnt[:], sums_of[:, C:SUMW], 1.0, None, ALU.max))
                    link(dve.reciprocal(cnt[:], cnt[:]))
                    dve.tensor_scalar(mean[:, u, :], sums_of[:, 0:C], cnt[:], None, ALU.mult
                                      ).then_inc(s_mean, 1)

                def add_and_norm(t, u):
                    dve.wait_ge(s_mm2, t + 1)
                    if not early(t, 2):
                        dve.wait_ge(s_u, t - 1)
                    link = Chain(dve, s_c1, 2 * t, 2)
                    row = x[:, bass.ds(t, 1), :].rearrange("p a c -> p (a c)")
                    link(dve.tensor_tensor(row, row, bank[1][:, 0:C], ALU.add))
                    dve_norm(dve, link, row, xn[:, u, :], t, s_xn)

                def shift(t, u):
                    dve.wait_ge(s_log, t + 1)
                    if not early(t, 2):
                        dve.wait_ge(s_wt, t - 1)
                        dve.wait_ge(s_wsum, t - 1)
                    link = Chain(dve, s_c2, 2 * t, 2)
                    link(dve.tensor_tensor(soft_flat[:, u, :], bank[3][:], b_logits[:], ALU.add))
                    link(dve.tensor_reduce(hmax[:], soft[:, u, :, :], AX, ALU.max))
                    dve.tensor_tensor(soft[:, u, :, :], soft[:, u, :, :],
                                      hmax[:].unsqueeze(2).broadcast_to((P, H0, G0)), ALU.subtract).then_inc(s_shift, 1)

                def weigh(t, u):
                    dve.wait_ge(s_exp, t + 1)
                    link = Chain(dve, s_c3, 3 * t, 3)
                    link(dve.tensor_reduce(hsum[:], soft[:, u, :, :], AX, ALU.add))
                    link(dve.reciprocal(hsum[:], hsum[:]))
                    link(dve.tensor_scalar(hsum[:], hsum[:], valid[:, bass.ds(t, 1)], None, ALU.mult))
                    dve.tensor_tensor(soft[:, u, :, :], soft[:, u, :, :],
                                      hsum[:].unsqueeze(2).broadcast_to((P, H0, G0)), ALU.mult).then_inc(s_wgt, 1)
                pipeline(dve, TILES, 2, [(3, weigh), (2, shift), (1, add_and_norm), (0, node_mean)])

            @block.scalar
            def _(act):
                def copy_wt(t, u):
                    act.wait_ge(s_wt, t + 1)
                    if not early(t, 2):
                        act.wait_ge(s_store[u], landed(t, u, 2) - 16)
                    act.copy(wt[:, u, :], bank[7][:]).then_inc(s_wtc, 1)

                def exponent(t, u):
                    act.wait_ge(s_shift, t + 1)
                    act.activation(soft_flat[:, u, :], soft_flat[:, u, :], ACT.Exp).then_inc(s_exp, 1)

                def copy_xnt(t, u):
                    act.wait_ge(s_xt, t + 1)
                    if not early(t, 2):
                        act.wait_ge(s_log, t - 1)
                    act.copy(xnt[:, u, :], bank[2][:, 0:C]).then_inc(s_xtc, 1)

                def copy_meant(t, u):
                    act.wait_ge(s_meant, t + 1)
                    if not early(t, 2):
                        act.wait_ge(s_mm2, t - 1)
                    act.copy(meant[:, u, :], bank[0][:, 0:C]).then_inc(s_meantc, 1)
                pipeline(act, TILES, 2, [(3, copy_wt), (2, exponent), (1, copy_xnt), (0, copy_meant)])

            @block.tensor
            def _(pe):
                def slices(t, u):
                    pe.wait_ge(s_wgt, t + 1)
                    for m in range(INNER // P):
                        mm = pe.matmul(bank[5 + m // 2][:, (m % 2) * C:(m % 2 + 1) * C], soft_flat[:, u, m * P:(m + 1) * P],
                                       xn[:, u, :], start=(early(t, 1) and m % 2 == 0), stop=False, skip_group_check=True)
                    mm.then_inc(s_u, 1)
                    if not early(t, 1):
                        pe.wait_ge(s_wtc, t)
                    for m in range(INNER // P):
                        mm = pe.transpose(bank[7][:, m * P:(m + 1) * P], soft_flat[:, u, m * P:(m + 1) * P], ident[:])
                    mm.then_inc(s_wt, 1)

                def logits(t, u):
                    pe.wait_ge(s_xtc, t + 1)
                    if not early(t, 1):
                        pe.wait_ge(s_shift, t)
                    for k in range(KC):
                        mm = pe.matmul(bank[3][:], xnt[:, u, k * P:(k + 1) * P], w_logits[:, k, :],
                                       start=(k == 0), stop=(k == KC - 1))
                    mm.then_inc(s_log, 1)

                def project_mean(t, u):
                    pe.wait_ge(s_meantc, t + 1)
                    if not early(t, 1):
                        pe.wait_ge(s_xn, t)
                    for k in range(KC):
                        mm = pe.matmul(bank[1][:, 0:C], meant[:, u, k * P:(k + 1) * P], w["l0_w2t"][:, k, :],
                                       start=(k == 0), stop=(k == KC - 1))
                    mm.then_inc(s_mm2, 1)

                def turn_xn(t, u):
                    pe.wait_ge(s_xn, t + 1)
                    if not early(t, 1):
                        pe.wait_ge(s_xtc, t)
                    for k in range(KC):
                        mm = pe.transpose(bank[2][:, k * P:(k + 1) * P], xn[:, u, k * P:(k + 1) * P], ident[:])
                    mm.then_inc(s_xt, 1)

                def turn_mean(t, u):
                    pe.wait_ge(s_mean, t + 1)
                    if not early(t, 1):
                        pe.wait_ge(s_meantc, t)
                    for k in range(KC):
                        mm = pe.transpose(bank[0][:, k * P:(k + 1) * P], mean[:, u, k * P:(k + 1) * P], ident[:])
                    mm.then_inc(s_meant, 1)
                pipeline(pe, TILES, 2, [(3, slices), (2, logits), (1, project_mean), (1, turn_xn), (0, turn_mean)])

        s_cv, s_cp, s_ca = sem("c_vector_steps"), sem("c_tensor_steps"), sem("c_exp_ready")
        s_pack = sem("c_slice_out_packed")
        with ExitStack() as scope:
            def sc(name, shape, dt=F32):
                return scope.enter_context(nc.sbuf_tensor(name, shape, dt))
            MI = INNER // P
            un = q_tab[:, 0:MI * C].rearrange("p (m c) -> p m c", m=MI)
            norm = sc("c_norm", [P, MI])
            share = sc("c_share", [P, MI])
            unt = q_tab[:, MI * C:MI * C + KC * INNER].rearrange("p (k n) -> p k n", k=KC)
            share_t = sc("c_share_t", [1, INNER])
            tokens_t = sc("c_tokens_t", [D0, INNER])
            qt, kt, vt = (sc("c_" + n, [D0, INNER]) for n in ("qt", "kt", "vt"))
            prob = sc("c_prob", [G0, H0, G0])
            prob_t = sc("c_prob_t", [G0, H0, G0])
            smax, ssum = sc("c_smax", [G0, H0]), sc("c_ssum", [G0, H0])
            vout = acc[0:G0, 0:H0 * C].rearrange("p (h c) -> p h c", h=H0)
            attended = acc[0:G0, H0 * C:2 * H0 * C].rearrange("p (h c) -> p h c", h=H0)
            block = scope.enter_context(nc.Block())

            C_SHARE = 3 + MI + 1
            C_SHT = C_SHARE + KC + 1
            C_TOK = C_SHT + 1
            C_VT = C_TOK + 3
            C_SUB = C_VT + 3
            C_PROB = C_SUB + 3
            C_PROBT = C_PROB + 1
            C_LAST = C_PROBT + H0
            T_NORM, T_UNT, T_TOK, T_QKV, T_SCORE, T_PROBT = range(1, 7)
            T_VOUT = T_PROBT + H0 // 2

            @block.vector
            def _(dve):
                count = [0]

                def link(ins):
                    ins.then_inc(s_cv, 1)
                    count[0] += 1
                    dve.wait_ge(s_cv, count[0])
                dve.wait_ge(s_cp, T_NORM)
                link(dve.tensor_copy(norm[:], bank[0][:, 0:MI]))
                link(dve.tensor_scalar(share[:], norm[:], 1e-5, None, ALU.add))
                link(dve.reciprocal(share[:], share[:]))
                for m in range(MI):
                    link(dve.tensor_scalar(un[:, m, :], bank[5 + m // 2][:, (m % 2) * C:(m % 2 + 1) * C], share[:, m:m + 1],
                                           None, ALU.mult))
                link(dve.tensor_tensor(share[:], share[:], norm[:], ALU.mult))
                dve.wait_ge(s_cp, T_UNT)
                for k in range(KC):
                    link(dve.tensor_copy(unt[:, k, :], bank[1 + k][:]))
                link(dve.tensor_copy(share_t[:], bank[3][0:1, :]))
                dve.wait_ge(s_cp, T_TOK)
                link(dve.tensor_copy(tokens_t[:], bank[4][0:D0, :]))
                dve.wait_ge(s_cp, T_QKV)
                link(dve.tensor_copy(qt[:], bank[0][0:D0, :]))
                link(dve.tensor_copy(kt[:], bank[1][0:D0, :]))
                link(dve.tensor_copy(vt[:], bank[2][0:D0, :]))
                dve.wait_ge(s_cp, T_SCORE)
                link(dve.tensor_scalar(prob[:], bank[3][0:G0, :].rearrange("p (h g) -> p h g", h=H0), float(D0) ** -0.5,
                                       None, ALU.mult))
                link(dve.tensor_reduce(smax[:], prob[:], AX, ALU.max))
                link(dve.tensor_tensor(prob[:], prob[:], smax[:].unsqueeze(2).broadcast_to((G0, H0, G0)), ALU.subtract))
                dve.wait_ge(s_ca, 1)
                link(dve.tensor_reduce(ssum[:], prob[:], AX, ALU.add))
                link(dve.reciprocal(ssum[:], ssum[:]))
                link(dve.tensor_tensor(prob[:], prob[:], ssum[:].unsqueeze(2).broadcast_to((G0, H0, G0)), ALU.mult))
                dve.wait_ge(s_cp, T_PROBT)
                link(dve.tensor_copy(prob_t[:], bank[0][0:G0, :].rearrange("p (h g) -> p h g", h=H0)))
                for i in range(H0 // 2):
                    dve.wait_ge(s_cp, T_PROBT + 1 + i)
                    link(dve.tensor_copy(vout[:, 2 * i:2 * i + 2, :], bank[1 + i][0:G0, :].rearrange("p (h c) -> p h c", h=2)))
                for i in range(H0 // 2):
                    dve.wait_ge(s_cp, T_VOUT + 1 + i)
                    link(dve.tensor_copy(attended[:, 2 * i:2 * i + 2, :],
                                         bank[(5, 6, 7, 0)[i]][0:G0, :].rearrange("p (h c) -> p h c", h=2)))
                assert count[0] == C_LAST

            @block.scalar
            def _(act):
                act.wait_ge(s_cv, C_SUB)
                act.activation(prob[:], prob[:], ACT.Exp).then_inc(s_ca, 1)

            @block.tensor
            def _(pe):
                for m in range(MI):
                    mm = pe.matmul(bank[0][:, m:m + 1], wsum[:, m * P:(m + 1) * P], ones[:, 0:1], start=True, stop=True)
                mm.then_inc(s_cp, 1)
                pe.wait_ge(s_cv, C_SHARE)
                for m in range(MI):
                    for k in range(KC):
                        pe.transpose(bank[1 + k][:, m * P:(m + 1) * P], un[:, m, k * P:(k + 1) * P], ident[:])
                    mm = pe.transpose(bank[3][0:1, m * P:(m + 1) * P], share[:, m:m + 1], ident[:])
                mm.then_inc(s_cp, 1)
                pe.wait_ge(s_cv, C_SHT)
                for h in range(H0):
                    cols = slice(h * G0, (h + 1) * G0)
                    for k in range(KC):
                        pe.matmul(bank[4][0:D0, cols], w["l0_fx"][:, k, cols], unt[:, k, cols], start=(k == 0), stop=False)
                    mm = pe.matmul(bank[4][0:D0, cols], w["b_fx_row"][0:1, cols], share_t[0:1, cols], start=False, stop=True)
                mm.then_inc(s_cp, 1)
                pe.wait_ge(s_cv, C_TOK)
                for i, name in enumerate(("w_q", "w_k", "w_v")):
                    mm = pe.matmul(bank[i][0:D0, :], w[name][:], tokens_t[:], start=True, stop=True)
                mm.then_inc(s_cp, 1)
                pe.wait_ge(s_cv, C_VT)
                for h in range(H0):
                    cols = slice(h * G0, (h + 1) * G0)
                    mm = pe.matmul(bank[3][0:G0, cols], qt[:, cols], kt[:, cols], start=True, stop=True)
                mm.then_inc(s_cp, 1)
                pe.wait_ge(s_cv, C_PROB)
                for h in range(H0):
                    mm = pe.transpose(bank[0][0:G0, h * G0:(h + 1) * G0], prob[:, h, :], ident[0:G0, 0:G0])
                mm.then_inc(s_cp, 1)
                for i in range(H0 // 2):
                    for h in (2 * i, 2 * i + 1):
                        mm = pe.matmul(bank[1 + i][0:G0, (h % 2) * C:(h % 2 + 1) * C], vt[:, h * G0:(h + 1) * G0],
                                       w["l0_slice_out"][:, h, :], start=True, stop=True)
                    mm.then_inc(s_cp, 1)
                for i in range(H0 // 2):
                    pe.wait_ge(s_cv, C_PROBT + 1 + i)
                    for h in (2 * i, 2 * i + 1):
                        mm = pe.matmul(bank[(5, 6, 7, 0)[i]][0:G0, (h % 2) * C:(h % 2 + 1) * C], prob_t[:, h, :], vout[:, h, :],
                                       start=True, stop=True)
                    mm.then_inc(s_cp, 1)

            @block.sync
            def _(sp):
                sp.wait_ge(s_cv, C_LAST)
                pairs = attended.rearrange("p (m two) c -> p two m c", two=2)
                for half in range(2):
                    sp.dma_start(slice_out[half * G0:(half + 1) * G0, :, :], pairs[:, half, :, :]).then_inc(s_pack, 16)
                sp.wait_ge(s_pack, 32)

        pool_norm, dve_norm = normalize_stages(0)
        s_o, s_xn, s_xt, s_xtc = sem("d_slices_ready"), sem("d_xn_ready"), sem("d_xn_transposed"), sem("d_xnt_copied")
        s_qkv, s_q, s_kv = sem("d_products_ready"), sem("d_queries_kept"), sem("d_kv_ready")
        s_c1, s_zero = sem("d_norm_chain"), sem("d_acc_zeroed")
        s_load = [sem(f"d_wt_landed{u}") for u in range(2)]
        s_store = [sem(f"d_kv_stored{u}") for u in range(2)]
        with ExitStack() as scope:
            def sc(name, shape, dt=F32):
                return scope.enter_context(nc.sbuf_tensor(name, shape, dt))
            wt = sc("d_wt", [P, 2, INNER])
            xn, xnt = sc("d_xn", [P, 2, C]), sc("d_xnt", [P, 2, C])
            kv = sc("d_kv", [P, 2, 2 * C])
            block = scope.enter_context(nc.Block())

            @block.sync
            def _(sp):
                def load(t, u):
                    if not early(t, 2):
                        sp.wait_ge(s_o, t - 1)
                    sp.dma_start(wt[:, u:u + 1, :], wt_rows[:, bass.ds(t, 1), :]).then_inc(s_load[u], 16)
                pipeline(sp, TILES, 2, [(0, load)])

            @block.gpsimd
            def _(pool):
                pool.memset(acc[:], 0.0).then_inc(s_zero, 1)
                pipeline(pool, TILES, 2, [(0, pool_norm(pool))])
                pool.wait_ge(s_zero, 1)

            @block.vector
            def _(dve):
                def keep(t, u):
                    dve.wait_ge(s_qkv, t + 1)
                    dve.tensor_tensor(q_tab[:, bass.ds(t * C, C)], bank[4 + u][:, 0:C], bias["bq"][:], ALU.add
                                      ).then_inc(s_q, 1)
                    if not early(t, 2):
                        dve.wait_ge(s_store[u], landed(t, u, 2) - 16)
                    dve.tensor_tensor(kv[:, u, :], bank[6 + u][:], bias["bkv"][:], ALU.add).then_inc(s_kv, 1)

                def add_and_norm(t, u):
                    dve.wait_ge(s_o, t + 1)
                    if not early(t, 2):
                        dve.wait_ge(s_xt, t - 1)
                    link = Chain(dve, s_c1, 3 * t, 3)
                    row = x[:, bass.ds(t, 1), :].rearrange("p a c -> p (a c)")
                    link(dve.tensor_tensor(row, row, bank[u][:, 0:C], ALU.add))
                    link(dve.tensor_tensor(row, row, bias["b_out"][:], ALU.add))
                    dve_norm(dve, link, row, xn[:, u, :], t, s_xn)
                pipeline(dve, TILES, 2, [(1, keep), (0, add_and_norm)])
                dve.wait_ge(s_q, TILES)

            @block.scalar
            def _(act):
                def copy_xnt(t, u):
                    act.wait_ge(s_xt, t + 1)
                    if not early(t, 2):
                        act.wait_ge(s_qkv, t - 1)
                    act.copy(xnt[:, u, :], bank[2 + u][:, 0:C]).then_inc(s_xtc, 1)

                def store(t, u):
                    act.wait_ge(s_kv, t + 1)
                    act.dma_start(kv_rows[:, bass.ds(t, 1), :], kv[:, u:u + 1, :]).then_inc(s_store[u], 16)
                pipeline(act, TILES, 2, [(1, store), (0, copy_xnt)])
                for u in range(2):
                    act.wait_ge(s_store[u], 16 * len(range(u, TILES, 2)))

            @block.tensor
            def _(pe):
                def project(t, u):
                    pe.wait_ge(s_xtc, t + 1)
                    if not early(t, 2):
                        pe.wait_ge(s_kv, t - 1)
                    for k in range(KC):
                        pe.matmul(bank[4 + u][:, 0:C], xnt[:, u, k * P:(k + 1) * P], w["l1_qt"][:, k, :],
                                  start=(k == 0), stop=(k == KC - 1))
                    for k in range(KC):
                        mm = pe.matmul(bank[6 + u][:], xnt[:, u, k * P:(k + 1) * P], w["l1_kvt"][:, k, :],
                                       start=(k == 0), stop=(k == KC - 1))
                    mm.then_inc(s_qkv, 1)

                def spread_slices(t, u):
                    pe.wait_ge(s_load[u], landed(t, u, 2))
                    if not early(t, 2):
                        pe.wait_ge(s_xn, t - 1)
                    for m in range(INNER // P):
                        mm = pe.matmul(bank[u][:, 0:C], wt[:, u, m * P:(m + 1) * P], slice_out[:, m, :],
                                       start=(m == 0), stop=(m == INNER // P - 1))
                    mm.then_inc(s_o, 1)

                def turn_xn(t, u):
                    pe.wait_ge(s_xn, t + 1)
                    if not early(t, 2):
                        pe.wait_ge(s_xtc, t - 1)
                    for k in range(KC):
                        mm = pe.transpose(bank[2 + u][:, k * P:(k + 1) * P], xn[:, u, k * P:(k + 1) * P], ident[:])
                    mm.then_inc(s_xt, 1)
                pipeline(pe, TILES, 2, [(1, project), (0, spread_slices), (0, turn_xn)])

        s_idx, s_oh, s_oht, s_ohc = sem("e_index_ready"), sem("e_onehot_ready"), sem("e_onehot_transposed"), sem("e_oht_copied")
        s_qe, s_prod, s_clip, s_exp = sem("e_queries_spread"), sem("e_product_ready"), sem("e_scores_clipped"), sem("e_exp_ready")
        s_msg, s_sum, s_acc, s_c = sem("e_message_ready"), sem("e_sum_ready"), sem("e_accumulated"), sem("e_chain")
        s_land = [sem(f"e_kv_landed{u}") for u in range(STEP_UNROLL)]
        with ExitStack() as scope:
            def sc(name, shape, dt=F32):
                return scope.enter_context(nc.sbuf_tensor(name, shape, dt))
            index = sc("e_index", [P, U], U32)
            kv = sc("e_kv", [P, U, 2 * C])
            onehot, onehot_t = sc("e_onehot", [P, U, P]), sc("e_onehot_t", [P, U, P])
            prod, score = sc("e_prod", [P, C]), sc("e_score", [P, U, H1])
            msg = sc("e_msg", [P, U, ACCW])
            block = scope.enter_context(nc.Block())

            @block.gpsimd
            def _(pool):
                def gather(s, u):
                    if not early(s, U):
                        pool.wait_ge(s_msg, s - (U - 1))
                    fence(pool, s_idx, s + 1)
                    pool.indirect_dma_start(out=kv[:, u, :], out_offset=None, in_=kv_dram,
                                            in_offset=bass.IndirectOffsetOnAxis(ap=index[:, u:u + 1], axis=0)
                                            ).then_inc(s_land[u], 16)
                pipeline(pool, STEPS_RUN, U, [(0, gather)])

            @block.scalar
            def _(act):
                def exponent(s, u):
                    act.wait_ge(s_clip, s + 1)
                    if not early(s, U):
                        act.wait_ge(s_sum, s - (U - 1))
                    act.activation(msg[:, u, C:ACCW], score[:, u, :], ACT.Exp).then_inc(s_exp, 1)

                def copy_onehot_t(s, u):
                    act.wait_ge(s_oht, s + 1)
                    if not early(s, U):
                        act.wait_ge(s_qe, s - (U - 1))
                    act.copy(onehot_t[:, u, :], bank[u % 2][:, 0:P]).then_inc(s_ohc, 1)

                def fetch_index(s, u):
                    if not early(s, U):
                        fence(act, s_land[u], landed(s, u, U) - 16)
                    act.copy(index[:, u:u + 1], src_step[:, bass.ds(s, 1)]).then_inc(s_idx, 1)
                pipeline(act, STEPS_RUN, U, [(0, fetch_index), (0, copy_onehot_t), (2, exponent)])

            @block.vector
            def _(dve):
                heads = "p (h d) -> p h d"

                def make_onehot(s, u):
                    if not early(s, U):
                        dve.wait_ge(s_sum, s - (U - 1))
                    dve.tensor_scalar(onehot[:, u, :], iota_row[:], dst_step[:, bass.ds(s, 1)], None,
                                      ALU.is_equal).then_inc(s_oh, 1)

                def scores(s, u):
                    dve.wait_ge(s_qe, s + 1)
                    dve.wait_ge(s_land[u], landed(s, u, U))
                    link = Chain(dve, s_c, 2 * s, 2)
                    link(dve.scalar_tensor_tensor(out=prod[:], in0=bank[2 + u % 2][:, 0:C], scalar=float(D1) ** -0.5,
                                                  in1=kv[:, u, 0:C], op0=ALU.mult, op1=ALU.mult))
                    link(dve.tensor_reduce(score[:, u, :], prod[:].rearrange(heads, h=H1), AX, ALU.add))
                    dve.tensor_scalar(score[:, u, :], score[:, u, :], 10.0, -10.0, ALU.min, ALU.max).then_inc(s_clip, 1)

                def message(s, u):
                    dve.wait_ge(s_exp, s + 1)
                    dve.tensor_tensor(msg[:, u, 0:C].rearrange(heads, h=H1), kv[:, u, C:2 * C].rearrange(heads, h=H1),
                                      msg[:, u, C:ACCW].unsqueeze(2).broadcast_to((P, H1, D1)), ALU.mult
                                      ).then_inc(s_msg, 1)

                def accumulate(s, u):
                    dve.wait_ge(s_sum, s + 1)
                    if not early(s, 1):
                        dve.wait_ge(s_acc, s)
                    off = dve.value_load(acc_off[0:1, bass.ds(s, 1)], min_val=0, max_val=(TILES - 1) * ACCW)
                    row = acc[:, bass.ds(off, ACCW)]
                    dve.tensor_tensor(row, row, bank[4 + u % 2][:, 0:ACCW], ALU.add).then_inc(s_acc, 1)
                pipeline(dve, STEPS_RUN, U, [(2, scores), (0, make_onehot), (3, accumulate), (2, message)])
                dve.wait_ge(s_acc, STEPS_RUN)

            @block.tensor
            def _(pe):
                def turn_onehot(s, u):
                    pe.wait_ge(s_oh, s + 1)
                    if not early(s, 2):
                        pe.wait_ge(s_ohc, s - 1)
                    pe.transpose(bank[u % 2][:, 0:P], onehot[:, u, :], ident[:]).then_inc(s_oht, 1)

                def spread_queries(s, u):
                    pe.wait_ge(s_ohc, s + 1)
                    if not early(s, 2):
                        pe.wait_ge(s_clip, s - 1)
                    off = pe.value_load(q_off[0:1, bass.ds(s, 1)], min_val=0, max_val=(TILES - 1) * C)
                    pe.matmul(bank[2 + u % 2][:, 0:C], onehot_t[:, u, :], q_tab[:, bass.ds(off, C)], start=True, stop=True
                              ).then_inc(s_qe, 1)

                def sum_messages(s, u):
                    pe.wait_ge(s_msg, s + 1)
                    if not early(s, 2):
                        pe.wait_ge(s_acc, s - 1)
                    pe.matmul(bank[4 + u % 2][:, 0:ACCW], onehot[:, u, :], msg[:, u, :], start=True, stop=True
                              ).then_inc(s_sum, 1)
                pipeline(pe, STEPS_RUN, U, [(0, turn_onehot), (1, spread_queries), (2, sum_messages)])
        pool_norm1, dve_norm1 = normalize_stages(0)
        pool_norm2, dve_norm2 = normalize_stages(1)
        pool_norm3, dve_norm3 = normalize_stages(2)
        s_wv, s_wvt, s_wvtc, s_y = sem("f_attended_ready"), sem("f_attended_transposed"), sem("f_attended_t_copied"), sem("f_y_ready")
        s_feat, s_hn, s_hnt, s_hntc = sem("f_features_ready"), sem("f_hn_ready"), sem("f_hn_transposed"), sem("f_hnt_copied")
        s_hid, s_gelu, s_down = sem("f_hidden_ready"), sem("f_gelu_ready"), sem("f_down_ready")
        s_xn, s_xnt, s_xntc = sem("g_xn_ready"), sem("g_xn_transposed"), sem("g_xnt_copied")
        s_route, s_pick, s_pickt, s_picktc = sem("g_router_ready"), sem("g_pick_ready"), sem("g_pick_transposed"), sem("g_pick_t_copied")
        s_eh, s_relu, s_eo = sem("g_expert_hidden_ready"), sem("g_relu_ready"), sem("g_expert_out_ready")
        s_done, s_pre = sem("g_rows_done"), sem("g_constants_ready")
        s_c0, s_c1, s_c3, s_c4, s_c6 = sem("f_attended_chain"), sem("f_y_chain"), sem("f_down_chain"), sem("g_route_chain"), sem("g_out_chain")
        s_n0, s_n1, s_n3 = sem("f_feature_norm_chain"), sem("f_hn_chain"), sem("g_xn_chain")
        s_store = [sem(f"g_rows_stored{u}") for u in range(2)]
        with ExitStack() as scope:
            def sc(name, shape, dt=F32):
                return scope.enter_context(nc.sbuf_tensor(name, shape, dt))
            inv_den = sc("f_inv_den", [P, H1])
            wv, wvt, feat, y = (sc("f_" + n, [P, 2, C]) for n in ("wv", "wvt", "feat", "y"))
            hn, hnt = sc("f_hn", [P, 2, C]), sc("f_hnt", [P, 2, C])
            units = q_tab[:].rearrange("p (m n) -> p m n", n=P)
            hidden = units[:, 0:2 * MC, :].rearrange("p (u m) n -> p u m n", u=2)
            e_hidden = units[:, 2 * MC:2 * (MC + EC), :].rearrange("p (u m) n -> p u m n", u=2)
            xn, xnt = sc("g_xn", [P, 2, C]), sc("g_xnt", [P, 2, C])
            logit, is_max, rank, best = (sc("g_" + n, [P, k]) for n, k in (("logit", EXPERTS), ("is_max", EXPERTS),
                                                                          ("rank", EXPERTS), ("best", 1)))
            pick = sc("g_pick", [P, 2, EXPERTS])
            pick_t, pick_tb = sc("g_pick_t", [EXPERTS, 2, P]), sc("g_pick_tb", [EXPERTS, 2, P], BF16)
            res = sc("g_res", [P, 2, C])
            block = scope.enter_context(nc.Block())
            QC = 4
            EQ = EC // QC

            @block.sync
            def _(sp):
                def store(t, u):
                    sp.wait_ge(s_done, t + 1)
                    sp.dma_start(out_rows[:, bass.ds(t, 1), :], res[:, u:u + 1, :]).then_inc(s_store[u], 16)
                pipeline(sp, TILES, 2, [(0, store)])
                for u in range(2):
                    sp.wait_ge(s_store[u], 16 * len(range(u, TILES, 2)))

            @block.gpsimd
            def _(pool):
                pipeline(pool, TILES, 2, [(3, pool_norm3(pool)), (1, pool_norm2(pool)), (0, pool_norm1(pool))])

            @block.vector
            def _(dve):
                heads = "p (h d) -> p h d"

                def row_of(t):
                    return x[:, bass.ds(t, 1), :].rearrange("p a c -> p (a c)")

                def attended(t, u):
                    if not early(t, 2):
                        dve.wait_ge(s_wvt, t - 1)
                    link = Chain(dve, s_c0, 2 * t, 2)
                    link(dve.tensor_scalar(inv_den[:], acc[:, bass.ds(t * ACCW + C, H1)], 1e-30, None, ALU.max))
                    link(dve.reciprocal(inv_den[:], inv_den[:]))
                    dve.tensor_tensor(wv[:, u, :].rearrange(heads, h=H1),
                                      acc[:, bass.ds(t * ACCW, C)].rearrange(heads, h=H1),
                                      inv_den[:].unsqueeze(2).broadcast_to((P, H1, D1)), ALU.mult).then_inc(s_wv, 1)
                    dve_norm1(dve, Chain(dve, s_n0, t, 1), row_of(t), feat[:, u, :], t, s_feat)

                def y_and_norm(t, u):
                    dve.wait_ge(s_y, t + 1)
                    dve.wait_ge(s_feat, t + 1)
                    link = Chain(dve, s_c1, 2 * t, 2)
                    link(dve.tensor_tensor(y[:, u, :], bank[2][:, 0:C], feat[:, u, :], ALU.add))
                    link(dve.tensor_tensor(y[:, u, :], y[:, u, :], bias["bp"][:], ALU.add))
                    if not early(t, 2):
                        dve.wait_ge(s_hnt, t - 1)
                    dve_norm2(dve, Chain(dve, s_n1, t, 1), y[:, u, :], hn[:, u, :], t, s_hn)

                def down_and_norm(t, u):
                    dve.wait_ge(s_down, t + 1)
                    link = Chain(dve, s_c3, 3 * t, 3)
                    link(dve.tensor_tensor(row_of(t), row_of(t), bank[3][:, 0:C], ALU.add))
                    link(dve.tensor_tensor(row_of(t), row_of(t), y[:, u, :], ALU.add))
                    link(dve.tensor_tensor(row_of(t), row_of(t), bias["b2m"][:], ALU.add))
                    if not early(t, 2):
                        dve.wait_ge(s_xnt, t - 1)
                    dve_norm3(dve, Chain(dve, s_n3, t, 1), row_of(t), xn[:, u, :], t, s_xn)

                def route(t, u):
                    dve.wait_ge(s_route, t + 1)
                    if not early(t, 2):
                        dve.wait_ge(s_pickt, t - 1)
                    link = Chain(dve, s_c4, 5 * t, 5)
                    link(dve.tensor_tensor(logit[:], bank[1][:, C:C + EXPERTS], bias["router_b"][:], ALU.add))
                    link(dve.tensor_reduce(best[:], logit[:], AX, ALU.max))
                    link(dve.tensor_scalar(is_max[:], logit[:], best[:], None, ALU.is_equal))
                    link(dve.tensor_tensor(rank[:], is_max[:], countdown[:], ALU.mult))
                    link(dve.tensor_reduce(best[:], rank[:], AX, ALU.max))
                    dve.tensor_scalar(pick[:, u, :], countdown[:], best[:], None, ALU.is_equal).then_inc(s_pick, 1)

                def finish(t, u):
                    dve.wait_ge(s_eo, t + 1)
                    if not early(t, 2):
                        dve.wait_ge(s_store[u], landed(t, u, 2) - 16)
                    dve.scalar_tensor_tensor(out=res[:, u, :], in0=bank[3][:, 0:C], scalar=0.0, in1=row_of(t),
                                             op0=ALU.max, op1=ALU.add).then_inc(s_done, 1)
                dve.tensor_scalar(countdown[:], iota_row[:, 0:EXPERTS], -1.0, float(EXPERTS), ALU.mult, ALU.add
                                  ).then_inc(s_pre, 1)
                dve.wait_ge(s_pre, 1)
                pipeline(dve, TILES, 2, [(6, finish), (4, route), (3, down_and_norm), (1, y_and_norm), (0, attended)])
                dve.wait_ge(s_done, TILES)

            @block.scalar
            def _(act):
                def relu(t, u):
                    for q in range(EQ):
                        act.wait_ge(s_eh, t * EQ + q + 1)
                        if q == 0 and not early(t, 2):
                            act.wait_ge(s_eo, t - 1)
                        for i in range(QC):
                            m = q * QC + i
                            ins = act.activation(e_hidden[:, u, m, :], bank[6 + q % 2][:, i * P:(i + 1) * P], ACT.Relu,
                                                 bias=w["moe_b1"][:, m:m + 1])
                        ins.then_inc(s_relu, 1)

                def copy_pick_t(t, u):
                    act.wait_ge(s_pickt, t + 1)
                    if not early(t, 2):
                        act.wait_ge(s_eo, t - 1)
                    act.copy(pick_t[:, u, :], bank[1][0:EXPERTS, C + P:C + 2 * P]).then_inc(s_picktc, 1)
                    act.copy(pick_tb[:, u, :], bank[1][0:EXPERTS, C + P:C + 2 * P]).then_inc(s_picktc, 1)

                def copy_xnt(t, u):
                    act.wait_ge(s_xnt, t + 1)
                    if not early(t, 2):
                        act.wait_ge(s_eh, (t - 1) * EQ)
                    act.copy(xnt[:, u, :], bank[1][:, 0:C]).then_inc(s_xntc, 1)

                def gelu(t, u):
                    act.wait_ge(s_hid, t + 1)
                    if not early(t, 2):
                        act.wait_ge(s_down, t - 1)
                    for m in range(MC):
                        ins = act.activation(hidden[:, u, m, :], bank[4 + m // 4][:, (m % 4) * P:(m % 4 + 1) * P], ACT.Gelu,
                                             bias=b1_mlp[:, m:m + 1])
                    ins.then_inc(s_gelu, 1)

                def copy_hnt(t, u):
                    act.wait_ge(s_hnt, t + 1)
                    if not early(t, 2):
                        act.wait_ge(s_hid, t - 1)
                    act.copy(hnt[:, u, :], bank[0][:, 0:C]).then_inc(s_hntc, 1)

                def copy_wvt(t, u):
                    act.wait_ge(s_wvt, t + 1)
                    if not early(t, 2):
                        act.wait_ge(s_y, t - 1)
                    act.copy(wvt[:, u, :], bank[2][:, 0:C]).then_inc(s_wvtc, 1)
                pipeline(act, TILES, 2, [(5, relu), (4, copy_pick_t), (3, copy_xnt), (2, gelu), (1, copy_hnt), (0, copy_wvt)])

            @block.tensor
            def _(pe):
                def turn(t, rows, target, done):
                    for k in range(KC):
                        mm = pe.transpose(target[:, k * P:(k + 1) * P], rows[:, k * P:(k + 1) * P], ident[:])
                    mm.then_inc(done, 1)

                def experts_out(t, u):
                    if not early(t, 1):
                        pe.wait_ge(s_done, t)
                    pe.wait_ge(s_xn, min(t + 3, TILES) if isinstance(t, int) else t + 3)
                    for m in range(EC):
                        if m % QC == 0:
                            pe.wait_ge(s_relu, t * EQ + m // QC + 1)
                        pe.matmul(bank[3][:, 0:C], e_hidden[:, u, m, :], w["moe_w2"][:, m, :], start=(m == 0), stop=False)
                    pe.matmul(bank[3][:, 0:C], pick_t[:, u, :], w["moe_b2"][:], start=False, stop=True).then_inc(s_eo, 1)

                def experts_hidden(t, u):
                    pe.wait_ge(s_picktc, 2 * t + 2)
                    for m in range(EC):
                        q = m // QC
                        if m % QC == 0 and not early(t * EQ + q, 2):
                            pe.wait_ge(s_relu, t * EQ + q - 1)
                        cols, target = slice(m * P, (m + 1) * P), bank[6 + q % 2][:, (m % QC) * P:(m % QC + 1) * P]
                        for k in range(KC):
                            pe.matmul(target, w["moe_w1"][:, k, cols], xnt[:, u, k * P:(k + 1) * P], start=(k == 0), stop=False)
                        mm = pe.matmul(target, moe_mask[:, cols], pick_tb[:, u, :], start=False, stop=True)
                        if m % QC == QC - 1:
                            mm.then_inc(s_eh, 1)

                def router(t, u):
                    pe.wait_ge(s_xntc, t + 1)
                    for k in range(KC):
                        mm = pe.matmul(bank[1][:, C:C + EXPERTS], xnt[:, u, k * P:(k + 1) * P], w["router_t"][:, k, :],
                                       start=(k == 0), stop=(k == KC - 1))
                    mm.then_inc(s_route, 1)

                def turn_pick(t, u):
                    pe.wait_ge(s_pick, t + 1)
                    pe.transpose(bank[1][0:EXPERTS, C + P:C + 2 * P], pick[:, u, :], ident[:]).then_inc(s_pickt, 1)

                def down(t, u):
                    pe.wait_ge(s_gelu, t + 1)
                    if not early(t, 1):
                        pe.wait_ge(s_xn, t)
                    if not early(t, 3):
                        pe.wait_ge(s_done, t - 2)
                    for m in range(MC):
                        mm = pe.matmul(bank[3][:, 0:C], hidden[:, u, m, :], w["l1_w2t"][:, m, :],
                                       start=(m == 0), stop=(m == MC - 1))
                    mm.then_inc(s_down, 1)

                def turn_xn(t, u):
                    pe.wait_ge(s_xn, t + 1)
                    if not early(t, 1):
                        pe.wait_ge(s_picktc, 2 * t)
                    turn(t, xn[:, u, :], bank[1][:, 0:C], s_xnt)

                def up(t, u):
                    pe.wait_ge(s_hntc, t + 1)
                    if not early(t, 1):
                        pe.wait_ge(s_gelu, t)
                    for m in range(MC):
                        for k in range(KC):
                            mm = pe.matmul(bank[4 + m // 4][:, (m % 4) * P:(m % 4 + 1) * P],
                                           w["l1_w1t"][:, k, m * P:(m + 1) * P], hnt[:, u, k * P:(k + 1) * P],
                                           start=(k == 0), stop=(k == KC - 1))
                    mm.then_inc(s_hid, 1)

                def attention_out(t, u):
                    pe.wait_ge(s_wvtc, t + 1)
                    for k in range(KC):
                        mm = pe.matmul(bank[2][:, 0:C], wvt[:, u, k * P:(k + 1) * P], w["l1_pt"][:, k, :],
                                       start=(k == 0), stop=(k == KC - 1))
                    mm.then_inc(s_y, 1)

                def turn_hn(t, u):
                    pe.wait_ge(s_hn, t + 1)
                    if not early(t, 1):
                        pe.wait_ge(s_hntc, t)
                    turn(t, hn[:, u, :], bank[0][:, 0:C], s_hnt)

                def turn_wv(t, u):
                    pe.wait_ge(s_wv, t + 1)
                    if not early(t, 1):
                        pe.wait_ge(s_hn, t)
                    turn(t, wv[:, u, :], bank[2][:, 0:C], s_wvt)
                pipeline(pe, TILES, 2, [(6, experts_out), (5, experts_hidden), (4, router), (4, turn_pick), (3, down), (3, turn_xn),
                                        (2, up), (1, attention_out), (1, turn_hn), (0, turn_wv)])


OUT_SHAPE = (ROWS, C)


def kernel(**inputs):
    import ml_dtypes
    import concourse.bacc as bacc
    from concourse.bass_utils import run_bass_kernel_spmd

    g = {k: np.asarray(v) for k, v in inputs.items()}

    def by_channel(m):
        return m.reshape(-1, P, m.shape[1]).transpose(1, 0, 2)

    pad = STEP_TABLE * P - EDGES
    src = np.pad(g["src"].astype(np.int32), (0, pad)).reshape(STEP_TABLE, P)
    dst = np.pad(g["dst"].astype(np.int32), (0, pad), constant_values=PAD_DST).reshape(STEP_TABLE, P)
    pad = MEAN_CHUNKS * P - EDGES
    first = np.pad(g["src"].astype(np.int32), (0, pad), constant_values=ROWS).reshape(MEAN_CHUNKS, P)
    second = np.pad(g["dst"].astype(np.int32), (0, pad)).reshape(MEAN_CHUNKS, P)
    moe_w1 = g["L1_ffn_W1"].transpose(1, 0, 2).reshape(C, EXPERTS * HID)
    mask = np.where(np.arange(EXPERTS * HID)[None] // HID == np.arange(EXPERTS)[:, None], 0.0, -1e30)
    arrays = {
        "x": np.pad(g["x"], ((0, ROWS - NODES), (0, 0))),
        "edge_rows": np.concatenate([src, dst], axis=1),
        "first_rows": first, "first_cols": first.T, "second_cols": second.T,
        "l0_w1t": by_channel(g["L0_gnn_W1"].T), "l0_w2t": by_channel(g["L0_gnn_W2"].T),
        "l0_fx": by_channel(g["L0_ffn_W_fx"]),
        "w_xt": g["L0_ffn_W_x"].T.reshape(H0, D0, C).transpose(1, 0, 2),
        "b_x": g["L0_ffn_b_x"].reshape(H0, D0).T,
        "w_slice": g["L0_ffn_W_slice"], "w_q": g["L0_ffn_W_q"], "w_k": g["L0_ffn_W_k"], "w_v": g["L0_ffn_W_v"],
        "b_fx_row": g["L0_ffn_b_fx"][None],
        "l0_slice_out": g["L0_ffn_W_out"].reshape(H0, D0, C).transpose(1, 0, 2),
        "l1_qt": by_channel(g["L1_gnn_Wq"].T),
        "l1_kvt": by_channel(np.concatenate([g["L1_gnn_Wk"].T, g["L1_gnn_Wv"].T], axis=1)),
        "l1_pt": by_channel(g["L1_gnn_Wp"].T),
        "l1_w1t": by_channel(g["L1_gnn_W1"].T), "l1_w2t": by_channel(g["L1_gnn_W2"].T),
        "l1_b1": g["L1_gnn_b1"].reshape(MC, P).T,
        "ln_g": g["L1_gnn_ln_g"].reshape(KC, P).T, "ln_b": g["L1_gnn_ln_b"].reshape(KC, P).T,
        "router_t": by_channel(g["L1_ffn_router_w"].T),
        "moe_w1": by_channel(moe_w1), "moe_b1": g["L1_ffn_b1"].reshape(EC, P).T,
        "moe_w2": by_channel(g["L1_ffn_W2"].reshape(EXPERTS * HID, C)), "moe_b2": g["L1_ffn_b2"],
        "moe_mask": mask.astype(ml_dtypes.bfloat16),
        "b1": g["L0_gnn_b1"][None], "b2": g["L0_gnn_b2"][None], "b_slice": g["L0_ffn_b_slice"][None],
        "b_out": g["L0_ffn_b_out"][None], "bq": g["L1_gnn_bq"][None],
        "bkv": np.concatenate([g["L1_gnn_bk"], g["L1_gnn_bv"]])[None],
        "bp": g["L1_gnn_bp"][None], "b2m": g["L1_gnn_b2"][None], "router_b": g["L1_ffn_router_b"][None],
        "temperature": g["L0_ffn_temperature"].reshape(1, H0),
    }
    arrays = {k: np.ascontiguousarray(v) for k, v in arrays.items()}
    nc = bacc.Bacc("TRN2", target_bir_lowering=False, num_devices=1)
    aps = {k: nc.dram_tensor("in_" + k, v.shape, mybir.dt.from_np(v.dtype), kind="ExternalInput").ap()
           for k, v in arrays.items()}
    out = nc.dram_tensor("out_rows", OUT_SHAPE, F32, kind="ExternalOutput").ap()
    build(nc, aps, out)
    r = run_bass_kernel_spmd(nc, [{"in_" + k: v for k, v in arrays.items()}], core_ids=[0])
    return r.results[0]["out_rows"][:NODES]
```

```python
from contextlib import ExitStack

import numpy as np

import concourse.bass as bass
from concourse import mybir

F32 = mybir.dt.float32
BF16 = mybir.dt.bfloat16
I32 = mybir.dt.int32
U32 = mybir.dt.uint32
ALU = mybir.AluOpType
ACT = mybir.ActivationFunctionType
AX = mybir.AxisListType.X

P = 128
NODES = 3125
EDGES = 50000
C = 256
KC = C // P
TILES = -(-NODES // P)
ROWS = TILES * P
CHUNKS = -(-EDGES // P)
STEPS = CHUNKS + TILES - 1
STEP_UNROLL = 16
LOADS = 2
SLOTS = 8
STEPS_RUN = -(-STEPS // STEP_UNROLL) * STEP_UNROLL
STEP_GROUPS = -(-(STEPS_RUN + 1) // P)
STEP_TABLE = STEP_GROUPS * P
ADD_LAG = 6
SPREAD_LAG = 2
PAD_DST = ROWS
U = 4
SUMW = C + 1
H0, D0, G0 = 8, 64, 64
INNER = H0 * D0
H1, D1 = 8, 32
ACCW = C + H1
MLP = 4 * C
MC = MLP // P
EXPERTS, HID = 32, C // 4
EC = EXPERTS * HID // P
EPS = 1e-5


def early(t, n):
    return isinstance(t, int) and t < n


def late(t, count, n):
    return isinstance(t, int) and t >= count - n


def pipeline(eng, count, unroll, stages, begin=None):
    depth = max(lag for lag, _ in stages)

    def turn(i, v):
        if begin is not None:
            begin(i, v)
        for lag, body in stages:
            if isinstance(i, int) and not 0 <= i - lag < count:
                continue
            body(i - lag, (v - lag) % unroll)

    head = -(-(depth + unroll) // unroll)
    last = count // unroll
    for i in range(head * unroll):
        turn(i, i % unroll)
    with eng.Fori(head, last) as g:
        for v in range(unroll):
            turn(g * unroll + v, v)
    for i in range(last * unroll, count + depth):
        turn(i, i % unroll)


def landed(t, slot, unroll):
    return (t - slot) * (16 // unroll) + 16


class Chain:

    def __init__(self, eng, sem, start, length):
        self.eng, self.sem, self.start, self.length, self.n = eng, sem, start, length, 0

    def __call__(self, ins):
        ins.then_inc(self.sem, 1)
        self.n += 1
        assert self.n <= self.length
        self.eng.wait_ge(self.sem, self.start + self.n)


def chain(eng, sem, length, at=0):
    return lambda t: Chain(eng, sem, length * t + at, length)



WEIGHTS = ["l0_w1t", "l0_w2t", "l0_fx", "l0_slice_out", "l1_qt", "l1_kvt", "l1_pt", "l1_w1t", "l1_w2t",
           "router_t", "moe_w1", "moe_b1", "moe_w2", "moe_b2", "w_slice", "w_q", "w_k", "w_v", "b_fx_row",
           "l1_b1", "ln_g", "ln_b"]
BIASES = ["b1", "b2", "b_slice", "b_out", "bq", "bkv", "bp", "b2m", "router_b", "temperature"]


def build(nc, a, out):
    with ExitStack() as ctx:
        def sem(name):
            return ctx.enter_context(nc.semaphore(name))

        def sb(name, shape, dt=F32):
            return ctx.enter_context(nc.sbuf_tensor(name, shape, dt))

        def dram(name, shape):
            return nc.dram_tensor(name, shape, F32, kind="Internal").ap()

        step_src_dram = dram("step_sources", (STEP_TABLE, P))
        kv_dram = dram("kv_rows", (ROWS, 2 * C))
        sums_dram = [dram(f"first_end_sums{u}", (ROWS + P, SUMW)) for u in range(U)]
        wt_dram = dram("slice_weights_t", (TILES, P, INNER))
        kv_rows = kv_dram.rearrange("(t p) c -> p t c", p=P)
        wt_rows = wt_dram.rearrange("t p n -> p t n")
        out_rows = out.rearrange("(t p) c -> p t c", p=P)

        s_fence = sem("fence")

        def carry_waits(eng):
            eng.sem_inc(s_fence, 1)

        def fence(eng, signal, value):
            eng.wait_ge(signal, value)
            carry_waits(eng)

        bank = [ctx.enter_context(nc.psum_tensor(f"bank{i}", [P, 512], F32)) for i in range(8)]

        x = sb("x", [P, TILES, C])
        acc = sb("acc", [P, TILES * ACCW])
        q_tab = sb("q_tab", [P, TILES * C])
        ident = sb("ident", [P, P])
        iota_row = sb("iota_row", [P, P])
        ones = sb("ones", [P, P])
        neg_half = sb("neg_half", [P, 1])
        valid = sb("valid", [P, TILES])
        src_step = sb("src_step", [P, STEP_TABLE])
        dst_step = sb("dst_step", [P, STEP_TABLE])
        acc_off = sb("acc_off", [1, STEP_TABLE + STEP_UNROLL], I32)
        q_off = sb("q_off", [1, STEP_TABLE + STEP_UNROLL], I32)
        w = {name: sb("w_" + name, list(a[name].shape)) for name in WEIGHTS}
        bias = {name: sb("b_" + name, [P, a[name].shape[1]]) for name in BIASES}
        slice_out = sb("slice_out", [P, INNER // P, C])
        b1_mlp = sb("b1_mlp", [P, MC])
        w_logits = sb("w_logits", [P, KC, INNER])
        b_logits = sb("b_logits", [P, INNER])
        moe_mask = sb("moe_mask", [EXPERTS, EXPERTS * HID], BF16)
        countdown = sb("countdown", [P, EXPERTS])
        stats = sb("stats", [P, 3, 2, 6])
        mean_var = sb("mean_var", [P, 3, 2, 2])
        rstd = sb("rstd", [P, 3, 2])

        norm_sems = [(sem(f"stats_ready{i}"), sem(f"rstd_ready{i}"), sem(f"var_eps{i}")) for i in range(3)]
        norms_before = [0, 0, 0]

        def normalize_stages(i):
            stats_ready, rstd_ready, pool_chain = norm_sems[i]
            base = norms_before[i]
            norms_before[i] += TILES

            def pool_stage(pool):
                def body(t, u):
                    rs = rstd[:, i, u % 2:u % 2 + 1]
                    fence(pool, stats_ready, base + t + 1)
                    pool.tensor_scalar(rs, mean_var[:, i, u % 2, 1:2], EPS, None, ALU.add).then_inc(pool_chain, 1)
                    pool.wait_ge(pool_chain, base + t + 1)
                    pool.tensor_tensor(rs, rs, neg_half[:], ALU.pow).then_inc(rstd_ready, 1)
                return body

            def measure(dve, link, row, t, u):
                carry_waits(dve)
                link(dve.bn_stats(stats[:, i, u % 2, :], row))
                carry_waits(dve)
                dve.bn_aggr(mean_var[:, i, u % 2, :], stats[:, i, u % 2, :]).then_inc(stats_ready, 1)

            def apply(dve, row, out, t, u, out_ready):
                dve.wait_ge(stats_ready, base + t + 1)
                dve.wait_ge(rstd_ready, base + t + 1)
                dve.tensor_scalar(out, row, mean_var[:, i, u % 2, 0:1], rstd[:, i, u % 2:u % 2 + 1], ALU.subtract, ALU.mult
                                  ).then_inc(out_ready, 1)
            return pool_stage, measure, apply

        s_x, s_w, s_rows = sem("x_in"), sem("weights_in"), sem("dst_rows_in")
        s_gathered = sem("step_rows_gathered")
        s_const, s_acc0 = sem("constants_ready"), sem("acc_zeroed")
        s_dchain, s_pchain = sem("table_chain_dve"), sem("table_chain_pool")
        s_below, s_bound = sem("chunk_ends_compared"), sem("tile_ends_counted")
        s_chunk, s_rel = sem("step_chunk_ready"), sem("step_rows_float")
        s_tr, s_tab = sem("step_rows_transposed"), sem("step_tables_ready")
        n_loads = 1 + len(WEIGHTS) + len(BIASES)
        JR = STEP_GROUPS

        with ExitStack() as scope:
            def sc(name, shape, dt=F32):
                return scope.enter_context(nc.sbuf_tensor(name, shape, dt))
            dst_i = sc("dst_i", [P, JR, P], I32)
            last_dst = sc("last_dst", [P, JR])
            iota_i = sc("iota_i", [P, P], I32)
            tile_no_i = sc("tile_no_i", [P, TILES - 1], I32)
            step_no_i = sc("step_no_i", [P, JR], I32)
            tile_end, tile_no = sc("tile_end", [P, TILES - 1]), sc("tile_no", [P, TILES - 1])
            step_no = sc("step_no", [P, JR])
            below = sc("below", [P, JR, TILES - 1])
            bound = sc("bound", [P, TILES - 1])
            passed = sc("passed", [P, TILES - 1])
            step_tile, tile_row0 = sc("step_tile", [P, JR]), sc("tile_row0", [P, JR])
            step_chunk = sc("step_chunk", [P, JR], U32)
            edges_i = sc("edges_i", [P, JR, 2 * P], I32)
            edges_f = sc("edges_f", [P, JR, 2 * P])
            block = scope.enter_context(nc.Block())

            @block.sync
            def _(sp):
                sp.dma_start(dst_i[:], a["edge_rows"].rearrange("(j p) e -> p j e", p=P)[:, :, P:2 * P]).then_inc(s_rows, 16)
                sp.dma_start(x[:], a["x"].rearrange("(t p) c -> p t c", p=P)).then_inc(s_x, 16)
                for name in WEIGHTS:
                    sp.dma_start(w[name][:], a[name]).then_inc(s_w, 16)
                for name in BIASES:
                    sp.dma_start(bias[name][:], a[name].broadcast_to((P, a[name].shape[1]))).then_inc(s_w, 16)
                sp.dma_start(moe_mask[:], a["moe_mask"]).then_inc(s_w, 16)
                sp.wait_ge(s_rel, 2 * JR)
                sp.dma_start(step_src_dram.rearrange("(j p) e -> p j e", p=P), edges_f[:, :, 0:P]).then_inc(s_rows, 16)
                sp.wait_ge(s_rows, 32)
                sp.wait_ge(s_x, 16)
                sp.wait_ge(s_w, 16 * n_loads)

            @block.gpsimd
            def _(pool):
                link = Chain(pool, s_pchain, 0, 2)
                pool.iota(iota_i[:], pattern=[[1, P]], base=0, channel_multiplier=0).then_inc(s_const, 1)
                pool.iota(tile_no_i[:], pattern=[[1, TILES - 1]], base=0, channel_multiplier=0).then_inc(s_const, 1)
                pool.iota(step_no_i[:], pattern=[[P, JR]], base=0, channel_multiplier=1).then_inc(s_const, 1)
                pool.memset(ones[:], 1.0).then_inc(s_const, 1)
                pool.memset(neg_half[:], -0.5).then_inc(s_const, 1)
                link(pool.memset(ident[:], 0.0))
                pool.affine_select(out=ident[:], in_=ident[:], compare_op=ALU.not_equal, fill=1.0, base=0,
                                   pattern=[[-1, P]], channel_multiplier=1).then_inc(s_const, 1)
                link(pool.memset(valid[:], 1.0))
                pool.affine_select(out=valid[:], in_=valid[:], compare_op=ALU.is_ge, fill=0.0, base=NODES - 1,
                                   pattern=[[-P, TILES]], channel_multiplier=-1).then_inc(s_const, 1)
                for j in range(JR):
                    pool.wait_ge(s_chunk, j + 1)
                    pool.indirect_dma_start(out=edges_i[:, j, :], out_offset=None, in_=a["edge_rows"],
                                            in_offset=bass.IndirectOffsetOnAxis(ap=step_chunk[:, j:j + 1], axis=0)
                                            ).then_inc(s_gathered, 16)
                pool.wait_ge(s_gathered, 16 * JR)

            @block.vector
            def _(dve):
                link = Chain(dve, s_dchain, 0, 8 + 3 * JR)
                link(dve.memset(acc_off[:], 0))
                link(dve.memset(q_off[:], 0))
                dve.memset(q_tab[:], 0.0).then_inc(s_acc0, 1)
                dve.memset(acc[:].rearrange("p (t w) -> p t w", w=ACCW)[:, :, C:ACCW], 1.0).then_inc(s_acc0, 1)
                dve.wait_ge(s_const, 7)
                dve.tensor_copy(iota_row[:], iota_i[:]).then_inc(s_acc0, 1)
                link(dve.tensor_scalar(tile_end[:], tile_no_i[:], float(P), float(P), ALU.mult, ALU.add))
                link(dve.tensor_copy(tile_no[:], tile_no_i[:]))
                link(dve.tensor_copy(step_no[:], step_no_i[:]))
                dve.wait_ge(s_rows, 16)
                link(dve.tensor_copy(last_dst[:], dst_i[:, :, P - 1]))
                for j in range(JR):
                    dve.tensor_scalar(below[:, j, :], tile_end[:], last_dst[:, j:j + 1], None, ALU.is_gt
                                      ).then_inc(s_below, 1)
                dve.wait_ge(s_bound, 1)
                link(dve.tensor_tensor(bound[:], bank[0][:, 0:TILES - 1], tile_no[:], ALU.add))
                for j in range(JR):
                    link(dve.tensor_scalar(passed[:], bound[:], step_no[:, j:j + 1], None, ALU.is_lt))
                    link(dve.tensor_reduce(step_tile[:, j:j + 1], passed[:], AX, ALU.add))
                    dve.tensor_tensor(step_chunk[:, j:j + 1], step_no[:, j:j + 1], step_tile[:, j:j + 1],
                                      ALU.subtract).then_inc(s_chunk, 1)
                link(dve.tensor_scalar(tile_row0[:], step_tile[:], float(P), None, ALU.mult))
                dve.wait_ge(s_gathered, 16 * JR)
                for j in range(JR):
                    dve.tensor_copy(edges_f[:, j, 0:P], edges_i[:, j, 0:P]).then_inc(s_rel, 1)
                    dve.tensor_scalar(edges_f[:, j, P:2 * P], edges_i[:, j, P:2 * P], tile_row0[:, j:j + 1], None,
                                      ALU.subtract).then_inc(s_rel, 1)
                dve.wait_ge(s_tr, 3 * JR)
                dve.tensor_copy(src_step[:], bank[1][:]).then_inc(s_tab, 1)
                dve.tensor_copy(dst_step[:], bank[2][:]).then_inc(s_tab, 1)
                dve.tensor_scalar(acc_off[:, ADD_LAG:ADD_LAG + STEP_TABLE], bank[3][0:1, :], float(ACCW), None, ALU.mult).then_inc(s_tab, 1)
                dve.tensor_scalar(q_off[:, SPREAD_LAG:SPREAD_LAG + STEP_TABLE], bank[3][0:1, :], float(C), None, ALU.mult).then_inc(s_tab, 1)
                dve.wait_ge(s_tab, 4)

            @block.tensor
            def _(pe):
                pe.wait_ge(s_const, 7)
                pe.wait_ge(s_below, JR)
                for j in range(JR):
                    mm = pe.matmul(bank[0][:, 0:TILES - 1], ones[:], below[:, j, :], start=(j == 0), stop=(j == JR - 1))
                mm.then_inc(s_bound, 1)
                for j in range(JR):
                    cols = slice(j * P, (j + 1) * P)
                    pe.wait_ge(s_rel, 2 * j + 2)
                    pe.transpose(bank[1][:, cols], edges_f[:, j, 0:P], ident[:]).then_inc(s_tr, 1)
                    pe.transpose(bank[2][:, cols], edges_f[:, j, P:2 * P], ident[:]).then_inc(s_tr, 1)
                    pe.transpose(bank[3][0:1, cols], step_tile[:, j:j + 1], ident[:]).then_inc(s_tr, 1)

        pool_norm, measure, apply = normalize_stages(0)
        s_fold_mm, s_fold, s_bcol = sem("fold_products"), sem("folded"), sem("bias_columns")
        s_fchain = sem("fold_chain")
        s_xn, s_xt, s_xtc = sem("a_xn_ready"), sem("a_xn_transposed"), sem("a_xnt_copied")
        s_mm, s_added = sem("a_product_ready"), sem("a_added")
        s_nchain, s_addchain = sem("a_norm_chain"), sem("a_add_chain")
        s_kept, s_zeroed = sem("a_xn_kept"), sem("a_mean_tables_zeroed")
        with ExitStack() as scope:
            def sc(name, shape, dt=F32):
                return scope.enter_context(nc.sbuf_tensor(name, shape, dt))
            xn = sc("a_xn", [P, 2, C])
            xnt = sc("a_xnt", [P, 2, C])
            w_xt = sc("w_xt", [D0, H0, C])
            bx_cols = sc("bx_cols", [D0, H0, P])
            b_x = sc("b_x", [D0, H0])
            inv_temp = sc("inv_temp", [P, H0])
            s_wx = sem("w_x_in")
            block = scope.enter_context(nc.Block())
            per_head = "p (h g) -> p h g"

            @block.sync
            def _(sp):
                sp.dma_start(w_xt[:], a["w_xt"]).then_inc(s_wx, 16)
                sp.dma_start(b_x[:], a["b_x"]).then_inc(s_wx, 16)

                for table in sums_dram:
                    sp.dma_start(table.rearrange("(t p) w -> p t w", p=P),
                                 q_tab[:, 0:SUMW].unsqueeze(1).broadcast_to((P, TILES + 1, SUMW))).then_inc(s_zeroed, 16)
                sp.wait_ge(s_zeroed, 16 * U)

            @block.gpsimd
            def _(pool):
                pipeline(pool, TILES, 2, [(0, pool_norm(pool))])

            @block.vector
            def _(dve):
                link = Chain(dve, s_fchain, 0, 4)
                link(dve.tensor_scalar(inv_temp[:], bias["temperature"][:], 0.1, 5.0, ALU.max, ALU.min))
                link(dve.reciprocal(inv_temp[:], inv_temp[:]))
                dve.wait_ge(s_wx, 32)
                for h in range(H0):
                    dve.tensor_scalar(bx_cols[:, h, :], ones[0:D0, :], b_x[:, h:h + 1], None, ALU.mult).then_inc(s_bcol, 1)
                dve.wait_ge(s_fold_mm, 1)
                scale = inv_temp[:].unsqueeze(2).broadcast_to((P, H0, G0))
                for k in range(KC):
                    dve.tensor_tensor(w_logits[:, k, :].rearrange(per_head, h=H0), bank[k][:].rearrange(per_head, h=H0),
                                      scale, ALU.mult).then_inc(s_fold, 1)
                link(dve.tensor_tensor(b_logits[:].rearrange(per_head, h=H0), bank[2][:].rearrange(per_head, h=H0),
                                       bias["b_slice"][:].unsqueeze(1).broadcast_to((P, H0, G0)), ALU.add))
                dve.tensor_tensor(b_logits[:].rearrange(per_head, h=H0), b_logits[:].rearrange(per_head, h=H0),
                                  scale, ALU.mult).then_inc(s_fold, 1)
                dve.tensor_tensor(b1_mlp[:], bank[3][:, 0:MC], w["l1_b1"][:], ALU.add).then_inc(s_fold, 1)
                for k in range(KC):
                    dve.tensor_scalar(w["l1_w1t"][:, k, :], w["l1_w1t"][:, k, :], w["ln_g"][:, k:k + 1], None,
                                      ALU.mult).then_inc(s_fold, 1)
                link(dve.tensor_tensor(bias["b1"][:], bias["b1"][:], bias["b2"][:], ALU.add))
                dve.wait_ge(s_fold, 2 * KC + 2)

                def row_of(t):
                    return x[:, bass.ds(t, 1), :].rearrange("p a c -> p (a c)")

                def normalize(t, u):
                    if not early(t, 2):
                        dve.wait_ge(s_xt, t - 1)
                        dve.wait_ge(s_kept, t - 1)
                    apply(dve, row_of(t), xn[:, u, :], t, u, s_xn)

                def add(t, u):
                    dve.wait_ge(s_mm, t + 1)
                    row = x[:, bass.ds(t, 1), :].rearrange("p a c -> p (a c)")
                    link = Chain(dve, s_addchain, t, 1)
                    link(dve.tensor_tensor(row, row, bank[6 + u][:, 0:C], ALU.add))
                    dve.tensor_tensor(row, row, bias["b1"][:], ALU.add).then_inc(s_added, 1)
                pipeline(dve, TILES, 2, [(0, lambda t, u: measure(dve, Chain(dve, s_nchain, t, 1), row_of(t), t, u)),
                                         (1, normalize), (3, add)])
                dve.wait_ge(s_added, TILES)

            @block.scalar
            def _(act):
                def copy(t, u):
                    act.wait_ge(s_xt, t + 1)
                    if not early(t, 2):
                        act.wait_ge(s_mm, t - 1)
                    act.copy(xnt[:, u, :], bank[4 + u][:, 0:C]).then_inc(s_xtc, 1)

                def keep(t, u):
                    act.wait_ge(s_xn, t + 1)
                    act.copy(acc[:, bass.ds(t * ACCW, C)], xn[:, u, :]).then_inc(s_kept, 1)
                pipeline(act, TILES, 2, [(1, keep), (1, copy)])
                act.wait_ge(s_kept, TILES)

            @block.tensor
            def _(pe):
                pe.wait_ge(s_wx, 32)
                pe.wait_ge(s_bcol, H0)
                for h in range(H0):
                    cols = slice(h * G0, (h + 1) * G0)
                    for k in range(KC):
                        pe.matmul(bank[k][:, cols], w_xt[:, h, k * P:(k + 1) * P], w["w_slice"][:], start=True, stop=True)
                    pe.matmul(bank[2][:, cols], bx_cols[:, h, :], w["w_slice"][:], start=True, stop=True)
                for m in range(MC):
                    for k in range(KC):
                        mm = pe.matmul(bank[3][:, m:m + 1], w["l1_w1t"][:, k, m * P:(m + 1) * P], w["ln_b"][:, k:k + 1],
                                       start=(k == 0), stop=(k == KC - 1))
                mm.then_inc(s_fold_mm, 1)

                def turn_rows(t, u):
                    pe.wait_ge(s_xn, t + 1)
                    if not early(t, 2):
                        pe.wait_ge(s_xtc, t - 1)
                    for k in range(KC):
                        mm = pe.transpose(bank[4 + u][:, k * P:(k + 1) * P], xn[:, u, k * P:(k + 1) * P], ident[:])
                    mm.then_inc(s_xt, 1)

                def product(t, u):
                    pe.wait_ge(s_xtc, t + 1)
                    if not early(t, 2):
                        pe.wait_ge(s_added, t - 1)
                    for k in range(KC):
                        mm = pe.matmul(bank[6 + u][:, 0:C], xnt[:, u, k * P:(k + 1) * P], w["l0_w1t"][:, k, :],
                                       start=(k == 0), stop=(k == KC - 1))
                    mm.then_inc(s_mm, 1)
                pipeline(pe, TILES, 2, [(1, turn_rows), (2, product)])

        E = SLOTS
        G = STEP_UNROLL
        s_oh, s_eq, s_dup, s_const = sem("m_onehot_ready"), sem("m_equal_ready"), sem("m_earlier_ready"), sem("m_constants_ready")
        s_max, s_target = sem("m_duplicates_found"), sem("m_target_ready")
        s_spread, s_spreadc = sem("m_spread_ready"), sem("m_spread_copied")
        s_sum, s_total = sem("m_sum_ready"), sem("m_total_copied")
        s_seg = [sem(f"m_first_ends_landed{u}") for u in range(2)]
        s_add = [sem(f"m_rows_added{u}") for u in range(U)]
        with ExitStack() as scope:
            def sc(name, shape, dt=F32):
                return scope.enter_context(nc.sbuf_tensor(name, shape, dt))
            target = sc("m_target", [P, G], U32)
            first_row = sc("m_first_row", [P, G, P])
            onehot, equal = sc("m_onehot", [P, E, P], BF16), sc("m_equal", [P, E, P], BF16)
            before, earlier = sc("m_before", [P, P]), sc("m_earlier", [P, 2, P])
            dup, spare, spare_i = sc("m_dup", [P, E]), sc("m_spare", [P, 1]), sc("m_spare_i", [P, 1], I32)
            to_spare = sc("m_to_spare", [P, STEP_TABLE])
            spread = slice_out[:].rearrange("p m c -> p (m c)")[:, 0:U * P].rearrange("p (u n) -> p u n", u=U)
            total = sc("m_total", [P, U, SUMW])
            block = scope.enter_context(nc.Block())

            @block.sync
            def _(sp):
                def load_first(g, u):
                    if not early(g, 2):
                        sp.wait_ge(s_eq, E * (g - 1))
                        sp.wait_ge(s_dup, E * (g - 1))
                    sp.dma_start(first_row[:, u * E:(u + 1) * E, :],
                                 step_src_dram[bass.ds(g * E, E), :].unsqueeze(0).broadcast_to((P, E, P))
                                 ).then_inc(s_seg[u], 16)
                pipeline(sp, STEPS_RUN // E, 2, [(0, load_first)])

            @block.scalar
            def _(act):
                def copy_spread(s, u):
                    act.wait_ge(s_spread, s + 1)
                    if not early(s, U):
                        act.wait_ge(s_sum, s - (U - 1))
                    act.copy(spread[:, u % U, :], bank[u % 2][:, 0:P]).then_inc(s_spreadc, 1)

                def copy_total(s, u):
                    act.wait_ge(s_sum, s + 1)
                    if not early(s, U):
                        act.wait_ge(s_add[u % U], landed(s, u % U, U) - 16)
                    act.copy(total[:, u % U, :], bank[2 + u % 2][:, 0:SUMW]).then_inc(s_total, 1)
                pipeline(act, STEPS_RUN, G, [(ADD_LAG, copy_total), (4, copy_spread)])

            @block.gpsimd
            def _(pool):
                pool.memset(before[:], 1.0).then_inc(s_const, 1)
                pool.iota(spare_i[:], pattern=[[0, 1]], base=ROWS, channel_multiplier=1).then_inc(s_const, 1)
                pool.wait_ge(s_const, 2)
                pool.affine_select(out=before[:], in_=before[:], compare_op=ALU.is_gt, fill=0.0, base=0,
                                   pattern=[[-1, P]], channel_multiplier=1).then_inc(s_const, 1)

                def add(s, u):
                    if not early(s, U):
                        pool.wait_ge(s_add[u % U], landed(s, u % U, U) - 16)
                    pool.wait_ge(s_target, s + 1)
                    fence(pool, s_total, s + 1)
                    pool.indirect_dma_start(out=sums_dram[u % U], in_=total[:, u % U, :], in_offset=None,
                                            out_offset=bass.IndirectOffsetOnAxis(ap=target[:, u:u + 1], axis=0),
                                            compute_op=ALU.add).then_inc(s_add[u % U], 16)
                pipeline(pool, STEPS_RUN, G, [(7, add)])
                for u in range(U):
                    pool.wait_ge(s_add[u], 16 * (STEPS_RUN // U))

            @block.vector
            def _(dve):
                dve.wait_ge(s_const, 3)
                dve.tensor_copy(spare[:], spare_i[:]).then_inc(s_const, 1)
                dve.wait_ge(s_const, 4)
                dve.tensor_scalar(to_spare[:], src_step[:], -1.0, spare[:], ALU.mult, ALU.add).then_inc(s_const, 1)
                dve.wait_ge(s_const, 5)

                def find_earlier(s, u):
                    if u % E == 0:
                        dve.wait_ge(s_seg[u // E], landed(s, u, G))
                    dve.scalar_tensor_tensor(out=earlier[:, u % 2, :], in0=first_row[:, u, :], scalar=src_step[:, bass.ds(s, 1)],
                                             in1=before[:], op0=ALU.is_equal, op1=ALU.mult).then_inc(s_dup, 1)

                def make_onehot(s, u):
                    if not early(s, E):
                        dve.wait_ge(s_spread, s - (E - 1))
                    dve.tensor_scalar(onehot[:, u % E, :], iota_row[:], dst_step[:, bass.ds(s, 1)], None,
                                      ALU.is_equal).then_inc(s_oh, 1)

                def any_earlier(s, u):
                    dve.wait_ge(s_dup, s + 1)
                    dve.tensor_reduce(dup[:, u % E:u % E + 1], earlier[:, u % 2, :], AX, ALU.max).then_inc(s_max, 1)

                def compare(s, u):
                    dve.tensor_scalar(equal[:, u % E, :], first_row[:, u, :], src_step[:, bass.ds(s, 1)], None,
                                      ALU.is_equal).then_inc(s_eq, 1)

                def choose(s, u):
                    dve.wait_ge(s_max, s + 1)
                    if not early(s, E):
                        dve.wait_ge(s_add[u % U], landed(s, u % U, U) - 16)
                    dve.scalar_tensor_tensor(out=target[:, u:u + 1], in0=dup[:, u % E:u % E + 1],
                                             scalar=to_spare[:, bass.ds(s, 1)], in1=src_step[:, bass.ds(s, 1)],
                                             op0=ALU.mult, op1=ALU.add).then_inc(s_target, 1)
                pipeline(dve, STEPS_RUN, G, [(2, find_earlier), (2, make_onehot), (2, any_earlier), (2, compare),
                                             (5, choose)])

            @block.tensor
            def _(pe):
                offsets = [None] * G

                def load_offsets(i, v):
                    if v % LOADS == 0:
                        offsets[v:v + LOADS] = nc.values_load_multi_w_load_instructions(
                            acc_off[0:1, bass.ds(i, LOADS)], engines=(mybir.EngineType.PE,), min_val=0,
                            max_val=(TILES - 1) * ACCW)[1]

                def count_ends(s, u):
                    pe.wait_ge(s_oh, s + 1)
                    pe.wait_ge(s_eq, s + 1)
                    if not early(s, 2):
                        pe.wait_ge(s_spreadc, s - 1)
                    pe.matmul(bank[u % 2][:, 0:P], onehot[:, u % E, :], equal[:, u % E, :], start=True, stop=True).then_inc(s_spread, 1)

                def sum_rows(s, u):
                    pe.wait_ge(s_spreadc, s + 1)
                    if not early(s, 2):
                        pe.wait_ge(s_total, s - 1)
                    pe.matmul(bank[2 + u % 2][:, 0:SUMW], spread[:, u % U, :],
                              acc[:, bass.ds(offsets[(u + ADD_LAG) % G], SUMW)], start=True, stop=True).then_inc(s_sum, 1)
                pipeline(pe, STEPS_RUN, G, [(ADD_LAG, sum_rows), (4, count_ends)], load_offsets)


        pool_norm, measure, apply = normalize_stages(0)
        s_mean, s_meant, s_meantc = sem("b_mean_ready"), sem("b_mean_transposed"), sem("b_meant_copied")
        s_mm2 = sem("b_product_ready")
        s_xn, s_xt, s_xtc = sem("b_xn_ready"), sem("b_xn_transposed"), sem("b_xnt_copied")
        s_log, s_shift, s_exp, s_wgt = sem("b_logits_ready"), sem("b_shifted"), sem("b_exp_ready"), sem("b_weights_ready")
        s_wsum, s_u, s_wt, s_wtc = sem("b_weights_summed"), sem("b_sliced"), sem("b_weights_transposed"), sem("b_wt_copied")
        s_c0, s_c1, s_c2, s_c3 = sem("b_mean_chain"), sem("b_norm_chain"), sem("b_shift_chain"), sem("b_weigh_chain")
        s_init, s_added = sem("b_zeroed"), sem("b_added")
        s_store = [sem(f"b_wt_stored{u}") for u in range(2)]
        s_load = [sem(f"b_sums_landed{u}") for u in range(2)]
        wsum = sb("wsum", [P, INNER])
        with ExitStack() as scope:
            def sc(name, shape, dt=F32):
                return scope.enter_context(nc.sbuf_tensor(name, shape, dt))
            mean, meant, xnt = sc("b_mean", [P, 2, C]), sc("b_meant", [P, 2, C]), sc("b_xnt", [P, 2, C])
            cnt, hmax, hsum = sc("b_cnt", [P, 1]), sc("b_hmax", [P, H0]), sc("b_hsum", [P, H0])
            wt = sc("b_wt", [P, 2, INNER])
            n_sums, n_xn = 2 * U * SUMW, 4 * C
            sums = q_tab[:, 0:n_sums].rearrange("p (u k w) -> p u k w", u=2, k=U)
            xn = q_tab[:, n_sums:n_sums + n_xn].rearrange("p (u c) -> p u c", u=4)
            soft_flat = q_tab[:, n_sums + n_xn:n_sums + n_xn + 4 * INNER].rearrange("p (u n) -> p u n", u=4)
            soft = soft_flat.rearrange("p u (h g) -> p u h g", h=H0)
            sums_of = sc("b_sums_of", [P, SUMW])
            block = scope.enter_context(nc.Block())

            @block.sync
            def _(sp):
                def load(t, u):
                    if not early(t, 2):
                        sp.wait_ge(s_mean, t - 1)
                    for i, table in enumerate(sums_dram):
                        sp.dma_start(sums[:, u % 2, i, :], table.rearrange("(t p) w -> p t w", p=P)[:, bass.ds(t, 1), :]
                                     ).then_inc(s_load[u % 2], 16)

                def store(t, u):
                    sp.wait_ge(s_wtc, t + 1)
                    sp.dma_start(wt_rows[:, bass.ds(t, 1), :], wt[:, u % 2:u % 2 + 1, :]).then_inc(s_store[u % 2], 16)
                pipeline(sp, TILES, 4, [(0, load), (6, store)])
                for u in range(2):
                    sp.wait_ge(s_store[u], 16 * len(range(u, TILES, 2)))

            @block.gpsimd
            def _(pool):
                pool.memset(wsum[:], 0.0).then_inc(s_init, 1)
                pool.wait_ge(s_init, 1)

                def sum_weights(t, u):
                    if not early(t, 1):
                        pool.wait_ge(s_wsum, t)
                    fence(pool, s_wgt, t + 1)
                    pool.tensor_tensor(wsum[:], wsum[:], soft_flat[:, u, :], ALU.add).then_inc(s_wsum, 1)
                pipeline(pool, TILES, 4, [(6, sum_weights), (2, pool_norm(pool))])
                pool.wait_ge(s_wsum, TILES)

            @block.vector
            def _(dve):
                def node_mean(t, u):
                    if not early(t, 2):
                        dve.wait_ge(s_meant, t - 1)
                    dve.wait_ge(s_load[u % 2], U * landed(t, u % 2, 2))
                    if not early(t, 1):
                        dve.wait_ge(s_mean, t)
                    link = Chain(dve, s_c0, 3 * t, 3)
                    link(dve.tensor_reduce(sums_of[:], sums[:, u % 2, :, :].rearrange("p k w -> p w k"), AX, ALU.add))
                    link(dve.tensor_scalar(cnt[:], sums_of[:, C:SUMW], 1.0, None, ALU.max))
                    link(dve.reciprocal(cnt[:], cnt[:]))
                    dve.tensor_scalar(mean[:, u % 2, :], sums_of[:, 0:C], cnt[:], None, ALU.mult
                                      ).then_inc(s_mean, 1)

                def row_of(t):
                    return x[:, bass.ds(t, 1), :].rearrange("p a c -> p (a c)")

                def add_and_measure(t, u):
                    dve.wait_ge(s_mm2, t + 1)
                    dve.tensor_tensor(row_of(t), row_of(t), bank[1][:, 0:C], ALU.add).then_inc(s_added, 1)
                    dve.wait_ge(s_added, t + 1)
                    measure(dve, Chain(dve, s_c1, t, 1), row_of(t), t, u)

                def normalize(t, u):
                    if not early(t, 4):
                        dve.wait_ge(s_u, t - 3)
                    apply(dve, row_of(t), xn[:, u, :], t, u, s_xn)

                def shift(t, u):
                    dve.wait_ge(s_log, t + 1)
                    if not early(t, 4):
                        dve.wait_ge(s_wt, t - 3)
                        dve.wait_ge(s_wsum, t - 3)
                    link = Chain(dve, s_c2, 2 * t, 2)
                    link(dve.tensor_tensor(soft_flat[:, u, :], bank[3][:], b_logits[:], ALU.add))
                    link(dve.tensor_reduce(hmax[:], soft[:, u, :, :], AX, ALU.max))
                    dve.tensor_tensor(soft[:, u, :, :], soft[:, u, :, :],
                                      hmax[:].unsqueeze(2).broadcast_to((P, H0, G0)), ALU.subtract).then_inc(s_shift, 1)

                def weigh(t, u):
                    dve.wait_ge(s_exp, t + 1)
                    link = Chain(dve, s_c3, 3 * t, 3)
                    link(dve.tensor_reduce(hsum[:], soft[:, u, :, :], AX, ALU.add))
                    link(dve.reciprocal(hsum[:], hsum[:]))
                    link(dve.tensor_scalar(hsum[:], hsum[:], valid[:, bass.ds(t, 1)], None, ALU.mult))
                    dve.tensor_tensor(soft[:, u, :, :], soft[:, u, :, :],
                                      hsum[:].unsqueeze(2).broadcast_to((P, H0, G0)), ALU.mult).then_inc(s_wgt, 1)
                pipeline(dve, TILES, 4, [(3, normalize), (5, weigh), (2, add_and_measure), (0, node_mean), (4, shift)])

            @block.scalar
            def _(act):
                def copy_wt(t, u):
                    act.wait_ge(s_wt, t + 1)
                    if not early(t, 2):
                        act.wait_ge(s_store[u % 2], landed(t, u % 2, 2) - 16)
                    act.copy(wt[:, u % 2, :], bank[7][:]).then_inc(s_wtc, 1)

                def exponent(t, u):
                    act.wait_ge(s_shift, t + 1)
                    act.activation(soft_flat[:, u, :], soft_flat[:, u, :], ACT.Exp).then_inc(s_exp, 1)

                def copy_xnt(t, u):
                    act.wait_ge(s_xt, t + 1)
                    if not early(t, 2):
                        act.wait_ge(s_log, t - 1)
                    act.copy(xnt[:, u % 2, :], bank[2][:, 0:C]).then_inc(s_xtc, 1)

                def copy_meant(t, u):
                    act.wait_ge(s_meant, t + 1)
                    if not early(t, 2):
                        act.wait_ge(s_mm2, t - 1)
                    act.copy(meant[:, u % 2, :], bank[0][:, 0:C]).then_inc(s_meantc, 1)
                pipeline(act, TILES, 4, [(6, copy_wt), (1, copy_meant), (3, copy_xnt), (4, exponent)])

            @block.tensor
            def _(pe):
                def slices(t, u):
                    pe.wait_ge(s_wgt, t + 1)
                    for m in range(INNER // P):
                        mm = pe.matmul(bank[5 + m // 2][:, (m % 2) * C:(m % 2 + 1) * C], soft_flat[:, u, m * P:(m + 1) * P],
                                       xn[:, u, :], start=(early(t, 1) and m % 2 == 0), stop=False, skip_group_check=True)
                    mm.then_inc(s_u, 1)
                    if not early(t, 1):
                        pe.wait_ge(s_wtc, t)
                    for m in range(INNER // P):
                        mm = pe.transpose(bank[7][:, m * P:(m + 1) * P], soft_flat[:, u, m * P:(m + 1) * P], ident[:])
                    mm.then_inc(s_wt, 1)

                def logits(t, u):
                    pe.wait_ge(s_xtc, t + 1)
                    if not early(t, 1):
                        pe.wait_ge(s_shift, t)
                    for k in range(KC):
                        mm = pe.matmul(bank[3][:], xnt[:, u % 2, k * P:(k + 1) * P], w_logits[:, k, :],
                                       start=(k == 0), stop=(k == KC - 1))
                    mm.then_inc(s_log, 1)

                def project_mean(t, u):
                    pe.wait_ge(s_meantc, t + 1)
                    if not early(t, 1):
                        pe.wait_ge(s_added, t)
                    for k in range(KC):
                        mm = pe.matmul(bank[1][:, 0:C], meant[:, u % 2, k * P:(k + 1) * P], w["l0_w2t"][:, k, :],
                                       start=(k == 0), stop=(k == KC - 1))
                    mm.then_inc(s_mm2, 1)

                def turn_xn(t, u):
                    pe.wait_ge(s_xn, t + 1)
                    if not early(t, 1):
                        pe.wait_ge(s_xtc, t)
                    for k in range(KC):
                        mm = pe.transpose(bank[2][:, k * P:(k + 1) * P], xn[:, u, k * P:(k + 1) * P], ident[:])
                    mm.then_inc(s_xt, 1)

                def turn_mean(t, u):
                    pe.wait_ge(s_mean, t + 1)
                    if not early(t, 1):
                        pe.wait_ge(s_meantc, t)
                    for k in range(KC):
                        mm = pe.transpose(bank[0][:, k * P:(k + 1) * P], mean[:, u % 2, k * P:(k + 1) * P], ident[:])
                    mm.then_inc(s_meant, 1)
                pipeline(pe, TILES, 4, [(6, slices), (1, turn_mean), (4, logits), (3, turn_xn), (1, project_mean)])

        s_cv, s_cp, s_ca = sem("c_vector_steps"), sem("c_tensor_steps"), sem("c_exp_ready")
        s_pack = sem("c_slice_out_packed")
        with ExitStack() as scope:
            def sc(name, shape, dt=F32):
                return scope.enter_context(nc.sbuf_tensor(name, shape, dt))
            MI = INNER // P
            un = q_tab[:, 0:MI * C].rearrange("p (m c) -> p m c", m=MI)
            norm = sc("c_norm", [P, MI])
            share = sc("c_share", [P, MI])
            unt = q_tab[:, MI * C:MI * C + KC * INNER].rearrange("p (k n) -> p k n", k=KC)
            share_t = sc("c_share_t", [1, INNER])
            tokens_t = sc("c_tokens_t", [D0, INNER])
            qt, kt, vt = (sc("c_" + n, [D0, INNER]) for n in ("qt", "kt", "vt"))
            prob = sc("c_prob", [G0, H0, G0])
            prob_t = sc("c_prob_t", [G0, H0, G0])
            smax, ssum = sc("c_smax", [G0, H0]), sc("c_ssum", [G0, H0])
            vout = acc[0:G0, 0:H0 * C].rearrange("p (h c) -> p h c", h=H0)
            attended = acc[0:G0, H0 * C:2 * H0 * C].rearrange("p (h c) -> p h c", h=H0)
            block = scope.enter_context(nc.Block())

            C_SHARE = 3 + MI + 1
            C_SHT = C_SHARE + KC + 1
            C_TOK = C_SHT + 1
            C_VT = C_TOK + 3
            C_SUB = C_VT + 3
            C_PROB = C_SUB + 3
            C_PROBT = C_PROB + 1
            C_LAST = C_PROBT + H0
            T_NORM, T_UNT, T_TOK, T_QKV, T_SCORE, T_PROBT = range(1, 7)
            T_VOUT = T_PROBT + H0 // 2

            @block.vector
            def _(dve):
                count = [0]

                def link(ins):
                    ins.then_inc(s_cv, 1)
                    count[0] += 1
                    dve.wait_ge(s_cv, count[0])
                dve.wait_ge(s_cp, T_NORM)
                link(dve.tensor_copy(norm[:], bank[0][:, 0:MI]))
                link(dve.tensor_scalar(share[:], norm[:], 1e-5, None, ALU.add))
                link(dve.reciprocal(share[:], share[:]))
                for m in range(MI):
                    link(dve.tensor_scalar(un[:, m, :], bank[5 + m // 2][:, (m % 2) * C:(m % 2 + 1) * C], share[:, m:m + 1],
                                           None, ALU.mult))
                link(dve.tensor_tensor(share[:], share[:], norm[:], ALU.mult))
                dve.wait_ge(s_cp, T_UNT)
                for k in range(KC):
                    link(dve.tensor_copy(unt[:, k, :], bank[1 + k][:]))
                link(dve.tensor_copy(share_t[:], bank[3][0:1, :]))
                dve.wait_ge(s_cp, T_TOK)
                link(dve.tensor_copy(tokens_t[:], bank[4][0:D0, :]))
                dve.wait_ge(s_cp, T_QKV)
                link(dve.tensor_copy(qt[:], bank[0][0:D0, :]))
                link(dve.tensor_copy(kt[:], bank[1][0:D0, :]))
                link(dve.tensor_copy(vt[:], bank[2][0:D0, :]))
                dve.wait_ge(s_cp, T_SCORE)
                link(dve.tensor_scalar(prob[:], bank[3][0:G0, :].rearrange("p (h g) -> p h g", h=H0), float(D0) ** -0.5,
                                       None, ALU.mult))
                link(dve.tensor_reduce(smax[:], prob[:], AX, ALU.max))
                link(dve.tensor_tensor(prob[:], prob[:], smax[:].unsqueeze(2).broadcast_to((G0, H0, G0)), ALU.subtract))
                dve.wait_ge(s_ca, 1)
                link(dve.tensor_reduce(ssum[:], prob[:], AX, ALU.add))
                link(dve.reciprocal(ssum[:], ssum[:]))
                link(dve.tensor_tensor(prob[:], prob[:], ssum[:].unsqueeze(2).broadcast_to((G0, H0, G0)), ALU.mult))
                dve.wait_ge(s_cp, T_PROBT)
                link(dve.tensor_copy(prob_t[:], bank[0][0:G0, :].rearrange("p (h g) -> p h g", h=H0)))
                for i in range(H0 // 2):
                    dve.wait_ge(s_cp, T_PROBT + 1 + i)
                    link(dve.tensor_copy(vout[:, 2 * i:2 * i + 2, :], bank[1 + i][0:G0, :].rearrange("p (h c) -> p h c", h=2)))
                for i in range(H0 // 2):
                    dve.wait_ge(s_cp, T_VOUT + 1 + i)
                    link(dve.tensor_copy(attended[:, 2 * i:2 * i + 2, :],
                                         bank[(5, 6, 7, 0)[i]][0:G0, :].rearrange("p (h c) -> p h c", h=2)))
                assert count[0] == C_LAST

            @block.scalar
            def _(act):
                act.wait_ge(s_cv, C_SUB)
                act.activation(prob[:], prob[:], ACT.Exp).then_inc(s_ca, 1)

            @block.tensor
            def _(pe):
                for m in range(MI):
                    mm = pe.matmul(bank[0][:, m:m + 1], wsum[:, m * P:(m + 1) * P], ones[:, 0:1], start=True, stop=True)
                mm.then_inc(s_cp, 1)
                pe.wait_ge(s_cv, C_SHARE)
                for m in range(MI):
                    for k in range(KC):
                        pe.transpose(bank[1 + k][:, m * P:(m + 1) * P], un[:, m, k * P:(k + 1) * P], ident[:])
                    mm = pe.transpose(bank[3][0:1, m * P:(m + 1) * P], share[:, m:m + 1], ident[:])
                mm.then_inc(s_cp, 1)
                pe.wait_ge(s_cv, C_SHT)
                for h in range(H0):
                    cols = slice(h * G0, (h + 1) * G0)
                    for k in range(KC):
                        pe.matmul(bank[4][0:D0, cols], w["l0_fx"][:, k, cols], unt[:, k, cols], start=(k == 0), stop=False)
                    mm = pe.matmul(bank[4][0:D0, cols], w["b_fx_row"][0:1, cols], share_t[0:1, cols], start=False, stop=True)
                mm.then_inc(s_cp, 1)
                pe.wait_ge(s_cv, C_TOK)
                for i, name in enumerate(("w_q", "w_k", "w_v")):
                    mm = pe.matmul(bank[i][0:D0, :], w[name][:], tokens_t[:], start=True, stop=True)
                mm.then_inc(s_cp, 1)
                pe.wait_ge(s_cv, C_VT)
                for h in range(H0):
                    cols = slice(h * G0, (h + 1) * G0)
                    mm = pe.matmul(bank[3][0:G0, cols], qt[:, cols], kt[:, cols], start=True, stop=True)
                mm.then_inc(s_cp, 1)
                pe.wait_ge(s_cv, C_PROB)
                for h in range(H0):
                    mm = pe.transpose(bank[0][0:G0, h * G0:(h + 1) * G0], prob[:, h, :], ident[0:G0, 0:G0])
                mm.then_inc(s_cp, 1)
                for i in range(H0 // 2):
                    for h in (2 * i, 2 * i + 1):
                        mm = pe.matmul(bank[1 + i][0:G0, (h % 2) * C:(h % 2 + 1) * C], vt[:, h * G0:(h + 1) * G0],
                                       w["l0_slice_out"][:, h, :], start=True, stop=True)
                    mm.then_inc(s_cp, 1)
                for i in range(H0 // 2):
                    pe.wait_ge(s_cv, C_PROBT + 1 + i)
                    for h in (2 * i, 2 * i + 1):
                        mm = pe.matmul(bank[(5, 6, 7, 0)[i]][0:G0, (h % 2) * C:(h % 2 + 1) * C], prob_t[:, h, :], vout[:, h, :],
                                       start=True, stop=True)
                    mm.then_inc(s_cp, 1)

            @block.sync
            def _(sp):
                sp.wait_ge(s_cv, C_LAST)
                pairs = attended.rearrange("p (m two) c -> p two m c", two=2)
                for half in range(2):
                    sp.dma_start(slice_out[half * G0:(half + 1) * G0, :, :], pairs[:, half, :, :]).then_inc(s_pack, 16)
                sp.wait_ge(s_pack, 32)

        pool_norm, measure, apply = normalize_stages(0)
        s_o, s_xn, s_xt, s_xtc = sem("d_slices_ready"), sem("d_xn_ready"), sem("d_xn_transposed"), sem("d_xnt_copied")
        s_qkv, s_q, s_kv = sem("d_products_ready"), sem("d_queries_kept"), sem("d_kv_ready")
        s_c1, s_zero, s_added = sem("d_norm_chain"), sem("d_acc_zeroed"), sem("d_added")
        s_load = [sem(f"d_wt_landed{u}") for u in range(2)]
        s_store = [sem(f"d_kv_stored{u}") for u in range(2)]
        with ExitStack() as scope:
            def sc(name, shape, dt=F32):
                return scope.enter_context(nc.sbuf_tensor(name, shape, dt))
            wt = sc("d_wt", [P, 2, INNER])
            xn, xnt = sc("d_xn", [P, 2, C]), sc("d_xnt", [P, 2, C])
            kv = sc("d_kv", [P, 2, 2 * C])
            block = scope.enter_context(nc.Block())

            @block.sync
            def _(sp):
                def load(t, u):
                    if not early(t, 2):
                        sp.wait_ge(s_o, t - 1)
                    sp.dma_start(wt[:, u:u + 1, :], wt_rows[:, bass.ds(t, 1), :]).then_inc(s_load[u], 16)
                pipeline(sp, TILES, 2, [(0, load)])

            @block.gpsimd
            def _(pool):
                pool.memset(acc[:], 0.0).then_inc(s_zero, 1)
                pipeline(pool, TILES, 2, [(1, pool_norm(pool))])
                pool.wait_ge(s_zero, 1)

            @block.vector
            def _(dve):
                def keep(t, u):
                    dve.wait_ge(s_qkv, t + 1)
                    dve.tensor_tensor(q_tab[:, bass.ds(t * C, C)], bank[4 + u][:, 0:C], bias["bq"][:], ALU.add
                                      ).then_inc(s_q, 1)
                    if not early(t, 2):
                        dve.wait_ge(s_store[u], landed(t, u, 2) - 16)
                    dve.tensor_tensor(kv[:, u, :], bank[6 + u][:], bias["bkv"][:], ALU.add).then_inc(s_kv, 1)

                def row_of(t):
                    return x[:, bass.ds(t, 1), :].rearrange("p a c -> p (a c)")

                def add_and_measure(t, u):
                    dve.wait_ge(s_o, t + 1)
                    dve.tensor_tensor(row_of(t), row_of(t), bank[u][:, 0:C], ALU.add).then_inc(s_added, 1)
                    dve.wait_ge(s_added, t + 1)
                    link = Chain(dve, s_c1, 2 * t, 2)
                    link(dve.tensor_tensor(row_of(t), row_of(t), bias["b_out"][:], ALU.add))
                    measure(dve, link, row_of(t), t, u)

                def normalize(t, u):
                    if not early(t, 2):
                        dve.wait_ge(s_xt, t - 1)
                    apply(dve, row_of(t), xn[:, u, :], t, u, s_xn)
                pipeline(dve, TILES, 2, [(2, normalize), (1, add_and_measure), (4, keep)])
                dve.wait_ge(s_q, TILES)

            @block.scalar
            def _(act):
                def copy_xnt(t, u):
                    act.wait_ge(s_xt, t + 1)
                    if not early(t, 2):
                        act.wait_ge(s_qkv, t - 1)
                    act.copy(xnt[:, u, :], bank[2 + u][:, 0:C]).then_inc(s_xtc, 1)

                def store(t, u):
                    act.wait_ge(s_kv, t + 1)
                    act.dma_start(kv_rows[:, bass.ds(t, 1), :], kv[:, u:u + 1, :]).then_inc(s_store[u], 16)
                pipeline(act, TILES, 2, [(2, copy_xnt), (4, store)])
                for u in range(2):
                    act.wait_ge(s_store[u], 16 * len(range(u, TILES, 2)))

            @block.tensor
            def _(pe):
                def project(t, u):
                    pe.wait_ge(s_xtc, t + 1)
                    if not early(t, 2):
                        pe.wait_ge(s_kv, t - 1)
                    for k in range(KC):
                        pe.matmul(bank[4 + u][:, 0:C], xnt[:, u, k * P:(k + 1) * P], w["l1_qt"][:, k, :],
                                  start=(k == 0), stop=(k == KC - 1))
                    for k in range(KC):
                        mm = pe.matmul(bank[6 + u][:], xnt[:, u, k * P:(k + 1) * P], w["l1_kvt"][:, k, :],
                                       start=(k == 0), stop=(k == KC - 1))
                    mm.then_inc(s_qkv, 1)

                def spread_slices(t, u):
                    pe.wait_ge(s_load[u], landed(t, u, 2))
                    if not early(t, 2):
                        pe.wait_ge(s_added, t - 1)
                    for m in range(INNER // P):
                        mm = pe.matmul(bank[u][:, 0:C], wt[:, u, m * P:(m + 1) * P], slice_out[:, m, :],
                                       start=(m == 0), stop=(m == INNER // P - 1))
                    mm.then_inc(s_o, 1)

                def turn_xn(t, u):
                    pe.wait_ge(s_xn, t + 1)
                    if not early(t, 2):
                        pe.wait_ge(s_xtc, t - 1)
                    for k in range(KC):
                        mm = pe.transpose(bank[2 + u][:, k * P:(k + 1) * P], xn[:, u, k * P:(k + 1) * P], ident[:])
                    mm.then_inc(s_xt, 1)
                pipeline(pe, TILES, 2, [(0, spread_slices), (2, turn_xn), (3, project)])

        s_idx, s_oh, s_oht, s_ohc = sem("e_index_ready"), sem("e_onehot_ready"), sem("e_onehot_transposed"), sem("e_oht_copied")
        s_qe, s_prod, s_clip, s_exp = sem("e_queries_spread"), sem("e_product_ready"), sem("e_scores_clipped"), sem("e_exp_ready")
        s_msg, s_sum, s_acc, s_c = sem("e_message_ready"), sem("e_sum_ready"), sem("e_accumulated"), sem("e_scores_ready")
        s_land = [sem(f"e_kv_landed{u}") for u in range(E)]
        G = STEP_UNROLL
        with ExitStack() as scope:
            def sc(name, shape, dt=F32):
                return scope.enter_context(nc.sbuf_tensor(name, shape, dt))
            M = 4
            index = sc("e_index", [P, E], U32)
            kv = sc("e_kv", [P, E, 2 * C])
            onehot = w_logits[:].rearrange("p k n -> p (k n)").rearrange("p (s e) -> p s e", s=E)
            spent = slice_out[:].rearrange("p m c -> p (m c)")
            onehot_t = spent[:, 0:M * P].rearrange("p (s e) -> p s e", s=M)
            prod = spent[:, M * P:M * P + 2 * C].rearrange("p (s c) -> p s c", s=2)
            score = sc("e_score", [P, M, H1])
            msg = sc("e_msg", [P, M, ACCW])
            block = scope.enter_context(nc.Block())

            @block.gpsimd
            def _(pool):
                def gather(s, u):
                    if not early(s, E):
                        pool.wait_ge(s_msg, s - (E - 1))
                    fence(pool, s_idx, s + 1)
                    pool.indirect_dma_start(out=kv[:, u % E, :], out_offset=None, in_=kv_dram,
                                            in_offset=bass.IndirectOffsetOnAxis(ap=index[:, u % E:u % E + 1], axis=0)
                                            ).then_inc(s_land[u % E], 16)
                pipeline(pool, STEPS_RUN, G, [(0, gather)])

            @block.scalar
            def _(act):
                def exponent(s, u):
                    act.wait_ge(s_clip, s + 1)
                    if not early(s, M):
                        act.wait_ge(s_sum, s - (M - 1))
                    act.activation(msg[:, u % M, C:ACCW], score[:, u % M, :], ACT.Exp).then_inc(s_exp, 1)

                def copy_onehot_t(s, u):
                    act.wait_ge(s_oht, s + 1)
                    if not early(s, M):
                        act.wait_ge(s_qe, s - (M - 1))
                    act.copy(onehot_t[:, u % M, :], bank[u % 2][:, 0:P]).then_inc(s_ohc, 1)

                def fetch_index(s, u):
                    if not early(s, E):
                        fence(act, s_land[u % E], landed(s, u % E, E) - 16)
                    act.copy(index[:, u % E:u % E + 1], src_step[:, bass.ds(s, 1)]).then_inc(s_idx, 1)
                pipeline(act, STEPS_RUN, G, [(0, fetch_index), (3, exponent), (1, copy_onehot_t)])

            @block.vector
            def _(dve):
                heads = "p (h d) -> p h d"
                offsets = [None] * G

                def load_offsets(i, v):
                    if v == 0:
                        offsets[:] = nc.values_load_multi_w_load_instructions(
                            acc_off[0:1, bass.ds(i, G)], engines=(mybir.EngineType.DVE,), min_val=0,
                            max_val=(TILES - 1) * ACCW)[1]

                def make_onehot(s, u):
                    if not early(s, E):
                        dve.wait_ge(s_sum, s - (E - 1))
                    dve.tensor_scalar(onehot[:, u % E, :], iota_row[:], dst_step[:, bass.ds(s, 1)], None,
                                      ALU.is_equal).then_inc(s_oh, 1)

                def product(s, u):
                    dve.wait_ge(s_qe, s + 1)
                    dve.wait_ge(s_land[u % E], landed(s, u % E, E))
                    dve.scalar_tensor_tensor(out=prod[:, u % 2, :], in0=bank[2 + u % 2][:, 0:C], scalar=float(D1) ** -0.5,
                                             in1=kv[:, u % E, 0:C], op0=ALU.mult, op1=ALU.mult).then_inc(s_prod, 1)

                def scores(s, u):
                    dve.wait_ge(s_prod, s + 1)
                    dve.tensor_reduce(score[:, u % M, :], prod[:, u % 2, :].rearrange(heads, h=H1), AX, ALU.add
                                      ).then_inc(s_c, 1)

                def clip(s, u):
                    dve.wait_ge(s_c, s + 1)
                    dve.tensor_scalar(score[:, u % M, :], score[:, u % M, :], 10.0, -10.0, ALU.min, ALU.max
                                      ).then_inc(s_clip, 1)

                def message(s, u):
                    dve.wait_ge(s_exp, s + 1)
                    dve.tensor_tensor(msg[:, u % M, 0:C].rearrange(heads, h=H1), kv[:, u % E, C:2 * C].rearrange(heads, h=H1),
                                      msg[:, u % M, C:ACCW].unsqueeze(2).broadcast_to((P, H1, D1)), ALU.mult
                                      ).then_inc(s_msg, 1)

                def accumulate(s, u):
                    dve.wait_ge(s_sum, s + 1)
                    if not early(s, 1):
                        dve.wait_ge(s_acc, s)
                    row = acc[:, bass.ds(offsets[(u + ADD_LAG) % G], ACCW)]
                    dve.tensor_tensor(row, row, bank[4 + u % 2][:, 0:ACCW], ALU.add).then_inc(s_acc, 1)
                pipeline(dve, STEPS_RUN, G, [(3, product), (4, message), (3, scores), (0, make_onehot), (3, clip),
                                             (ADD_LAG, accumulate)], load_offsets)
                dve.wait_ge(s_acc, STEPS_RUN)

            @block.tensor
            def _(pe):
                offsets = [None] * G

                def load_offsets(i, v):
                    if v % LOADS == 0:
                        offsets[v:v + LOADS] = nc.values_load_multi_w_load_instructions(
                            q_off[0:1, bass.ds(i, LOADS)], engines=(mybir.EngineType.PE,), min_val=0, max_val=(TILES - 1) * C)[1]

                def turn_onehot(s, u):
                    pe.wait_ge(s_oh, s + 1)
                    if not early(s, 2):
                        pe.wait_ge(s_ohc, s - 1)
                    pe.transpose(bank[u % 2][:, 0:P], onehot[:, u % E, :], ident[:]).then_inc(s_oht, 1)

                def spread_queries(s, u):
                    pe.wait_ge(s_ohc, s + 1)
                    if not early(s, 2):
                        pe.wait_ge(s_prod, s - 1)
                    pe.matmul(bank[2 + u % 2][:, 0:C], onehot_t[:, u % M, :],
                              q_tab[:, bass.ds(offsets[(u + SPREAD_LAG) % G], C)], start=True, stop=True
                              ).then_inc(s_qe, 1)

                def sum_messages(s, u):
                    pe.wait_ge(s_msg, s + 1)
                    if not early(s, 2):
                        pe.wait_ge(s_acc, s - 1)
                    pe.matmul(bank[4 + u % 2][:, 0:ACCW], onehot[:, u % E, :], msg[:, u % M, :], start=True, stop=True
                              ).then_inc(s_sum, 1)
                pipeline(pe, STEPS_RUN, G, [(5, sum_messages), (SPREAD_LAG, spread_queries), (1, turn_onehot)],
                         load_offsets)
        pool_norm1, measure1, apply1 = normalize_stages(0)
        pool_norm2, measure2, apply2 = normalize_stages(1)
        pool_norm3, measure3, apply3 = normalize_stages(2)
        s_wv, s_wvt, s_wvtc, s_y = sem("f_attended_ready"), sem("f_attended_transposed"), sem("f_attended_t_copied"), sem("f_y_ready")
        s_feat, s_hn, s_hnt, s_hntc = sem("f_features_ready"), sem("f_hn_ready"), sem("f_hn_transposed"), sem("f_hnt_copied")
        s_hid, s_gelu, s_down = sem("f_hidden_ready"), sem("f_gelu_ready"), sem("f_down_ready")
        s_xn, s_xnt, s_xntc = sem("g_xn_ready"), sem("g_xn_transposed"), sem("g_xnt_copied")
        s_route, s_pick, s_pickt, s_picktc = sem("g_router_ready"), sem("g_pick_ready"), sem("g_pick_transposed"), sem("g_pick_t_copied")
        s_eh, s_relu, s_eo = sem("g_expert_hidden_ready"), sem("g_relu_ready"), sem("g_expert_out_ready")
        s_done, s_pre = sem("g_rows_done"), sem("g_constants_ready")
        s_c0, s_c1, s_c3, s_c4, s_c6 = sem("f_attended_chain"), sem("f_y_chain"), sem("f_down_chain"), sem("g_route_chain"), sem("g_out_chain")
        s_n0, s_n1, s_n3 = sem("f_feature_norm_chain"), sem("f_hn_chain"), sem("g_xn_chain")
        s_store = [sem(f"g_rows_stored{u}") for u in range(2)]
        with ExitStack() as scope:
            def sc(name, shape, dt=F32):
                return scope.enter_context(nc.sbuf_tensor(name, shape, dt))
            inv_den = sc("f_inv_den", [P, H1])
            wv, wvt, feat = (sc("f_" + n, [P, 2, C]) for n in ("wv", "wvt", "feat"))
            y = sc("f_y", [P, C])
            hn, hnt = sc("f_hn", [P, 2, C]), sc("f_hnt", [P, 2, C])
            units = q_tab[:].rearrange("p (m n) -> p m n", n=P)
            hidden = units[:, 0:2 * MC, :].rearrange("p (u m) n -> p u m n", u=2)
            e_hidden = units[:, 2 * MC:2 * (MC + EC), :].rearrange("p (u m) n -> p u m n", u=2)
            xn, xnt = sc("g_xn", [P, 2, C]), sc("g_xnt", [P, 2, C])
            logit, is_max, rank, best = (sc("g_" + n, [P, k]) for n, k in (("logit", EXPERTS), ("is_max", EXPERTS),
                                                                          ("rank", EXPERTS), ("best", 1)))
            pick = sc("g_pick", [P, 2, EXPERTS])
            pick_t, pick_tb = sc("g_pick_t", [EXPERTS, 2, P]), sc("g_pick_tb", [EXPERTS, 2, P], BF16)
            res = sc("g_res", [P, 2, C])
            block = scope.enter_context(nc.Block())
            QC = 4
            EQ = EC // QC

            @block.sync
            def _(sp):
                def store(t, u):
                    sp.wait_ge(s_done, t + 1)
                    sp.dma_start(out_rows[:, bass.ds(t, 1), :], res[:, u:u + 1, :]).then_inc(s_store[u], 16)
                pipeline(sp, TILES, 2, [(0, store)])
                for u in range(2):
                    sp.wait_ge(s_store[u], 16 * len(range(u, TILES, 2)))

            @block.gpsimd
            def _(pool):
                pipeline(pool, TILES, 2, [(5, pool_norm3(pool)), (2, pool_norm2(pool)), (0, pool_norm1(pool))])

            @block.vector
            def _(dve):
                heads = "p (h d) -> p h d"

                def row_of(t):
                    return x[:, bass.ds(t, 1), :].rearrange("p a c -> p (a c)")

                def attended(t, u):
                    if not early(t, 2):
                        dve.wait_ge(s_wvt, t - 1)
                    link = Chain(dve, s_c0, 2 * t, 2)
                    link(dve.tensor_scalar(inv_den[:], acc[:, bass.ds(t * ACCW + C, H1)], 1e-30, None, ALU.max))
                    link(dve.reciprocal(inv_den[:], inv_den[:]))
                    dve.tensor_tensor(wv[:, u, :].rearrange(heads, h=H1),
                                      acc[:, bass.ds(t * ACCW, C)].rearrange(heads, h=H1),
                                      inv_den[:].unsqueeze(2).broadcast_to((P, H1, D1)), ALU.mult).then_inc(s_wv, 1)
                    measure1(dve, Chain(dve, s_n0, t, 1), row_of(t), t, u)
                    apply1(dve, row_of(t), feat[:, u, :], t, u, s_feat)

                def y_and_norm(t, u):
                    dve.wait_ge(s_y, t + 1)
                    dve.wait_ge(s_feat, t + 1)
                    link = Chain(dve, s_c1, 3 * t, 3)
                    link(dve.tensor_tensor(y[:], bank[2][:, 0:C], feat[:, u, :], ALU.add))
                    link(dve.tensor_tensor(y[:], y[:], bias["bp"][:], ALU.add))
                    link(dve.tensor_tensor(row_of(t), row_of(t), y[:], ALU.add))
                    measure2(dve, Chain(dve, s_n1, t, 1), y[:], t, u)
                    if not early(t, 2):
                        dve.wait_ge(s_hnt, t - 1)
                    apply2(dve, y[:], hn[:, u, :], t, u, s_hn)

                def down_and_norm(t, u):
                    dve.wait_ge(s_down, t + 1)
                    link = Chain(dve, s_c3, 2 * t, 2)
                    link(dve.tensor_tensor(row_of(t), row_of(t), bank[3][:, 0:C], ALU.add))
                    link(dve.tensor_tensor(row_of(t), row_of(t), bias["b2m"][:], ALU.add))
                    measure3(dve, Chain(dve, s_n3, t, 1), row_of(t), t, u)
                    if not early(t, 2):
                        dve.wait_ge(s_xnt, t - 1)
                    apply3(dve, row_of(t), xn[:, u, :], t, u, s_xn)

                def route(t, u):
                    dve.wait_ge(s_route, t + 1)
                    if not early(t, 2):
                        dve.wait_ge(s_pickt, t - 1)
                    link = Chain(dve, s_c4, 5 * t, 5)
                    link(dve.tensor_tensor(logit[:], bank[1][:, C:C + EXPERTS], bias["router_b"][:], ALU.add))
                    link(dve.tensor_reduce(best[:], logit[:], AX, ALU.max))
                    link(dve.tensor_scalar(is_max[:], logit[:], best[:], None, ALU.is_equal))
                    link(dve.tensor_tensor(rank[:], is_max[:], countdown[:], ALU.mult))
                    link(dve.tensor_reduce(best[:], rank[:], AX, ALU.max))
                    dve.tensor_scalar(pick[:, u, :], countdown[:], best[:], None, ALU.is_equal).then_inc(s_pick, 1)

                def finish(t, u):
                    dve.wait_ge(s_eo, t + 1)
                    if not early(t, 2):
                        dve.wait_ge(s_store[u], landed(t, u, 2) - 16)
                    dve.scalar_tensor_tensor(out=res[:, u, :], in0=bank[3][:, 0:C], scalar=0.0, in1=row_of(t),
                                             op0=ALU.max, op1=ALU.add).then_inc(s_done, 1)
                dve.tensor_scalar(countdown[:], iota_row[:, 0:EXPERTS], -1.0, float(EXPERTS), ALU.mult, ALU.add
                                  ).then_inc(s_pre, 1)
                dve.wait_ge(s_pre, 1)
                pipeline(dve, TILES, 2, [(9, finish), (7, route), (5, down_and_norm), (2, y_and_norm), (0, attended)])
                dve.wait_ge(s_done, TILES)

            @block.scalar
            def _(act):
                def relu(t, u):
                    for q in range(EQ):
                        act.wait_ge(s_eh, t * EQ + q + 1)
                        if q == 0 and not early(t, 2):
                            act.wait_ge(s_eo, t - 1)
                        for i in range(QC):
                            m = q * QC + i
                            ins = act.activation(e_hidden[:, u, m, :], bank[6 + q % 2][:, i * P:(i + 1) * P], ACT.Relu,
                                                 bias=w["moe_b1"][:, m:m + 1])
                        ins.then_inc(s_relu, 1)

                def copy_pick_t(t, u):
                    act.wait_ge(s_pickt, t + 1)
                    if not early(t, 2):
                        act.wait_ge(s_eo, t - 1)
                    act.copy(pick_t[:, u, :], bank[1][0:EXPERTS, C + P:C + 2 * P]).then_inc(s_picktc, 1)
                    act.copy(pick_tb[:, u, :], bank[1][0:EXPERTS, C + P:C + 2 * P]).then_inc(s_picktc, 1)

                def copy_xnt(t, u):
                    act.wait_ge(s_xnt, t + 1)
                    if not early(t, 2):
                        act.wait_ge(s_eh, (t - 1) * EQ)
                    act.copy(xnt[:, u, :], bank[0][:, 0:C]).then_inc(s_xntc, 1)

                def gelu(t, u):
                    act.wait_ge(s_hid, t + 1)
                    if not early(t, 2):
                        act.wait_ge(s_down, t - 1)
                    for m in range(MC):
                        ins = act.activation(hidden[:, u, m, :], bank[4 + m // 4][:, (m % 4) * P:(m % 4 + 1) * P], ACT.Gelu,
                                             bias=b1_mlp[:, m:m + 1])
                    ins.then_inc(s_gelu, 1)

                def copy_hnt(t, u):
                    act.wait_ge(s_hnt, t + 1)
                    if not early(t, 2):
                        act.wait_ge(s_hid, t - 1)
                    act.copy(hnt[:, u, :], bank[0][:, 0:C]).then_inc(s_hntc, 1)

                def copy_wvt(t, u):
                    act.wait_ge(s_wvt, t + 1)
                    if not early(t, 2):
                        act.wait_ge(s_y, t - 1)
                    act.copy(wvt[:, u, :], bank[2][:, 0:C]).then_inc(s_wvtc, 1)
                pipeline(act, TILES, 2, [(8, copy_pick_t), (8, relu), (1, copy_wvt), (6, copy_xnt), (4, gelu), (3, copy_hnt)])

            @block.tensor
            def _(pe):
                def turn(t, rows, target, done):
                    for k in range(KC):
                        mm = pe.transpose(target[:, k * P:(k + 1) * P], rows[:, k * P:(k + 1) * P], ident[:])
                    mm.then_inc(done, 1)

                def experts_out(t, u):
                    pe.wait_ge(s_xn, TILES if late(t, TILES, 4) else t + 4)
                    if late(t, TILES, 3):
                        pe.wait_ge(s_done, t)
                    for m in range(EC):
                        if m % QC == 0:
                            pe.wait_ge(s_relu, t * EQ + m // QC + 1)
                        pe.matmul(bank[3][:, 0:C], e_hidden[:, u, m, :], w["moe_w2"][:, m, :], start=(m == 0), stop=False)
                    pe.matmul(bank[3][:, 0:C], pick_t[:, u, :], w["moe_b2"][:], start=False, stop=True).then_inc(s_eo, 1)

                def experts_hidden(t, u):
                    pe.wait_ge(s_picktc, 2 * t + 2)
                    for m in range(EC):
                        q = m // QC
                        if m % QC == 0 and not early(t * EQ + q, 2):
                            pe.wait_ge(s_relu, t * EQ + q - 1)
                        cols, target = slice(m * P, (m + 1) * P), bank[6 + q % 2][:, (m % QC) * P:(m % QC + 1) * P]
                        for k in range(KC):
                            pe.matmul(target, w["moe_w1"][:, k, cols], xnt[:, u, k * P:(k + 1) * P], start=(k == 0), stop=False)
                        mm = pe.matmul(target, moe_mask[:, cols], pick_tb[:, u, :], start=False, stop=True)
                        if m % QC == QC - 1:
                            mm.then_inc(s_eh, 1)

                def router(t, u):
                    pe.wait_ge(s_xntc, t + 1)
                    if not early(t, 1):
                        pe.wait_ge(s_picktc, 2 * t)
                    for k in range(KC):
                        mm = pe.matmul(bank[1][:, C:C + EXPERTS], xnt[:, u, k * P:(k + 1) * P], w["router_t"][:, k, :],
                                       start=(k == 0), stop=(k == KC - 1))
                    mm.then_inc(s_route, 1)

                def turn_pick(t, u):
                    pe.wait_ge(s_pick, t + 1)
                    pe.transpose(bank[1][0:EXPERTS, C + P:C + 2 * P], pick[:, u, :], ident[:]).then_inc(s_pickt, 1)

                def down(t, u):
                    pe.wait_ge(s_gelu, t + 1)
                    if not early(t, 4):
                        pe.wait_ge(s_done, t - 3)
                    elif not early(t, 1):
                        pe.wait_ge(s_xn, t)
                    for m in range(MC):
                        mm = pe.matmul(bank[3][:, 0:C], hidden[:, u, m, :], w["l1_w2t"][:, m, :],
                                       start=(m == 0), stop=(m == MC - 1))
                    mm.then_inc(s_down, 1)

                def turn_xn(t, u):
                    pe.wait_ge(s_xn, t + 1)
                    pe.wait_ge(s_hntc, TILES if late(t, TILES, 3) else t + 3)
                    if late(t, TILES, 2):
                        pe.wait_ge(s_xntc, t)
                    turn(t, xn[:, u, :], bank[0][:, 0:C], s_xnt)

                def up(t, u):
                    pe.wait_ge(s_hntc, t + 1)
                    if not early(t, 1):
                        pe.wait_ge(s_gelu, t)
                    for m in range(MC):
                        for k in range(KC):
                            mm = pe.matmul(bank[4 + m // 4][:, (m % 4) * P:(m % 4 + 1) * P],
                                           w["l1_w1t"][:, k, m * P:(m + 1) * P], hnt[:, u, k * P:(k + 1) * P],
                                           start=(k == 0), stop=(k == KC - 1))
                    mm.then_inc(s_hid, 1)

                def attention_out(t, u):
                    pe.wait_ge(s_wvtc, TILES if late(t, TILES, 2) else t + 2)
                    if late(t, TILES, 1):
                        pe.wait_ge(s_hn, t)
                    for k in range(KC):
                        mm = pe.matmul(bank[2][:, 0:C], wvt[:, u, k * P:(k + 1) * P], w["l1_pt"][:, k, :],
                                       start=(k == 0), stop=(k == KC - 1))
                    mm.then_inc(s_y, 1)

                def turn_hn(t, u):
                    pe.wait_ge(s_hn, t + 1)
                    if not early(t, 3):
                        pe.wait_ge(s_xntc, t - 2)
                    elif not early(t, 1):
                        pe.wait_ge(s_hntc, t)
                    turn(t, hn[:, u, :], bank[0][:, 0:C], s_hnt)

                def turn_wv(t, u):
                    pe.wait_ge(s_wv, t + 1)
                    if not early(t, 2):
                        pe.wait_ge(s_hn, t - 1)
                    elif t == 1:
                        pe.wait_ge(s_wvtc, 1)
                    turn(t, wv[:, u, :], bank[2][:, 0:C], s_wvt)
                pipeline(pe, TILES, 2, [(6, turn_xn), (8, turn_pick), (9, experts_out), (8, experts_hidden),
                                        (7, router), (1, turn_wv), (5, down), (4, up), (3, turn_hn), (2, attention_out)])


OUT_SHAPE = (ROWS, C)


def kernel(**inputs):
    import ml_dtypes
    import concourse.bacc as bacc
    from concourse.bass_utils import run_bass_kernel_spmd

    g = {k: np.asarray(v) for k, v in inputs.items()}

    def by_channel(m):
        return m.reshape(-1, P, m.shape[1]).transpose(1, 0, 2)

    pad = STEP_TABLE * P - EDGES
    src = np.pad(g["src"].astype(np.int32), (0, pad)).reshape(STEP_TABLE, P)
    dst = np.pad(g["dst"].astype(np.int32), (0, pad), constant_values=PAD_DST).reshape(STEP_TABLE, P)
    moe_w1 = g["L1_ffn_W1"].transpose(1, 0, 2).reshape(C, EXPERTS * HID)
    mask = np.where(np.arange(EXPERTS * HID)[None] // HID == np.arange(EXPERTS)[:, None], 0.0, -1e30)
    arrays = {
        "x": np.pad(g["x"], ((0, ROWS - NODES), (0, 0))),
        "edge_rows": np.concatenate([src, dst], axis=1),
        "l0_w1t": by_channel(g["L0_gnn_W1"].T), "l0_w2t": by_channel(g["L0_gnn_W2"].T),
        "l0_fx": by_channel(g["L0_ffn_W_fx"]),
        "w_xt": g["L0_ffn_W_x"].T.reshape(H0, D0, C).transpose(1, 0, 2),
        "b_x": g["L0_ffn_b_x"].reshape(H0, D0).T,
        "w_slice": g["L0_ffn_W_slice"], "w_q": g["L0_ffn_W_q"], "w_k": g["L0_ffn_W_k"], "w_v": g["L0_ffn_W_v"],
        "b_fx_row": g["L0_ffn_b_fx"][None],
        "l0_slice_out": g["L0_ffn_W_out"].reshape(H0, D0, C).transpose(1, 0, 2),
        "l1_qt": by_channel(g["L1_gnn_Wq"].T),
        "l1_kvt": by_channel(np.concatenate([g["L1_gnn_Wk"].T, g["L1_gnn_Wv"].T], axis=1)),
        "l1_pt": by_channel(g["L1_gnn_Wp"].T),
        "l1_w1t": by_channel(g["L1_gnn_W1"].T), "l1_w2t": by_channel(g["L1_gnn_W2"].T),
        "l1_b1": g["L1_gnn_b1"].reshape(MC, P).T,
        "ln_g": g["L1_gnn_ln_g"].reshape(KC, P).T, "ln_b": g["L1_gnn_ln_b"].reshape(KC, P).T,
        "router_t": by_channel(g["L1_ffn_router_w"].T),
        "moe_w1": by_channel(moe_w1), "moe_b1": g["L1_ffn_b1"].reshape(EC, P).T,
        "moe_w2": by_channel(g["L1_ffn_W2"].reshape(EXPERTS * HID, C)), "moe_b2": g["L1_ffn_b2"],
        "moe_mask": mask.astype(ml_dtypes.bfloat16),
        "b1": g["L0_gnn_b1"][None], "b2": g["L0_gnn_b2"][None], "b_slice": g["L0_ffn_b_slice"][None],
        "b_out": g["L0_ffn_b_out"][None], "bq": g["L1_gnn_bq"][None],
        "bkv": np.concatenate([g["L1_gnn_bk"], g["L1_gnn_bv"]])[None],
        "bp": g["L1_gnn_bp"][None], "b2m": g["L1_gnn_b2"][None], "router_b": g["L1_ffn_router_b"][None],
        "temperature": g["L0_ffn_temperature"].reshape(1, H0),
    }
    arrays = {k: np.ascontiguousarray(v) for k, v in arrays.items()}
    nc = bacc.Bacc("TRN2", target_bir_lowering=False, num_devices=1)
    aps = {k: nc.dram_tensor("in_" + k, v.shape, mybir.dt.from_np(v.dtype), kind="ExternalInput").ap()
           for k, v in arrays.items()}
    out = nc.dram_tensor("out_rows", OUT_SHAPE, F32, kind="ExternalOutput").ap()
    build(nc, aps, out)
    r = run_bass_kernel_spmd(nc, [{"in_" + k: v for k, v in arrays.items()}], core_ids=[0])
    return r.results[0]["out_rows"][:NODES]
```

```python
from contextlib import ExitStack

import numpy as np

import concourse.bass as bass
from concourse import mybir

F32 = mybir.dt.float32
BF16 = mybir.dt.bfloat16
I32 = mybir.dt.int32
U32 = mybir.dt.uint32
ALU = mybir.AluOpType
ACT = mybir.ActivationFunctionType
AX = mybir.AxisListType.X

P = 128
NODES = 3125
EDGES = 50000
C = 256
KC = C // P
TILES = -(-NODES // P)
ROWS = TILES * P
CHUNKS = -(-EDGES // P)
STEPS = CHUNKS + TILES - 1
STEP_UNROLL = 16
LOADS = 2
SLOTS = 8
STEPS_RUN = -(-STEPS // STEP_UNROLL) * STEP_UNROLL
STEP_GROUPS = -(-(STEPS_RUN + 1) // P)
STEP_TABLE = STEP_GROUPS * P
ADD_LAG = 8
SPREAD_LAG = 2
PAD_DST = ROWS
U = 4
SUMW = C + 1
H0, D0, G0 = 8, 64, 64
INNER = H0 * D0
H1, D1 = 8, 32
ACCW = C + H1
MLP = 4 * C
MC = MLP // P
EXPERTS, HID = 32, C // 4
EC = EXPERTS * HID // P
EPS = 1e-5


def early(t, n):
    return isinstance(t, int) and t < n


def late(t, count, n):
    return isinstance(t, int) and t >= count - n


def pipeline(eng, count, unroll, stages, begin=None):
    depth = max(lag for lag, _ in stages)

    def turn(i, v):
        if begin is not None:
            begin(i, v)
        for lag, body in stages:
            if isinstance(i, int) and not 0 <= i - lag < count:
                continue
            body(i - lag, (v - lag) % unroll)

    head = -(-(depth + unroll) // unroll)
    last = count // unroll
    for i in range(head * unroll):
        turn(i, i % unroll)
    with eng.Fori(head, last) as g:
        for v in range(unroll):
            turn(g * unroll + v, v)
    for i in range(last * unroll, count + depth):
        turn(i, i % unroll)


def landed(t, slot, unroll):
    return (t - slot) * (16 // unroll) + 16


class Chain:

    def __init__(self, eng, sem, start, length):
        self.eng, self.sem, self.start, self.length, self.n = eng, sem, start, length, 0

    def __call__(self, ins):
        ins.then_inc(self.sem, 1)
        self.n += 1
        assert self.n <= self.length
        self.eng.wait_ge(self.sem, self.start + self.n)


WEIGHTS = ["l0_w1t", "l0_w2t", "l0_fx", "l0_slice_out", "l1_qt", "l1_kvt", "l1_pt", "l1_w1t", "l1_w2t",
           "router_t", "moe_w1", "moe_b1", "moe_w2", "moe_b2", "w_slice", "w_q", "w_k", "w_v", "b_fx_row",
           "l1_b1", "ln_g", "ln_b"]
LATE = {"l0_w2t", "l0_fx", "l0_slice_out", "l1_qt", "l1_kvt", "l1_pt", "l1_w2t", "router_t", "moe_w1", "moe_b1", "moe_w2",
        "moe_b2", "w_q", "w_k", "w_v", "b_fx_row"}
BIASES = ["b1", "b2", "b_slice", "b_out", "bq", "bkv", "bp", "b2m", "router_b", "temperature"]


def build(nc, a, out):
    with ExitStack() as ctx:
        held = []

        def sem(name):
            held.append(nc.alloc_semaphore(name=name))
            return held[-1]

        def sb(name, shape, dt=F32):
            return ctx.enter_context(nc.sbuf_tensor(name, shape, dt))

        def dram(name, shape):
            return nc.dram_tensor(name, shape, F32, kind="Internal").ap()

        step_src_dram = dram("step_sources", (STEP_TABLE, P))
        kv_dram = dram("kv_rows", (ROWS, 2 * C))
        sums_dram = [dram(f"first_end_sums{u}", (ROWS + P, SUMW)) for u in range(U)]
        wt_dram = dram("slice_weights_t", (TILES, P, INNER))
        kv_rows = kv_dram.rearrange("(t p) c -> p t c", p=P)
        wt_rows = wt_dram.rearrange("t p n -> p t n")
        out_rows = out.rearrange("(t p) c -> p t c", p=P)

        s_fence = ctx.enter_context(nc.semaphore("fence"))

        def carry_waits(eng):
            eng.sem_inc(s_fence, 1)

        def fence(eng, signal, value):
            eng.wait_ge(signal, value)
            carry_waits(eng)

        bank = [ctx.enter_context(nc.psum_tensor(f"bank{i}", [P, 512], F32)) for i in range(8)]

        x = sb("x", [P, TILES, C])
        acc = sb("acc", [P, TILES * ACCW])
        q_tab = sb("q_tab", [P, TILES * C])
        ident = sb("ident", [P, P])
        iota_row = sb("iota_row", [P, P])
        ones = sb("ones", [P, P])
        neg_half = sb("neg_half", [P, 1])
        valid = sb("valid", [P, TILES])
        src_step = sb("src_step", [P, STEP_TABLE])
        dst_step = sb("dst_step", [P, STEP_TABLE])
        tile_words = sb("tile_words", [1, (STEP_TABLE + STEP_UNROLL) // 4], I32)
        acc_off = sb("acc_off", [1, STEP_TABLE + STEP_UNROLL], I32)
        q_off = sb("q_off", [1, STEP_TABLE + STEP_UNROLL], I32)
        w = {name: sb("w_" + name, list(a[name].shape)) for name in WEIGHTS}
        bias = {name: sb("b_" + name, [P, a[name].shape[1]]) for name in BIASES}
        slice_out = sb("slice_out", [P, INNER // P, C])
        b1_mlp = sb("b1_mlp", [P, MC])
        w_logits = sb("w_logits", [P, KC, INNER])
        b_logits = sb("b_logits", [P, INNER])
        moe_mask = sb("moe_mask", [EXPERTS, EXPERTS * HID], BF16)
        countdown = sb("countdown", [P, EXPERTS])
        stats = sb("stats", [P, 3, 2, 6])
        mean_var = sb("mean_var", [P, 3, 2, 2])
        rstd = sb("rstd", [P, 3, 2])

        norm_sems = [(sem(f"stats_ready{i}"), sem(f"rstd_ready{i}"), sem(f"var_eps{i}")) for i in range(3)]
        norms_before = [0, 0, 0]

        def normalize_stages(i):
            stats_ready, rstd_ready, pool_chain = norm_sems[i]
            base = norms_before[i]
            norms_before[i] += TILES

            def pool_stage(pool):
                def body(t, u):
                    rs = rstd[:, i, u % 2:u % 2 + 1]
                    fence(pool, stats_ready, base + t + 1)
                    pool.tensor_scalar(rs, mean_var[:, i, u % 2, 1:2], EPS, None, ALU.add).then_inc(pool_chain, 1)
                    pool.wait_ge(pool_chain, base + t + 1)
                    pool.tensor_tensor(rs, rs, neg_half[:], ALU.pow).then_inc(rstd_ready, 1)
                return body

            def measure(dve, link, row, t, u):
                carry_waits(dve)
                link(dve.bn_stats(stats[:, i, u % 2, :], row))
                carry_waits(dve)
                dve.bn_aggr(mean_var[:, i, u % 2, :], stats[:, i, u % 2, :]).then_inc(stats_ready, 1)

            def apply(dve, row, out, t, u, out_ready):
                dve.wait_ge(stats_ready, base + t + 1)
                dve.wait_ge(rstd_ready, base + t + 1)
                dve.tensor_scalar(out, row, mean_var[:, i, u % 2, 0:1], rstd[:, i, u % 2:u % 2 + 1], ALU.subtract, ALU.mult
                                  ).then_inc(out_ready, 1)
            return pool_stage, measure, apply

        s_x, s_w, s_rows = sem("x_in"), sem("weights_in"), sem("dst_rows_in")
        s_gathered = sem("step_rows_gathered")
        s_const, s_acc0 = sem("constants_ready"), sem("acc_zeroed")
        s_dchain, s_pchain = sem("table_chain_dve"), sem("table_chain_pool")
        s_below, s_bound = sem("chunk_ends_compared"), sem("tile_ends_counted")
        s_chunk, s_rel = sem("step_chunk_ready"), sem("step_rows_float")
        s_tr, s_tab = sem("step_rows_transposed"), sem("step_tables_ready")
        n_loads = len(WEIGHTS) - len(LATE) - 3 + len(BIASES)
        JR = STEP_GROUPS

        with ExitStack() as scope:
            def sc(name, shape, dt=F32):
                return scope.enter_context(nc.sbuf_tensor(name, shape, dt))
            dst_i = sc("dst_i", [P, JR, P], I32)
            last_dst = sc("last_dst", [P, JR])
            iota_i = sc("iota_i", [P, P], I32)
            tile_no_i = sc("tile_no_i", [P, TILES - 1], I32)
            step_no_i = sc("step_no_i", [P, JR], I32)
            tile_end, tile_no = sc("tile_end", [P, TILES - 1]), sc("tile_no", [P, TILES - 1])
            step_no = sc("step_no", [P, JR])
            below = sc("below", [P, JR, TILES - 1])
            bound = sc("bound", [P, TILES - 1])
            passed = sc("passed", [P, TILES - 1])
            step_tile, tile_row0 = sc("step_tile", [P, JR]), sc("tile_row0", [P, JR])
            words = sc("words", [1, STEP_TABLE // 4])
            step_chunk = sc("step_chunk", [P, JR], U32)
            w_xt = w["moe_w1"][0:D0, 0, 0:H0 * C].rearrange("p (h c) -> p h c", h=H0)
            bx_cols = w["moe_w1"][0:D0, 1, 0:H0 * P].rearrange("p (h n) -> p h n", h=H0)
            b_x = sc("b_x", [D0, H0])
            s_wx = sem("w_x_in")
            s_fold_mm, s_bcol = sem("fold_products"), sem("bias_columns")
            edges_i = sc("edges_i", [P, JR, 2 * P], I32)
            edges_f = sc("edges_f", [P, JR, 2 * P])
            block = scope.enter_context(nc.Block())

            FOLDED = ["w_slice", "ln_b", "l1_w1t"]

            @block.scalar
            def _(act):
                act.dma_start(w_xt, a["w_xt"]).then_inc(s_wx, 16)
                act.dma_start(b_x[:], a["b_x"]).then_inc(s_wx, 16)
                for name in FOLDED:
                    act.dma_start(w[name][:], a[name]).then_inc(s_wx, 16)
                act.wait_ge(s_wx, 16 * (2 + len(FOLDED)))

            @block.sync
            def _(sp):
                sp.dma_start(dst_i[:], a["edge_rows"].rearrange("(j p) e -> p j e", p=P)[:, :, P:2 * P]).then_inc(s_rows, 16)
                sp.dma_start(x[:], a["x"].rearrange("(t p) c -> p t c", p=P)).then_inc(s_x, 16)
                for name in [n for n in WEIGHTS if n not in LATE and n not in FOLDED]:
                    sp.dma_start(w[name][:], a[name]).then_inc(s_w, 16)
                for name in BIASES:
                    sp.dma_start(bias[name][:], a[name].broadcast_to((P, a[name].shape[1]))).then_inc(s_w, 16)
                sp.wait_ge(s_rel, 2 * JR)
                sp.dma_start(step_src_dram.rearrange("(j p) e -> p j e", p=P), edges_f[:, :, 0:P]).then_inc(s_rows, 16)
                sp.wait_ge(s_rows, 32)
                sp.wait_ge(s_x, 16)
                sp.wait_ge(s_w, 16 * n_loads)

            @block.gpsimd
            def _(pool):
                link = Chain(pool, s_pchain, 0, 2)
                pool.iota(iota_i[:], pattern=[[1, P]], base=0, channel_multiplier=0).then_inc(s_const, 1)
                pool.iota(tile_no_i[:], pattern=[[1, TILES - 1]], base=0, channel_multiplier=0).then_inc(s_const, 1)
                pool.iota(step_no_i[:], pattern=[[P, JR]], base=0, channel_multiplier=1).then_inc(s_const, 1)
                pool.memset(ones[:], 1.0).then_inc(s_const, 1)
                pool.memset(neg_half[:], -0.5).then_inc(s_const, 1)
                link(pool.memset(ident[:], 0.0))
                pool.affine_select(out=ident[:], in_=ident[:], compare_op=ALU.not_equal, fill=1.0, base=0,
                                   pattern=[[-1, P]], channel_multiplier=1).then_inc(s_const, 1)
                link(pool.memset(valid[:], 1.0))
                pool.affine_select(out=valid[:], in_=valid[:], compare_op=ALU.is_ge, fill=0.0, base=NODES - 1,
                                   pattern=[[-P, TILES]], channel_multiplier=-1).then_inc(s_const, 1)
                for j in range(JR):
                    pool.wait_ge(s_chunk, j + 1)
                    pool.indirect_dma_start(out=edges_i[:, j, :], out_offset=None, in_=a["edge_rows"],
                                            in_offset=bass.IndirectOffsetOnAxis(ap=step_chunk[:, j:j + 1], axis=0)
                                            ).then_inc(s_gathered, 16)
                pool.wait_ge(s_gathered, 16 * JR)

            @block.vector
            def _(dve):
                assert TILES <= 32
                link = Chain(dve, s_dchain, 0, 12 + 3 * JR)
                link(dve.memset(tile_words[:], 0))
                link(dve.memset(acc_off[:], 0))
                link(dve.memset(q_off[:], 0))
                dve.memset(q_tab[:], 0.0).then_inc(s_acc0, 1)
                dve.memset(acc[:].rearrange("p (t w) -> p t w", w=ACCW)[:, :, C:ACCW], 1.0).then_inc(s_acc0, 1)
                dve.wait_ge(s_const, 7)
                dve.tensor_copy(iota_row[:], iota_i[:]).then_inc(s_acc0, 1)
                dve.wait_ge(s_wx, 16 * (2 + len(FOLDED)))
                for h in range(H0):
                    dve.tensor_scalar(bx_cols[:, h, :], ones[0:D0, :], b_x[:, h:h + 1], None, ALU.mult).then_inc(s_bcol, 1)
                link(dve.tensor_scalar(tile_end[:], tile_no_i[:], float(P), float(P), ALU.mult, ALU.add))
                link(dve.tensor_copy(tile_no[:], tile_no_i[:]))
                link(dve.tensor_copy(step_no[:], step_no_i[:]))
                dve.wait_ge(s_rows, 16)
                link(dve.tensor_copy(last_dst[:], dst_i[:, :, P - 1]))
                for j in range(JR):
                    dve.tensor_scalar(below[:, j, :], tile_end[:], last_dst[:, j:j + 1], None, ALU.is_gt
                                      ).then_inc(s_below, 1)
                dve.wait_ge(s_bound, 1)
                link(dve.tensor_tensor(bound[:], bank[0][:, 0:TILES - 1], tile_no[:], ALU.add))
                for j in range(JR):
                    link(dve.tensor_scalar(passed[:], bound[:], step_no[:, j:j + 1], None, ALU.is_lt))
                    link(dve.tensor_reduce(step_tile[:, j:j + 1], passed[:], AX, ALU.add))
                    dve.tensor_tensor(step_chunk[:, j:j + 1], step_no[:, j:j + 1], step_tile[:, j:j + 1],
                                      ALU.subtract).then_inc(s_chunk, 1)
                link(dve.tensor_scalar(tile_row0[:], step_tile[:], float(P), None, ALU.mult))
                dve.wait_ge(s_gathered, 16 * JR)
                for j in range(JR):
                    dve.tensor_copy(edges_f[:, j, 0:P], edges_i[:, j, 0:P]).then_inc(s_rel, 1)
                    dve.tensor_scalar(edges_f[:, j, P:2 * P], edges_i[:, j, P:2 * P], tile_row0[:, j:j + 1], None,
                                      ALU.subtract).then_inc(s_rel, 1)
                dve.wait_ge(s_tr, 3 * JR)
                dve.tensor_copy(src_step[:], bank[1][:]).then_inc(s_tab, 1)
                dve.tensor_copy(dst_step[:], bank[2][:]).then_inc(s_tab, 1)
                dve.tensor_scalar(acc_off[:, ADD_LAG:ADD_LAG + STEP_TABLE], bank[3][0:1, :], float(ACCW), None, ALU.mult).then_inc(s_tab, 1)
                dve.tensor_scalar(q_off[:, SPREAD_LAG:SPREAD_LAG + STEP_TABLE], bank[3][0:1, :], float(C), None, ALU.mult).then_inc(s_tab, 1)
                digits = bank[3][0:1, :].rearrange("p (g k) -> p g k", k=4)
                link(dve.tensor_copy(words[:].unsqueeze(2), digits[:, :, 3:4]))
                for k in (2, 1):
                    link(dve.scalar_tensor_tensor(out=words[:].unsqueeze(2), in0=words[:].unsqueeze(2), scalar=32.0,
                                                  in1=digits[:, :, k:k + 1], op0=ALU.mult, op1=ALU.add))
                dve.scalar_tensor_tensor(out=tile_words[:, ADD_LAG // 4:ADD_LAG // 4 + STEP_TABLE // 4].unsqueeze(2),
                                         in0=words[:].unsqueeze(2), scalar=32.0, in1=digits[:, :, 0:1],
                                         op0=ALU.mult, op1=ALU.add).then_inc(s_tab, 1)
                dve.wait_ge(s_tab, 5)
                dve.wait_ge(s_fold_mm, 1)

            @block.tensor
            def _(pe):
                pe.wait_ge(s_const, 7)
                pe.wait_ge(s_below, JR)
                for j in range(JR):
                    mm = pe.matmul(bank[0][:, 0:TILES - 1], ones[:], below[:, j, :], start=(j == 0), stop=(j == JR - 1))
                mm.then_inc(s_bound, 1)
                pe.wait_ge(s_wx, 16 * (2 + len(FOLDED)))
                pe.wait_ge(s_bcol, H0)
                for h in range(H0):
                    cols = slice(h * G0, (h + 1) * G0)
                    for k in range(KC):
                        pe.matmul(bank[4 + k][:, cols], w_xt[:, h, k * P:(k + 1) * P], w["w_slice"][:], start=True, stop=True)
                    pe.matmul(bank[6][:, cols], bx_cols[:, h, :], w["w_slice"][:], start=True, stop=True)
                for m in range(MC):
                    for k in range(KC):
                        mm = pe.matmul(bank[7][:, m:m + 1], w["l1_w1t"][:, k, m * P:(m + 1) * P], w["ln_b"][:, k:k + 1],
                                       start=(k == 0), stop=(k == KC - 1))
                mm.then_inc(s_fold_mm, 1)
                for j in range(JR):
                    cols = slice(j * P, (j + 1) * P)
                    pe.wait_ge(s_rel, 2 * j + 2)
                    pe.transpose(bank[1][:, cols], edges_f[:, j, 0:P], ident[:]).then_inc(s_tr, 1)
                    pe.transpose(bank[2][:, cols], edges_f[:, j, P:2 * P], ident[:]).then_inc(s_tr, 1)
                    pe.transpose(bank[3][0:1, cols], step_tile[:, j:j + 1], ident[:]).then_inc(s_tr, 1)

        pool_norm, measure, apply = normalize_stages(0)
        s_fold = sem("folded")
        s_fchain = sem("fold_chain")
        s_xn, s_xt, s_xtc = sem("a_xn_ready"), sem("a_xn_transposed"), sem("a_xnt_copied")
        s_mm, s_added = sem("a_product_ready"), sem("a_added")
        s_nchain, s_addchain = sem("a_norm_chain"), sem("a_add_chain")
        s_late = sem("late_weights_in")
        s_kept, s_zeroed = sem("a_xn_kept"), sem("a_mean_tables_zeroed")
        with ExitStack() as scope:
            def sc(name, shape, dt=F32):
                return scope.enter_context(nc.sbuf_tensor(name, shape, dt))
            xn = sc("a_xn", [P, 2, C])
            xnt = sc("a_xnt", [P, 2, C])
            inv_temp = sc("inv_temp", [P, H0])
            block = scope.enter_context(nc.Block())
            per_head = "p (h g) -> p h g"

            @block.sync
            def _(sp):
                for table in sums_dram:
                    sp.dma_start(table.rearrange("(t p) w -> p t w", p=P),
                                 q_tab[:, 0:SUMW].unsqueeze(1).broadcast_to((P, TILES + 1, SUMW))).then_inc(s_zeroed, 16)
                for name in sorted(LATE):
                    sp.dma_start(w[name][:], a[name]).then_inc(s_late, 16)
                sp.dma_start(moe_mask[:], a["moe_mask"]).then_inc(s_late, 16)
                sp.wait_ge(s_zeroed, 16 * U)

            @block.gpsimd
            def _(pool):
                pipeline(pool, TILES, 2, [(0, pool_norm(pool))])

            @block.vector
            def _(dve):
                link = Chain(dve, s_fchain, 0, 4)
                link(dve.tensor_scalar(inv_temp[:], bias["temperature"][:], 0.1, 5.0, ALU.max, ALU.min))
                link(dve.reciprocal(inv_temp[:], inv_temp[:]))
                scale = inv_temp[:].unsqueeze(2).broadcast_to((P, H0, G0))
                for k in range(KC):
                    dve.tensor_tensor(w_logits[:, k, :].rearrange(per_head, h=H0), bank[4 + k][:].rearrange(per_head, h=H0),
                                      scale, ALU.mult).then_inc(s_fold, 1)
                link(dve.tensor_tensor(b_logits[:].rearrange(per_head, h=H0), bank[6][:].rearrange(per_head, h=H0),
                                       bias["b_slice"][:].unsqueeze(1).broadcast_to((P, H0, G0)), ALU.add))
                dve.tensor_tensor(b_logits[:].rearrange(per_head, h=H0), b_logits[:].rearrange(per_head, h=H0),
                                  scale, ALU.mult).then_inc(s_fold, 1)
                dve.tensor_tensor(b1_mlp[:], bank[7][:, 0:MC], w["l1_b1"][:], ALU.add).then_inc(s_fold, 1)
                for k in range(KC):
                    dve.tensor_scalar(w["l1_w1t"][:, k, :], w["l1_w1t"][:, k, :], w["ln_g"][:, k:k + 1], None,
                                      ALU.mult).then_inc(s_fold, 1)
                link(dve.tensor_tensor(bias["b1"][:], bias["b1"][:], bias["b2"][:], ALU.add))
                dve.wait_ge(s_fold, 2 * KC + 2)

                def row_of(t):
                    return x[:, bass.ds(t, 1), :].rearrange("p a c -> p (a c)")

                def normalize(t, u):
                    if not early(t, 2):
                        dve.wait_ge(s_xt, t - 1)
                        dve.wait_ge(s_kept, t - 1)
                    apply(dve, row_of(t), xn[:, u, :], t, u, s_xn)

                def add(t, u):
                    dve.wait_ge(s_mm, t + 1)
                    row = x[:, bass.ds(t, 1), :].rearrange("p a c -> p (a c)")
                    link = Chain(dve, s_addchain, t, 1)
                    link(dve.tensor_tensor(row, row, bank[2 + u][:, 0:C], ALU.add))
                    dve.tensor_tensor(row, row, bias["b1"][:], ALU.add).then_inc(s_added, 1)
                pipeline(dve, TILES, 2, [(0, lambda t, u: measure(dve, Chain(dve, s_nchain, t, 1), row_of(t), t, u)),
                                         (1, normalize), (3, add)])
                dve.wait_ge(s_added, TILES)

            @block.scalar
            def _(act):
                def copy(t, u):
                    act.wait_ge(s_xt, t + 1)
                    if not early(t, 2):
                        act.wait_ge(s_mm, t - 1)
                    act.copy(xnt[:, u, :], bank[u][:, 0:C]).then_inc(s_xtc, 1)

                def keep(t, u):
                    act.wait_ge(s_xn, t + 1)
                    act.copy(acc[:, bass.ds(t * ACCW, C)], xn[:, u, :]).then_inc(s_kept, 1)
                pipeline(act, TILES, 2, [(1, keep), (1, copy)])
                act.wait_ge(s_kept, TILES)

            @block.tensor
            def _(pe):
                def turn_rows(t, u):
                    pe.wait_ge(s_xn, t + 1)
                    if not early(t, 2):
                        pe.wait_ge(s_xtc, t - 1)
                    for k in range(KC):
                        mm = pe.transpose(bank[u][:, k * P:(k + 1) * P], xn[:, u, k * P:(k + 1) * P], ident[:])
                    mm.then_inc(s_xt, 1)

                def product(t, u):
                    pe.wait_ge(s_xtc, t + 1)
                    if not early(t, 2):
                        pe.wait_ge(s_added, t - 1)
                    for k in range(KC):
                        mm = pe.matmul(bank[2 + u][:, 0:C], xnt[:, u, k * P:(k + 1) * P], w["l0_w1t"][:, k, :],
                                       start=(k == 0), stop=(k == KC - 1))
                    mm.then_inc(s_mm, 1)
                pipeline(pe, TILES, 2, [(1, turn_rows), (2, product)])

        E = SLOTS
        G = STEP_UNROLL
        s_oh, s_eq, s_dup, s_const = sem("m_onehot_ready"), sem("m_equal_ready"), sem("m_earlier_ready"), sem("m_constants_ready")
        s_max, s_target = sem("m_duplicates_found"), sem("m_target_ready")
        s_spread, s_spreadc = sem("m_spread_ready"), sem("m_spread_copied")
        s_sum, s_total = sem("m_sum_ready"), sem("m_total_copied")
        s_seg = [sem(f"m_first_ends_landed{u}") for u in range(2)]
        s_add = [sem(f"m_rows_added{u}") for u in range(U)]
        with ExitStack() as scope:
            def sc(name, shape, dt=F32):
                return scope.enter_context(nc.sbuf_tensor(name, shape, dt))
            target = sc("m_target", [P, G], U32)
            first_row = sc("m_first_row", [P, G, P])
            onehot, equal = sc("m_onehot", [P, E, P], BF16), sc("m_equal", [P, E, P], BF16)
            before, earlier = sc("m_before", [P, P]), sc("m_earlier", [P, 2, P])
            dup, spare, spare_i = sc("m_dup", [P, E]), sc("m_spare", [P, 1]), sc("m_spare_i", [P, 1], I32)
            to_spare = sc("m_to_spare", [P, STEP_TABLE])
            spread = slice_out[:].rearrange("p m c -> p (m c)")[:, 0:U * P].rearrange("p (u n) -> p u n", u=U)
            total = sc("m_total", [P, U, SUMW])
            block = scope.enter_context(nc.Block())

            @block.sync
            def _(sp):
                def load_first(g, u):
                    if not early(g, 2):
                        sp.wait_ge(s_eq, E * (g - 1))
                        sp.wait_ge(s_dup, E * (g - 1))
                    sp.dma_start(first_row[:, u * E:(u + 1) * E, :],
                                 step_src_dram[bass.ds(g * E, E), :].unsqueeze(0).broadcast_to((P, E, P))
                                 ).then_inc(s_seg[u], 16)
                pipeline(sp, STEPS_RUN // E, 2, [(0, load_first)])
                sp.wait_ge(s_late, 16 * (len(LATE) + 1))

            @block.scalar
            def _(act):
                def copy_spread(s, u):
                    act.wait_ge(s_spread, s + 1)
                    if not early(s, U):
                        act.wait_ge(s_sum, s - (U - 1))
                    act.copy(spread[:, u % U, :], bank[u % 2][:, 0:P]).then_inc(s_spreadc, 1)

                def copy_total(s, u):
                    act.wait_ge(s_sum, s + 1)
                    if not early(s, U):
                        act.wait_ge(s_add[u % U], landed(s, u % U, U) - 16)
                    act.copy(total[:, u % U, :], bank[2 + u % 2][:, 0:SUMW]).then_inc(s_total, 1)
                pipeline(act, STEPS_RUN, G, [(ADD_LAG, copy_total), (6, copy_spread)])

            @block.gpsimd
            def _(pool):
                pool.memset(before[:], 1.0).then_inc(s_const, 1)
                pool.iota(spare_i[:], pattern=[[0, 1]], base=ROWS, channel_multiplier=1).then_inc(s_const, 1)
                pool.wait_ge(s_const, 2)
                pool.affine_select(out=before[:], in_=before[:], compare_op=ALU.is_gt, fill=0.0, base=0,
                                   pattern=[[-1, P]], channel_multiplier=1).then_inc(s_const, 1)

                def add(s, u):
                    if not early(s, U):
                        pool.wait_ge(s_add[u % U], landed(s, u % U, U) - 16)
                    pool.wait_ge(s_target, s + 1)
                    fence(pool, s_total, s + 1)
                    pool.indirect_dma_start(out=sums_dram[u % U], in_=total[:, u % U, :], in_offset=None,
                                            out_offset=bass.IndirectOffsetOnAxis(ap=target[:, u:u + 1], axis=0),
                                            compute_op=ALU.add).then_inc(s_add[u % U], 16)
                pipeline(pool, STEPS_RUN, G, [(ADD_LAG + 1, add)])
                for u in range(U):
                    pool.wait_ge(s_add[u], 16 * (STEPS_RUN // U))

            @block.vector
            def _(dve):
                dve.wait_ge(s_const, 3)
                dve.tensor_copy(spare[:], spare_i[:]).then_inc(s_const, 1)
                dve.wait_ge(s_const, 4)
                dve.tensor_scalar(to_spare[:], src_step[:], -1.0, spare[:], ALU.mult, ALU.add).then_inc(s_const, 1)
                dve.wait_ge(s_const, 5)

                def find_earlier(s, u):
                    if u % E == 0:
                        dve.wait_ge(s_seg[u // E], landed(s, u, G))
                    dve.scalar_tensor_tensor(out=earlier[:, u % 2, :], in0=first_row[:, u, :], scalar=src_step[:, bass.ds(s, 1)],
                                             in1=before[:], op0=ALU.is_equal, op1=ALU.mult).then_inc(s_dup, 1)

                def make_onehot(s, u):
                    if not early(s, E):
                        dve.wait_ge(s_spread, s - (E - 1))
                    dve.tensor_scalar(onehot[:, u % E, :], iota_row[:], dst_step[:, bass.ds(s, 1)], None,
                                      ALU.is_equal).then_inc(s_oh, 1)

                def any_earlier(s, u):
                    dve.wait_ge(s_dup, s + 1)
                    dve.tensor_reduce(dup[:, u % E:u % E + 1], earlier[:, u % 2, :], AX, ALU.max).then_inc(s_max, 1)

                def compare(s, u):
                    dve.tensor_scalar(equal[:, u % E, :], first_row[:, u, :], src_step[:, bass.ds(s, 1)], None,
                                      ALU.is_equal).then_inc(s_eq, 1)

                def choose(s, u):
                    dve.wait_ge(s_max, s + 1)
                    if not early(s, E):
                        dve.wait_ge(s_add[u % U], landed(s, u % U, U) - 16)
                    dve.scalar_tensor_tensor(out=target[:, u:u + 1], in0=dup[:, u % E:u % E + 1],
                                             scalar=to_spare[:, bass.ds(s, 1)], in1=src_step[:, bass.ds(s, 1)],
                                             op0=ALU.mult, op1=ALU.add).then_inc(s_target, 1)
                pipeline(dve, STEPS_RUN, G, [(2, find_earlier), (2, make_onehot), (2, any_earlier), (2, compare),
                                             (5, choose)])

            @block.tensor
            def _(pe):
                offsets = [None] * G

                def load_offsets(i, v):
                    if v % LOADS == 0:
                        offsets[v:v + LOADS] = nc.values_load_multi_w_load_instructions(
                            acc_off[0:1, bass.ds(i, LOADS)], engines=(mybir.EngineType.PE,), min_val=0,
                            max_val=(TILES - 1) * ACCW)[1]

                def count_ends(s, u):
                    pe.wait_ge(s_oh, s + 1)
                    pe.wait_ge(s_eq, s + 1)
                    if not early(s, 2):
                        pe.wait_ge(s_spreadc, s - 1)
                    pe.matmul(bank[u % 2][:, 0:P], onehot[:, u % E, :], equal[:, u % E, :], start=True, stop=True).then_inc(s_spread, 1)

                def sum_rows(s, u):
                    pe.wait_ge(s_spreadc, s + 1)
                    if not early(s, 2):
                        pe.wait_ge(s_total, s - 1)
                    pe.matmul(bank[2 + u % 2][:, 0:SUMW], spread[:, u % U, :],
                              acc[:, bass.ds(offsets[(u + ADD_LAG) % G], SUMW)], start=True, stop=True).then_inc(s_sum, 1)
                pipeline(pe, STEPS_RUN, G, [(ADD_LAG, sum_rows), (6, count_ends)], load_offsets)


        pool_norm, measure, apply = normalize_stages(0)
        s_mean, s_meant, s_meantc = sem("b_mean_ready"), sem("b_mean_transposed"), sem("b_meant_copied")
        s_mm2 = sem("b_product_ready")
        s_xn, s_xt, s_xtc = sem("b_xn_ready"), sem("b_xn_transposed"), sem("b_xnt_copied")
        s_log, s_shift, s_exp, s_wgt = sem("b_logits_ready"), sem("b_shifted"), sem("b_exp_ready"), sem("b_weights_ready")
        s_wsum, s_u, s_wt, s_wtc = sem("b_weights_summed"), sem("b_sliced"), sem("b_weights_transposed"), sem("b_wt_copied")
        s_c0, s_c1, s_c2, s_c3 = sem("b_mean_chain"), sem("b_norm_chain"), sem("b_shift_chain"), sem("b_weigh_chain")
        s_init, s_added, s_tables = sem("b_zeroed"), sem("b_added"), sem("b_tables_added")
        s_store = [sem(f"b_wt_stored{u}") for u in range(2)]
        s_load = [sem(f"b_sums_landed{u}") for u in range(2)]
        wsum = sb("wsum", [P, INNER])
        with ExitStack() as scope:
            def sc(name, shape, dt=F32):
                return scope.enter_context(nc.sbuf_tensor(name, shape, dt))
            mean, meant, xnt = sc("b_mean", [P, 2, C]), sc("b_meant", [P, 2, C]), sc("b_xnt", [P, 2, C])
            cnt, hmax, hsum = sc("b_cnt", [P, 1]), sc("b_hmax", [P, H0]), sc("b_hsum", [P, H0])
            wt = sc("b_wt", [P, 2, INNER])
            n_sums, n_xn = 2 * U * SUMW, 4 * C
            sums = q_tab[:, 0:n_sums].rearrange("p (u k w) -> p u k w", u=2, k=U)
            xn = q_tab[:, n_sums:n_sums + n_xn].rearrange("p (u c) -> p u c", u=4)
            soft_flat = q_tab[:, n_sums + n_xn:n_sums + n_xn + 4 * INNER].rearrange("p (u n) -> p u n", u=4)
            soft = soft_flat.rearrange("p u (h g) -> p u h g", h=H0)
            block = scope.enter_context(nc.Block())

            @block.sync
            def _(sp):
                def load(t, u):
                    if not early(t, 2):
                        sp.wait_ge(s_mean, t - 1)
                    for i, table in enumerate(sums_dram):
                        sp.dma_start(sums[:, u % 2, i, :], table.rearrange("(t p) w -> p t w", p=P)[:, bass.ds(t, 1), :]
                                     ).then_inc(s_load[u % 2], 16)

                def store(t, u):
                    sp.wait_ge(s_wtc, t + 1)
                    sp.dma_start(wt_rows[:, bass.ds(t, 1), :], wt[:, u % 2:u % 2 + 1, :]).then_inc(s_store[u % 2], 16)
                pipeline(sp, TILES, 4, [(0, load), (7, store)])
                for u in range(2):
                    sp.wait_ge(s_store[u], 16 * len(range(u, TILES, 2)))

            @block.gpsimd
            def _(pool):
                pool.memset(wsum[:], 0.0).then_inc(s_init, 1)
                pool.wait_ge(s_init, 1)

                def add_tables(t, u):
                    assert U == 4
                    fence(pool, s_load[u % 2], U * landed(t, u % 2, 2))
                    pool.tensor_tensor(sums[:, u % 2, 0:2, :], sums[:, u % 2, 0:2, :], sums[:, u % 2, 2:4, :], ALU.add
                                       ).then_inc(s_tables, 1)
                    fence(pool, s_tables, 2 * t + 1)
                    pool.tensor_tensor(sums[:, u % 2, 0, :], sums[:, u % 2, 0, :], sums[:, u % 2, 1, :], ALU.add
                                       ).then_inc(s_tables, 1)

                def sum_weights(t, u):
                    if not early(t, 1):
                        pool.wait_ge(s_wsum, t)
                    fence(pool, s_wgt, t + 1)
                    pool.tensor_tensor(wsum[:], wsum[:], soft_flat[:, u, :], ALU.add).then_inc(s_wsum, 1)
                pipeline(pool, TILES, 4, [(3, pool_norm(pool)), (7, sum_weights), (0, add_tables)])
                pool.wait_ge(s_wsum, TILES)

            @block.vector
            def _(dve):
                def node_mean(t, u):
                    if not early(t, 2):
                        dve.wait_ge(s_meant, t - 1)
                    dve.wait_ge(s_tables, 2 * t + 2)
                    if not early(t, 1):
                        dve.wait_ge(s_mean, t)
                    link = Chain(dve, s_c0, 2 * t, 2)
                    link(dve.tensor_scalar(cnt[:], sums[:, u % 2, 0, C:SUMW], 1.0, None, ALU.max))
                    link(dve.reciprocal(cnt[:], cnt[:]))
                    dve.tensor_scalar(mean[:, u % 2, :], sums[:, u % 2, 0, 0:C], cnt[:], None, ALU.mult
                                      ).then_inc(s_mean, 1)

                def row_of(t):
                    return x[:, bass.ds(t, 1), :].rearrange("p a c -> p (a c)")

                def add_and_measure(t, u):
                    dve.wait_ge(s_mm2, t + 1)
                    dve.tensor_tensor(row_of(t), row_of(t), bank[1][:, 0:C], ALU.add).then_inc(s_added, 1)
                    dve.wait_ge(s_added, t + 1)
                    measure(dve, Chain(dve, s_c1, t, 1), row_of(t), t, u)

                def normalize(t, u):
                    if not early(t, 4):
                        dve.wait_ge(s_u, t - 3)
                    apply(dve, row_of(t), xn[:, u, :], t, u, s_xn)

                def shift(t, u):
                    dve.wait_ge(s_log, t + 1)
                    if not early(t, 4):
                        dve.wait_ge(s_wt, t - 3)
                        dve.wait_ge(s_wsum, t - 3)
                    link = Chain(dve, s_c2, 2 * t, 2)
                    link(dve.tensor_tensor(soft_flat[:, u, :], bank[3][:], b_logits[:], ALU.add))
                    link(dve.tensor_reduce(hmax[:], soft[:, u, :, :], AX, ALU.max))
                    dve.tensor_tensor(soft[:, u, :, :], soft[:, u, :, :],
                                      hmax[:].unsqueeze(2).broadcast_to((P, H0, G0)), ALU.subtract).then_inc(s_shift, 1)

                def weigh(t, u):
                    dve.wait_ge(s_exp, t + 1)
                    link = Chain(dve, s_c3, 3 * t, 3)
                    link(dve.tensor_reduce(hsum[:], soft[:, u, :, :], AX, ALU.add))
                    link(dve.reciprocal(hsum[:], hsum[:]))
                    link(dve.tensor_scalar(hsum[:], hsum[:], valid[:, bass.ds(t, 1)], None, ALU.mult))
                    dve.tensor_tensor(soft[:, u, :, :], soft[:, u, :, :],
                                      hsum[:].unsqueeze(2).broadcast_to((P, H0, G0)), ALU.mult).then_inc(s_wgt, 1)
                pipeline(dve, TILES, 4, [(4, normalize), (3, add_and_measure), (6, weigh), (1, node_mean), (5, shift)])

            @block.scalar
            def _(act):
                def copy_wt(t, u):
                    act.wait_ge(s_wt, t + 1)
                    if not early(t, 2):
                        act.wait_ge(s_store[u % 2], landed(t, u % 2, 2) - 16)
                    act.copy(wt[:, u % 2, :], bank[7][:]).then_inc(s_wtc, 1)

                def exponent(t, u):
                    act.wait_ge(s_shift, t + 1)
                    act.activation(soft_flat[:, u, :], soft_flat[:, u, :], ACT.Exp).then_inc(s_exp, 1)

                def copy_xnt(t, u):
                    act.wait_ge(s_xt, t + 1)
                    if not early(t, 2):
                        act.wait_ge(s_log, t - 1)
                    act.copy(xnt[:, u % 2, :], bank[2][:, 0:C]).then_inc(s_xtc, 1)

                def copy_meant(t, u):
                    act.wait_ge(s_meant, t + 1)
                    if not early(t, 2):
                        act.wait_ge(s_mm2, t - 1)
                    act.copy(meant[:, u % 2, :], bank[0][:, 0:C]).then_inc(s_meantc, 1)
                pipeline(act, TILES, 4, [(7, copy_wt), (2, copy_meant), (4, copy_xnt), (5, exponent)])

            @block.tensor
            def _(pe):
                def slices(t, u):
                    pe.wait_ge(s_wgt, t + 1)
                    for m in range(INNER // P):
                        mm = pe.matmul(bank[5 + m // 2][:, (m % 2) * C:(m % 2 + 1) * C], soft_flat[:, u, m * P:(m + 1) * P],
                                       xn[:, u, :], start=(early(t, 1) and m % 2 == 0), stop=False, skip_group_check=True)
                    mm.then_inc(s_u, 1)
                    if not early(t, 1):
                        pe.wait_ge(s_wtc, t)
                    for m in range(INNER // P):
                        mm = pe.transpose(bank[7][:, m * P:(m + 1) * P], soft_flat[:, u, m * P:(m + 1) * P], ident[:])
                    mm.then_inc(s_wt, 1)

                def logits(t, u):
                    pe.wait_ge(s_xtc, t + 1)
                    if not early(t, 1):
                        pe.wait_ge(s_shift, t)
                    for k in range(KC):
                        mm = pe.matmul(bank[3][:], xnt[:, u % 2, k * P:(k + 1) * P], w_logits[:, k, :],
                                       start=(k == 0), stop=(k == KC - 1))
                    mm.then_inc(s_log, 1)

                def project_mean(t, u):
                    pe.wait_ge(s_meantc, t + 1)
                    if not early(t, 1):
                        pe.wait_ge(s_added, t)
                    for k in range(KC):
                        mm = pe.matmul(bank[1][:, 0:C], meant[:, u % 2, k * P:(k + 1) * P], w["l0_w2t"][:, k, :],
                                       start=(k == 0), stop=(k == KC - 1))
                    mm.then_inc(s_mm2, 1)

                def turn_xn(t, u):
                    pe.wait_ge(s_xn, t + 1)
                    if not early(t, 1):
                        pe.wait_ge(s_xtc, t)
                    for k in range(KC):
                        mm = pe.transpose(bank[2][:, k * P:(k + 1) * P], xn[:, u, k * P:(k + 1) * P], ident[:])
                    mm.then_inc(s_xt, 1)

                def turn_mean(t, u):
                    pe.wait_ge(s_mean, t + 1)
                    if not early(t, 1):
                        pe.wait_ge(s_meantc, t)
                    for k in range(KC):
                        mm = pe.transpose(bank[0][:, k * P:(k + 1) * P], mean[:, u % 2, k * P:(k + 1) * P], ident[:])
                    mm.then_inc(s_meant, 1)
                pipeline(pe, TILES, 4, [(7, slices), (2, turn_mean), (5, logits), (4, turn_xn), (2, project_mean)])

        s_cv, s_cp, s_ca = sem("c_vector_steps"), sem("c_tensor_steps"), sem("c_exp_ready")
        s_pack = sem("c_slice_out_packed")
        with ExitStack() as scope:
            def sc(name, shape, dt=F32):
                return scope.enter_context(nc.sbuf_tensor(name, shape, dt))
            MI = INNER // P
            un = q_tab[:, 0:MI * C].rearrange("p (m c) -> p m c", m=MI)
            norm = sc("c_norm", [P, MI])
            share = sc("c_share", [P, MI])
            unt = q_tab[:, MI * C:MI * C + KC * INNER].rearrange("p (k n) -> p k n", k=KC)
            share_t = sc("c_share_t", [1, INNER])
            tokens_t = sc("c_tokens_t", [D0, INNER])
            qt, kt, vt = (sc("c_" + n, [D0, INNER]) for n in ("qt", "kt", "vt"))
            prob = sc("c_prob", [G0, H0, G0])
            prob_t = sc("c_prob_t", [G0, H0, G0])
            smax, ssum = sc("c_smax", [G0, H0]), sc("c_ssum", [G0, H0])
            vout = acc[0:G0, 0:H0 * C].rearrange("p (h c) -> p h c", h=H0)
            attended = acc[0:G0, H0 * C:2 * H0 * C].rearrange("p (h c) -> p h c", h=H0)
            block = scope.enter_context(nc.Block())

            C_SHARE = 3 + MI + 1
            C_SHT = C_SHARE + KC + 1
            C_TOK = C_SHT + 1
            C_VT = C_TOK + 3
            C_SUB = C_VT + 3
            C_PROB = C_SUB + 3
            C_PROBT = C_PROB + 1
            C_LAST = C_PROBT + H0
            T_NORM, T_UNT, T_TOK, T_QKV, T_SCORE, T_PROBT = range(1, 7)
            T_VOUT = T_PROBT + H0 // 2

            @block.vector
            def _(dve):
                count = [0]

                def link(ins):
                    ins.then_inc(s_cv, 1)
                    count[0] += 1
                    dve.wait_ge(s_cv, count[0])
                dve.wait_ge(s_cp, T_NORM)
                link(dve.tensor_copy(norm[:], bank[0][:, 0:MI]))
                link(dve.tensor_scalar(share[:], norm[:], 1e-5, None, ALU.add))
                link(dve.reciprocal(share[:], share[:]))
                for m in range(MI):
                    link(dve.tensor_scalar(un[:, m, :], bank[5 + m // 2][:, (m % 2) * C:(m % 2 + 1) * C], share[:, m:m + 1],
                                           None, ALU.mult))
                link(dve.tensor_tensor(share[:], share[:], norm[:], ALU.mult))
                dve.wait_ge(s_cp, T_UNT)
                for k in range(KC):
                    link(dve.tensor_copy(unt[:, k, :], bank[1 + k][:]))
                link(dve.tensor_copy(share_t[:], bank[3][0:1, :]))
                dve.wait_ge(s_cp, T_TOK)
                link(dve.tensor_copy(tokens_t[:], bank[4][0:D0, :]))
                dve.wait_ge(s_cp, T_QKV)
                link(dve.tensor_copy(qt[:], bank[0][0:D0, :]))
                link(dve.tensor_copy(kt[:], bank[1][0:D0, :]))
                link(dve.tensor_copy(vt[:], bank[2][0:D0, :]))
                dve.wait_ge(s_cp, T_SCORE)
                link(dve.tensor_scalar(prob[:], bank[3][0:G0, :].rearrange("p (h g) -> p h g", h=H0), float(D0) ** -0.5,
                                       None, ALU.mult))
                link(dve.tensor_reduce(smax[:], prob[:], AX, ALU.max))
                link(dve.tensor_tensor(prob[:], prob[:], smax[:].unsqueeze(2).broadcast_to((G0, H0, G0)), ALU.subtract))
                dve.wait_ge(s_ca, 1)
                link(dve.tensor_reduce(ssum[:], prob[:], AX, ALU.add))
                link(dve.reciprocal(ssum[:], ssum[:]))
                link(dve.tensor_tensor(prob[:], prob[:], ssum[:].unsqueeze(2).broadcast_to((G0, H0, G0)), ALU.mult))
                dve.wait_ge(s_cp, T_PROBT)
                link(dve.tensor_copy(prob_t[:], bank[0][0:G0, :].rearrange("p (h g) -> p h g", h=H0)))
                for i in range(H0 // 2):
                    dve.wait_ge(s_cp, T_PROBT + 1 + i)
                    link(dve.tensor_copy(vout[:, 2 * i:2 * i + 2, :], bank[1 + i][0:G0, :].rearrange("p (h c) -> p h c", h=2)))
                for i in range(H0 // 2):
                    dve.wait_ge(s_cp, T_VOUT + 1 + i)
                    link(dve.tensor_copy(attended[:, 2 * i:2 * i + 2, :],
                                         bank[(5, 6, 7, 0)[i]][0:G0, :].rearrange("p (h c) -> p h c", h=2)))
                assert count[0] == C_LAST

            @block.scalar
            def _(act):
                act.wait_ge(s_cv, C_SUB)
                act.activation(prob[:], prob[:], ACT.Exp).then_inc(s_ca, 1)

            @block.tensor
            def _(pe):
                for m in range(MI):
                    mm = pe.matmul(bank[0][:, m:m + 1], wsum[:, m * P:(m + 1) * P], ones[:, 0:1], start=True, stop=True)
                mm.then_inc(s_cp, 1)
                pe.wait_ge(s_cv, C_SHARE)
                for m in range(MI):
                    for k in range(KC):
                        pe.transpose(bank[1 + k][:, m * P:(m + 1) * P], un[:, m, k * P:(k + 1) * P], ident[:])
                    mm = pe.transpose(bank[3][0:1, m * P:(m + 1) * P], share[:, m:m + 1], ident[:])
                mm.then_inc(s_cp, 1)
                pe.wait_ge(s_cv, C_SHT)
                for h in range(H0):
                    cols = slice(h * G0, (h + 1) * G0)
                    for k in range(KC):
                        pe.matmul(bank[4][0:D0, cols], w["l0_fx"][:, k, cols], unt[:, k, cols], start=(k == 0), stop=False)
                    mm = pe.matmul(bank[4][0:D0, cols], w["b_fx_row"][0:1, cols], share_t[0:1, cols], start=False, stop=True)
                mm.then_inc(s_cp, 1)
                pe.wait_ge(s_cv, C_TOK)
                for i, name in enumerate(("w_q", "w_k", "w_v")):
                    mm = pe.matmul(bank[i][0:D0, :], w[name][:], tokens_t[:], start=True, stop=True)
                mm.then_inc(s_cp, 1)
                pe.wait_ge(s_cv, C_VT)
                for h in range(H0):
                    cols = slice(h * G0, (h + 1) * G0)
                    mm = pe.matmul(bank[3][0:G0, cols], qt[:, cols], kt[:, cols], start=True, stop=True)
                mm.then_inc(s_cp, 1)
                pe.wait_ge(s_cv, C_PROB)
                for h in range(H0):
                    mm = pe.transpose(bank[0][0:G0, h * G0:(h + 1) * G0], prob[:, h, :], ident[0:G0, 0:G0])
                mm.then_inc(s_cp, 1)
                for i in range(H0 // 2):
                    for h in (2 * i, 2 * i + 1):
                        mm = pe.matmul(bank[1 + i][0:G0, (h % 2) * C:(h % 2 + 1) * C], vt[:, h * G0:(h + 1) * G0],
                                       w["l0_slice_out"][:, h, :], start=True, stop=True)
                    mm.then_inc(s_cp, 1)
                for i in range(H0 // 2):
                    pe.wait_ge(s_cv, C_PROBT + 1 + i)
                    for h in (2 * i, 2 * i + 1):
                        mm = pe.matmul(bank[(5, 6, 7, 0)[i]][0:G0, (h % 2) * C:(h % 2 + 1) * C], prob_t[:, h, :], vout[:, h, :],
                                       start=True, stop=True)
                    mm.then_inc(s_cp, 1)

            @block.sync
            def _(sp):
                sp.wait_ge(s_cv, C_LAST)
                pairs = attended.rearrange("p (m two) c -> p two m c", two=2)
                for half in range(2):
                    sp.dma_start(slice_out[half * G0:(half + 1) * G0, :, :], pairs[:, half, :, :]).then_inc(s_pack, 16)
                sp.wait_ge(s_pack, 32)

        pool_norm, measure, apply = normalize_stages(0)
        s_o, s_xn, s_xt, s_xtc = sem("d_slices_ready"), sem("d_xn_ready"), sem("d_xn_transposed"), sem("d_xnt_copied")
        s_qkv, s_q, s_kv = sem("d_products_ready"), sem("d_queries_kept"), sem("d_kv_ready")
        s_c1, s_zero, s_added = sem("d_norm_chain"), sem("d_acc_zeroed"), sem("d_added")
        s_load = [sem(f"d_wt_landed{u}") for u in range(2)]
        s_store = [sem(f"d_kv_stored{u}") for u in range(2)]
        with ExitStack() as scope:
            def sc(name, shape, dt=F32):
                return scope.enter_context(nc.sbuf_tensor(name, shape, dt))
            wt = sc("d_wt", [P, 2, INNER])
            xn, xnt = sc("d_xn", [P, 2, C]), sc("d_xnt", [P, 2, C])
            kv = sc("d_kv", [P, 2, 2 * C])
            block = scope.enter_context(nc.Block())

            @block.sync
            def _(sp):
                def load(t, u):
                    if not early(t, 2):
                        sp.wait_ge(s_o, t - 1)
                    sp.dma_start(wt[:, u:u + 1, :], wt_rows[:, bass.ds(t, 1), :]).then_inc(s_load[u], 16)
                pipeline(sp, TILES, 2, [(0, load)])

            @block.gpsimd
            def _(pool):
                pool.memset(acc[:], 0.0).then_inc(s_zero, 1)
                pipeline(pool, TILES, 2, [(1, pool_norm(pool))])
                pool.wait_ge(s_zero, 1)

            @block.vector
            def _(dve):
                def keep(t, u):
                    dve.wait_ge(s_qkv, t + 1)
                    dve.tensor_tensor(q_tab[:, bass.ds(t * C, C)], bank[4 + u][:, 0:C], bias["bq"][:], ALU.add
                                      ).then_inc(s_q, 1)
                    if not early(t, 2):
                        dve.wait_ge(s_store[u], landed(t, u, 2) - 16)
                    dve.tensor_tensor(kv[:, u, :], bank[6 + u][:], bias["bkv"][:], ALU.add).then_inc(s_kv, 1)

                def row_of(t):
                    return x[:, bass.ds(t, 1), :].rearrange("p a c -> p (a c)")

                def add_and_measure(t, u):
                    dve.wait_ge(s_o, t + 1)
                    dve.tensor_tensor(row_of(t), row_of(t), bank[u][:, 0:C], ALU.add).then_inc(s_added, 1)
                    dve.wait_ge(s_added, t + 1)
                    link = Chain(dve, s_c1, 2 * t, 2)
                    link(dve.tensor_tensor(row_of(t), row_of(t), bias["b_out"][:], ALU.add))
                    measure(dve, link, row_of(t), t, u)

                def normalize(t, u):
                    if not early(t, 2):
                        dve.wait_ge(s_xt, t - 1)
                    apply(dve, row_of(t), xn[:, u, :], t, u, s_xn)
                pipeline(dve, TILES, 2, [(2, normalize), (1, add_and_measure), (4, keep)])
                dve.wait_ge(s_q, TILES)

            @block.scalar
            def _(act):
                def copy_xnt(t, u):
                    act.wait_ge(s_xt, t + 1)
                    if not early(t, 2):
                        act.wait_ge(s_qkv, t - 1)
                    act.copy(xnt[:, u, :], bank[2 + u][:, 0:C]).then_inc(s_xtc, 1)

                def store(t, u):
                    act.wait_ge(s_kv, t + 1)
                    act.dma_start(kv_rows[:, bass.ds(t, 1), :], kv[:, u:u + 1, :]).then_inc(s_store[u], 16)
                pipeline(act, TILES, 2, [(2, copy_xnt), (4, store)])
                for u in range(2):
                    act.wait_ge(s_store[u], 16 * len(range(u, TILES, 2)))

            @block.tensor
            def _(pe):
                def project(t, u):
                    pe.wait_ge(s_xtc, t + 1)
                    if not early(t, 2):
                        pe.wait_ge(s_kv, t - 1)
                    for k in range(KC):
                        pe.matmul(bank[4 + u][:, 0:C], xnt[:, u, k * P:(k + 1) * P], w["l1_qt"][:, k, :],
                                  start=(k == 0), stop=(k == KC - 1))
                    for k in range(KC):
                        mm = pe.matmul(bank[6 + u][:], xnt[:, u, k * P:(k + 1) * P], w["l1_kvt"][:, k, :],
                                       start=(k == 0), stop=(k == KC - 1))
                    mm.then_inc(s_qkv, 1)

                def spread_slices(t, u):
                    pe.wait_ge(s_load[u], landed(t, u, 2))
                    if not early(t, 2):
                        pe.wait_ge(s_added, t - 1)
                    for m in range(INNER // P):
                        mm = pe.matmul(bank[u][:, 0:C], wt[:, u, m * P:(m + 1) * P], slice_out[:, m, :],
                                       start=(m == 0), stop=(m == INNER // P - 1))
                    mm.then_inc(s_o, 1)

                def turn_xn(t, u):
                    pe.wait_ge(s_xn, t + 1)
                    if not early(t, 2):
                        pe.wait_ge(s_xtc, t - 1)
                    for k in range(KC):
                        mm = pe.transpose(bank[2 + u][:, k * P:(k + 1) * P], xn[:, u, k * P:(k + 1) * P], ident[:])
                    mm.then_inc(s_xt, 1)
                pipeline(pe, TILES, 2, [(0, spread_slices), (2, turn_xn), (3, project)])

        s_idx, s_oh, s_oht, s_ohc = sem("e_index_ready"), sem("e_onehot_ready"), sem("e_onehot_transposed"), sem("e_oht_copied")
        s_qe, s_prod, s_clip, s_exp = sem("e_queries_spread"), sem("e_product_ready"), sem("e_scores_clipped"), sem("e_exp_ready")
        s_msg, s_sum, s_acc, s_c = sem("e_message_ready"), sem("e_sum_ready"), sem("e_accumulated"), sem("e_scores_ready")
        s_sq = sem("e_distance_squared")
        Q = SLOTS // 2
        G = STEP_UNROLL
        PAIRS, PG = STEPS_RUN // 2, G // 2
        s_land = [sem(f"e_kv_landed{u}") for u in range(Q)]
        with ExitStack() as scope:
            def sc(name, shape, dt=F32):
                return scope.enter_context(nc.sbuf_tensor(name, shape, dt))
            index = sc("e_index", [P, Q, 2], U32)
            kv = sc("e_kv", [P, Q, 2, 2 * C])
            onehot = w_logits[:].rearrange("p k n -> p (k n)").rearrange("p (q i e) -> p q i e", q=Q, i=2)
            spent = slice_out[:].rearrange("p m c -> p (m c)")
            onehot_t = spent[:, 0:4 * P].rearrange("p (q e) -> p q e", q=2)
            prod = spent[:, 4 * P:4 * P + 2 * C].rearrange("p (i c) -> p i c", i=2)
            score = sc("e_score", [P, 2, 2, H1])
            msg = sc("e_msg", [P, 2, 2, ACCW])
            block = scope.enter_context(nc.Block())

            def pair_landed(q, u):
                return 2 * (q - u) * (16 // Q) + 32

            @block.gpsimd
            def _(pool):
                def gather(q, u):
                    u %= Q
                    if not early(q, Q):
                        pool.wait_ge(s_msg, q - (Q - 1))
                    fence(pool, s_idx, q + 1)
                    for i in range(2):
                        pool.indirect_dma_start(out=kv[:, u, i, :], out_offset=None, in_=kv_dram,
                                                in_offset=bass.IndirectOffsetOnAxis(ap=index[:, u, i:i + 1], axis=0)
                                                ).then_inc(s_land[u], 16)
                pipeline(pool, PAIRS, PG, [(0, gather)])

            @block.scalar
            def _(act):
                def exponent(q, u):
                    act.wait_ge(s_clip, q + 1)
                    if not early(q, 2):
                        act.wait_ge(s_sum, 2 * (q - 1))
                    act.activation(msg[:, u % 2, :, C:ACCW], score[:, u % 2, :, :], ACT.Exp).then_inc(s_exp, 1)

                def make_onehot(q, u):
                    if not early(q, Q):
                        act.wait_ge(s_sum, 2 * (q - (Q - 1)))
                    for i in range(2):
                        act.activation(onehot[:, u % Q, i, :], iota_row[:], ACT.Square, scale=-1.0,
                                       bias=dst_step[:, bass.ds(2 * q + i, 1)]).then_inc(s_sq, 1)
                    act.wait_ge(s_sq, 2 * (q + 1))
                    act.activation(onehot[:, u % Q, :, :], onehot[:, u % Q, :, :], ACT.Relu, scale=-1.0,
                                   bias=ones[:, 0:1]).then_inc(s_oh, 1)

                def copy_onehot_t(q, u):
                    act.wait_ge(s_oht, q + 1)
                    if not early(q, 2):
                        act.wait_ge(s_qe, q - 1)
                    act.copy(onehot_t[:, u % 2, :], bank[u % 2][:, 0:2 * P]).then_inc(s_ohc, 1)

                def fetch_index(q, u):
                    u %= Q
                    if not early(q, Q):
                        fence(act, s_land[u], pair_landed(q, u) - 32)
                    act.copy(index[:, u, :], src_step[:, bass.ds(2 * q, 2)]).then_inc(s_idx, 1)
                pipeline(act, PAIRS, PG, [(3, exponent), (0, fetch_index), (1, copy_onehot_t), (0, make_onehot)])

            @block.vector
            def _(dve):
                heads = "p i (h d) -> p i h d"
                offsets = [None] * G

                def load_offsets(i, v):
                    if v == 0:
                        found = nc.values_load_multi_w_load_instructions(
                            tile_words[0:1, bass.ds(i // 2, G // 4)], engines=(mybir.EngineType.DVE,), min_val=0,
                            max_val=32 ** 4 - 1)[1]
                        for k in range(G):
                            tile = (found[k // 4] >> (5 * (k % 4))) & 31
                            offsets[k] = (tile * ACCW).with_bounds(min_val=0, max_val=(TILES - 1) * ACCW)

                def product(q, u):
                    dve.wait_ge(s_qe, q + 1)
                    dve.wait_ge(s_land[u % Q], pair_landed(q, u % Q))
                    if not early(q, 1):
                        dve.wait_ge(s_c, q)
                    dve.scalar_tensor_tensor(out=prod, in0=bank[2 + u % 2][:].rearrange("p (i c) -> p i c", i=2),
                                             scalar=float(D1) ** -0.5, in1=kv[:, u % Q, :, 0:C],
                                             op0=ALU.mult, op1=ALU.mult).then_inc(s_prod, 1)

                def scores(q, u):
                    dve.wait_ge(s_prod, q + 1)
                    dve.tensor_reduce(score[:, u % 2, :, :], prod.rearrange(heads, h=H1), AX, ALU.add).then_inc(s_c, 1)

                def clip(q, u):
                    dve.wait_ge(s_c, q + 1)
                    dve.tensor_scalar(score[:, u % 2, :, :], score[:, u % 2, :, :], 10.0, -10.0, ALU.min, ALU.max
                                      ).then_inc(s_clip, 1)

                def message(q, u):
                    dve.wait_ge(s_exp, q + 1)
                    dve.tensor_tensor(msg[:, u % 2, :, 0:C].rearrange(heads, h=H1),
                                      kv[:, u % Q, :, C:2 * C].rearrange(heads, h=H1),
                                      msg[:, u % 2, :, C:ACCW].unsqueeze(3).broadcast_to((P, 2, H1, D1)), ALU.mult
                                      ).then_inc(s_msg, 1)

                def accumulate(i):
                    def body(q, u):
                        dve.wait_ge(s_sum, 2 * q + i + 1)
                        if i == 1 or not early(q, 1):
                            dve.wait_ge(s_acc, 2 * q + i)
                        row = acc[:, bass.ds(offsets[(2 * u + i + ADD_LAG) % G], ACCW)]
                        dve.tensor_tensor(row, row, bank[4 + 2 * (u % 2) + i][:, 0:ACCW], ALU.add).then_inc(s_acc, 1)
                    return body
                pipeline(dve, PAIRS, PG, [(3, clip), (2, product), (ADD_LAG // 2, accumulate(0)), (3, message), (2, scores),
                                          (ADD_LAG // 2, accumulate(1))],
                         load_offsets)
                dve.wait_ge(s_acc, STEPS_RUN)

            @block.tensor
            def _(pe):
                offsets = [None] * G

                def load_offsets(i, v):
                    offsets[2 * v:2 * v + 2] = nc.values_load_multi_w_load_instructions(
                        q_off[0:1, bass.ds(2 * i, 2)], engines=(mybir.EngineType.PE,), min_val=0,
                        max_val=(TILES - 1) * C)[1]

                def turn_onehot(q, u):
                    pe.wait_ge(s_oh, q + 1)
                    if not early(q, 2):
                        pe.wait_ge(s_ohc, q - 1)
                    for i in range(2):
                        mm = pe.transpose(bank[u % 2][:, i * P:(i + 1) * P], onehot[:, u % Q, i, :], ident[:])
                    mm.then_inc(s_oht, 1)

                def spread_queries(q, u):
                    pe.wait_ge(s_ohc, q + 1)
                    if not early(q, 2):
                        pe.wait_ge(s_prod, q - 1)
                    for i in range(2):
                        mm = pe.matmul(bank[2 + u % 2][:, i * C:(i + 1) * C], onehot_t[:, u % 2, i * P:(i + 1) * P],
                                       q_tab[:, bass.ds(offsets[(2 * u + i + SPREAD_LAG) % G], C)], start=True, stop=True)
                    mm.then_inc(s_qe, 1)

                def sum_messages(q, u):
                    pe.wait_ge(s_msg, q + 1)
                    for i in range(2):
                        if not early(q, 2):
                            pe.wait_ge(s_acc, 2 * (q - 2) + i + 1)
                        pe.matmul(bank[4 + 2 * (u % 2) + i][:, 0:ACCW], onehot[:, u % Q, i, :], msg[:, u % 2, i, :],
                                  start=True, stop=True).then_inc(s_sum, 1)
                pipeline(pe, PAIRS, PG, [(1, turn_onehot), (SPREAD_LAG // 2, spread_queries), (3, sum_messages)],
                         load_offsets)
        picks_flat = w_logits[:].rearrange("p k n -> p (k n)")[:, 0:EXPERTS * TILES]
        picks = picks_flat.rearrange("p (e t) -> p e t", e=EXPERTS)
        pool_norm1, measure1, apply1 = normalize_stages(0)
        pool_norm2, measure2, apply2 = normalize_stages(1)
        pool_norm3, measure3, apply3 = normalize_stages(2)
        s_wv, s_wvt, s_wvtc, s_y = sem("f_attended_ready"), sem("f_attended_transposed"), sem("f_attended_t_copied"), sem("f_y_ready")
        s_feat, s_hn, s_hnt, s_hntc = sem("f_features_ready"), sem("f_hn_ready"), sem("f_hn_transposed"), sem("f_hnt_copied")
        s_hid, s_gelu, s_down = sem("f_hidden_ready"), sem("f_gelu_ready"), sem("f_down_ready")
        s_xn, s_xnt, s_xntc = sem("g_xn_ready"), sem("g_xn_transposed"), sem("g_xnt_copied")
        s_route, s_pick, s_kept, s_pre = sem("g_router_ready"), sem("g_pick_ready"), sem("g_xn_kept"), sem("g_constants_ready")
        s_c0, s_c1, s_c3, s_c4 = sem("f_attended_chain"), sem("f_y_chain"), sem("f_down_chain"), sem("g_route_chain")
        s_n0, s_n1, s_n3 = sem("f_feature_norm_chain"), sem("f_hn_chain"), sem("g_xn_chain")
        with ExitStack() as scope:
            def sc(name, shape, dt=F32):
                return scope.enter_context(nc.sbuf_tensor(name, shape, dt))
            HB = MC // 4
            inv_den = sc("f_inv_den", [P, H1])
            wv, wvt, feat = (sc("f_" + n, [P, 2, C]) for n in ("wv", "wvt", "feat"))
            y = sc("f_y", [P, 2, C])
            hn, hnt = sc("f_hn", [P, 2, C]), sc("f_hnt", [P, 2, C])
            units = q_tab[:].rearrange("p (m n) -> p m n", n=P)
            hidden = units[:, 0:2 * MC, :].rearrange("p (u m) n -> p u m n", u=2)
            xn, xnt = sc("g_xn", [P, 2, C]), sc("g_xnt", [P, 2, C])
            logit, is_max, rank, best = (sc("g_" + n, [P, k]) for n, k in (("logit", EXPERTS), ("is_max", EXPERTS),
                                                                          ("rank", EXPERTS), ("best", 1)))
            block = scope.enter_context(nc.Block())

            @block.gpsimd
            def _(pool):
                pipeline(pool, TILES, 2, [(5, pool_norm3(pool)), (2, pool_norm2(pool)), (0, pool_norm1(pool))])

            @block.vector
            def _(dve):
                heads = "p (h d) -> p h d"

                def row_of(t):
                    return x[:, bass.ds(t, 1), :].rearrange("p a c -> p (a c)")

                def attended(t, u):
                    if not early(t, 2):
                        dve.wait_ge(s_wvt, t - 1)
                    link = Chain(dve, s_c0, 2 * t, 2)
                    link(dve.tensor_scalar(inv_den[:], acc[:, bass.ds(t * ACCW + C, H1)], 1e-30, None, ALU.max))
                    link(dve.reciprocal(inv_den[:], inv_den[:]))
                    dve.tensor_tensor(wv[:, u, :].rearrange(heads, h=H1),
                                      acc[:, bass.ds(t * ACCW, C)].rearrange(heads, h=H1),
                                      inv_den[:].unsqueeze(2).broadcast_to((P, H1, D1)), ALU.mult).then_inc(s_wv, 1)
                    measure1(dve, Chain(dve, s_n0, t, 1), row_of(t), t, u)

                def normalize_features(t, u):
                    apply1(dve, row_of(t), feat[:, u, :], t, u, s_feat)

                def add_y(t, u):
                    dve.wait_ge(s_y, t + 1)
                    dve.wait_ge(s_feat, t + 1)
                    link = Chain(dve, s_c1, 3 * t, 3)
                    link(dve.tensor_tensor(y[:, u, :], bank[2][:, 0:C], feat[:, u, :], ALU.add))
                    link(dve.tensor_tensor(y[:, u, :], y[:, u, :], bias["bp"][:], ALU.add))
                    link(dve.tensor_tensor(row_of(t), row_of(t), y[:, u, :], ALU.add))
                    measure2(dve, Chain(dve, s_n1, t, 1), y[:, u, :], t, u)

                def normalize_y(t, u):
                    if not early(t, 2):
                        dve.wait_ge(s_hnt, t - 1)
                    apply2(dve, y[:, u, :], hn[:, u, :], t, u, s_hn)

                def add_down(t, u):
                    dve.wait_ge(s_down, t + 1)
                    link = Chain(dve, s_c3, 2 * t, 2)
                    link(dve.tensor_tensor(row_of(t), row_of(t), bank[3][:, 0:C], ALU.add))
                    link(dve.tensor_tensor(row_of(t), row_of(t), bias["b2m"][:], ALU.add))
                    measure3(dve, Chain(dve, s_n3, t, 1), row_of(t), t, u)

                def normalize_row(t, u):
                    if not early(t, 2):
                        dve.wait_ge(s_xnt, t - 1)
                        dve.wait_ge(s_kept, t - 1)
                    apply3(dve, row_of(t), xn[:, u, :], t, u, s_xn)

                def route(t, u):
                    dve.wait_ge(s_route, t + 1)
                    link = Chain(dve, s_c4, 5 * t, 5)
                    link(dve.tensor_tensor(logit[:], bank[1][:, C:C + EXPERTS], bias["router_b"][:], ALU.add))
                    link(dve.tensor_reduce(best[:], logit[:], AX, ALU.max))
                    link(dve.tensor_scalar(is_max[:], logit[:], best[:], None, ALU.is_equal))
                    link(dve.tensor_tensor(rank[:], is_max[:], countdown[:], ALU.mult))
                    link(dve.tensor_reduce(best[:], rank[:], AX, ALU.max))
                    dve.tensor_scalar(picks[:, :, bass.ds(t, 1)], countdown[:].unsqueeze(2), best[:], None, ALU.is_equal
                                      ).then_inc(s_pick, 1)

                dve.tensor_scalar(countdown[:], iota_row[:, 0:EXPERTS], -1.0, float(EXPERTS), ALU.mult, ALU.add
                                  ).then_inc(s_pre, 1)
                dve.wait_ge(s_pre, 1)
                pipeline(dve, TILES, 2, [(6, normalize_row), (3, normalize_y), (1, normalize_features), (0, attended), (7, route),
                                         (5, add_down), (2, add_y)])
                dve.wait_ge(s_pick, TILES)

            @block.scalar
            def _(act):
                def keep(t, u):
                    act.wait_ge(s_xn, t + 1)
                    act.copy(acc[:, bass.ds(t * ACCW, C)], xn[:, u, :]).then_inc(s_kept, 1)

                def copy_xnt(t, u):
                    act.wait_ge(s_xnt, t + 1)
                    if not early(t, 2):
                        act.wait_ge(s_route, t - 1)
                    act.copy(xnt[:, u, :], bank[0][:, 0:C]).then_inc(s_xntc, 1)

                def gelu(t, u):
                    if not early(t, 2):
                        act.wait_ge(s_down, t - 1)
                    for m in range(MC):
                        if m % 4 == 0:
                            act.wait_ge(s_hid, HB * t + m // 4 + 1)
                        ins = act.activation(hidden[:, u, m, :], bank[4 + m // 4][:, (m % 4) * P:(m % 4 + 1) * P], ACT.Gelu,
                                             bias=b1_mlp[:, m:m + 1])
                    ins.then_inc(s_gelu, 1)

                def copy_hnt(t, u):
                    act.wait_ge(s_hnt, t + 1)
                    if not early(t, 2):
                        act.wait_ge(s_hid, HB * (t - 1))
                    act.copy(hnt[:, u, :], bank[0][:, 0:C]).then_inc(s_hntc, 1)

                def copy_wvt(t, u):
                    act.wait_ge(s_wvt, t + 1)
                    if not early(t, 2):
                        act.wait_ge(s_y, t - 1)
                    act.copy(wvt[:, u, :], bank[2][:, 0:C]).then_inc(s_wvtc, 1)
                pipeline(act, TILES, 2, [(6, copy_xnt), (1, copy_wvt), (6, keep), (4, gelu), (3, copy_hnt)])
                act.wait_ge(s_kept, TILES)

            @block.tensor
            def _(pe):
                def turn(t, rows, target, done):
                    for k in range(KC):
                        mm = pe.transpose(target[:, k * P:(k + 1) * P], rows[:, k * P:(k + 1) * P], ident[:])
                    mm.then_inc(done, 1)

                def router(t, u):
                    pe.wait_ge(s_xntc, t + 1)
                    if not early(t, 1):
                        pe.wait_ge(s_pick, t)
                    for k in range(KC):
                        mm = pe.matmul(bank[1][:, C:C + EXPERTS], xnt[:, u, k * P:(k + 1) * P], w["router_t"][:, k, :],
                                       start=(k == 0), stop=(k == KC - 1))
                    mm.then_inc(s_route, 1)

                def down(t, u):
                    pe.wait_ge(s_gelu, t + 1)
                    if not early(t, 1):
                        pe.wait_ge(s_c3, 2 * t - 1)
                    for m in range(MC):
                        mm = pe.matmul(bank[3][:, 0:C], hidden[:, u, m, :], w["l1_w2t"][:, m, :],
                                       start=(m == 0), stop=(m == MC - 1))
                    mm.then_inc(s_down, 1)

                def turn_xn(t, u):
                    pe.wait_ge(s_xn, t + 1)
                    pe.wait_ge(s_hntc, TILES if late(t, TILES, 3) else t + 3)
                    if late(t, TILES, 2):
                        pe.wait_ge(s_xntc, t)
                    turn(t, xn[:, u, :], bank[0][:, 0:C], s_xnt)

                def up(t, u):
                    pe.wait_ge(s_hntc, t + 1)
                    if not early(t, 1):
                        pe.wait_ge(s_gelu, t)
                    for m in range(MC):
                        for k in range(KC):
                            mm = pe.matmul(bank[4 + m // 4][:, (m % 4) * P:(m % 4 + 1) * P],
                                           w["l1_w1t"][:, k, m * P:(m + 1) * P], hnt[:, u, k * P:(k + 1) * P],
                                           start=(k == 0), stop=(k == KC - 1))
                        if m % 4 == 3:
                            mm.then_inc(s_hid, 1)

                def attention_out(t, u):
                    pe.wait_ge(s_wvtc, TILES if late(t, TILES, 2) else t + 2)
                    if late(t, TILES, 1):
                        pe.wait_ge(s_hn, t)
                    for k in range(KC):
                        mm = pe.matmul(bank[2][:, 0:C], wvt[:, u, k * P:(k + 1) * P], w["l1_pt"][:, k, :],
                                       start=(k == 0), stop=(k == KC - 1))
                    mm.then_inc(s_y, 1)

                def turn_hn(t, u):
                    pe.wait_ge(s_hn, t + 1)
                    if not early(t, 3):
                        pe.wait_ge(s_xntc, t - 2)
                    elif not early(t, 1):
                        pe.wait_ge(s_hntc, t)
                    turn(t, hn[:, u, :], bank[0][:, 0:C], s_hnt)

                def turn_wv(t, u):
                    pe.wait_ge(s_wv, t + 1)
                    if not early(t, 2):
                        pe.wait_ge(s_c1, 3 * t - 5)
                    elif t == 1:
                        pe.wait_ge(s_wvtc, 1)
                    turn(t, wv[:, u, :], bank[2][:, 0:C], s_wvt)
                pipeline(pe, TILES, 2, [(7, router), (1, turn_wv), (5, down), (6, turn_xn), (4, up), (2, attention_out),
                                        (3, turn_hn)])

        nc.clear_and_free_semaphores(held)
        nc.all_engine_barrier()
        held.clear()
        s_gc, s_gp, s_gd = sem("h_constants_ready"), sem("h_tensor_steps"), sem("h_vector_chain")
        EPAIRS = EXPERTS // 2
        MOE_STEPS = TILES + EPAIRS - 1
        MOE_RUN = -(-MOE_STEPS // 4) * 4
        ET = EXPERTS * TILES
        BANKW = 512
        ROWW = C + EXPERTS
        sorted_dram = dram("rows_by_expert", (ROWS, ROWW))
        out_dram = dram("expert_outputs", (ROWS, C))
        hs = ExitStack()

        def hsc(name, shape, dt=F32):
            return hs.enter_context(nc.sbuf_tensor(name, shape, dt))
        place = hsc("h_place", [P, TILES], U32)
        walk = hsc("h_walk", [1, 2 * MOE_RUN], I32)
        less = slice_out[:].rearrange("p m c -> p (m c)")[:, 0:ET]
        FULL, REST = ET // P, ET % P
        with ExitStack() as scope:
            def sc(name, shape, dt=F32):
                return scope.enter_context(nc.sbuf_tensor(name, shape, dt))
            totals = sc("h_totals", [P, FULL + 1])
            totals_b = sc("h_totals_b", [P, FULL + 1, P])
            chosen = sc("h_chosen", [P, ET])
            place_f = sc("h_place_f", [P, TILES])
            tile_end = sc("h_tile_end", [1, TILES])
            ends, bound = sc("h_ends", [1, EPAIRS - 1]), sc("h_bound", [1, EPAIRS - 1])
            beyond = sc("h_beyond", [1, EPAIRS - 1, TILES])
            passed = sc("h_passed", [1, MOE_RUN, EPAIRS - 1])
            pair_f = sc("h_pair_f", [1, MOE_RUN])
            block = scope.enter_context(nc.Block())

            @block.gpsimd
            def _(pool):
                pool.memset(less, 1.0).then_inc(s_gc, 1)
                pool.wait_ge(s_gc, 1)
                pool.affine_select(out=less, in_=less, compare_op=ALU.is_gt, fill=0.0, base=0,
                                   pattern=[[1, ET]], channel_multiplier=-1).then_inc(s_gc, 1)

            @block.tensor
            def _(pe):
                pe.wait_ge(s_gc, 2)
                for c in range(FULL + 1):
                    n = P if c < FULL else REST
                    mm = pe.matmul(bank[2][0:n, c:c + 1], picks_flat[:, c * P:c * P + n], ones[:, 0:1], start=True, stop=True)
                mm.then_inc(s_gp, 1)
                pe.wait_ge(s_gd, FULL + 3)
                for b in range(-(-ET // BANKW)):
                    first, last = b * BANKW, min(ET, (b + 1) * BANKW)
                    used = [c for c in range(FULL + 1) if c * P < last]
                    pe.matmul(bank[b][:, 0:last - first], less[:, 0:P], picks_flat[:, first:last], start=True, stop=False,
                              skip_group_check=True)
                    for c in used:
                        n, lo = (P if c < FULL else REST), max(first, c * P)
                        mm = pe.matmul(bank[b][:, lo - first:last - first], totals_b[0:n, c, :],
                                       less[0:n, lo - c * P:last - c * P], start=False, stop=(c == used[-1]),
                                       skip_group_check=True)
                mm.then_inc(s_gp, 1)

            @block.vector
            def _(dve):
                count = [0]

                def link(ins):
                    ins.then_inc(s_gd, 1)
                    count[0] += 1
                    dve.wait_ge(s_gd, count[0])
                dve.wait_ge(s_gp, 1)
                link(dve.tensor_copy(totals[:, 0:FULL], bank[2][:, 0:FULL]))
                link(dve.tensor_copy(totals[0:REST, FULL:FULL + 1], bank[2][0:REST, FULL:FULL + 1]))
                for c in range(FULL + 1):
                    n = P if c < FULL else REST
                    link(dve.tensor_scalar(totals_b[0:n, c, :], ones[0:n, :], totals[0:n, c:c + 1], None, ALU.mult))
                dve.wait_ge(s_gp, 2)
                for b in range(-(-ET // BANKW)):
                    first, last = b * BANKW, min(ET, (b + 1) * BANKW)
                    link(dve.tensor_tensor(chosen[:, first:last], bank[b][:, 0:last - first], picks_flat[:, first:last], ALU.mult))
                link(dve.tensor_reduce(place_f[:], chosen[:].rearrange("p (e t) -> p t e", e=EXPERTS), AX, ALU.add))
                link(dve.tensor_copy(place[:], place_f[:]))
                for m in range(EPAIRS - 1):
                    j = 2 * (m + 1) * TILES
                    link(dve.tensor_copy(ends[:, m:m + 1], bank[j // BANKW][0:1, j % BANKW:j % BANKW + 1]))
                link(dve.tensor_scalar(tile_end[:], iota_row[0:1, 0:TILES], float(P), float(P), ALU.mult, ALU.add))
                link(dve.tensor_tensor(beyond[:], ends[:].unsqueeze(2).broadcast_to((1, EPAIRS - 1, TILES)),
                                       tile_end[:].unsqueeze(1).broadcast_to((1, EPAIRS - 1, TILES)), ALU.is_gt))
                link(dve.tensor_reduce(bound[:], beyond[:], AX, ALU.add))
                link(dve.tensor_tensor(bound[:], bound[:], iota_row[0:1, 0:EPAIRS - 1], ALU.add))
                link(dve.tensor_tensor(passed[:], bound[:].unsqueeze(1).broadcast_to((1, MOE_RUN, EPAIRS - 1)),
                                       iota_row[0:1, 0:MOE_RUN].unsqueeze(2).broadcast_to((1, MOE_RUN, EPAIRS - 1)), ALU.is_lt))
                link(dve.tensor_reduce(pair_f[:], passed[:], AX, ALU.add))
                steps = walk[:].rearrange("p (s two) -> p s two", two=2)
                link(dve.tensor_copy(steps[:, :, 0:1], pair_f[:].unsqueeze(2)))
                link(dve.tensor_tensor(steps[:, :, 1:2], iota_row[0:1, 0:MOE_RUN].unsqueeze(2), pair_f[:].unsqueeze(2),
                                       ALU.subtract))

        s_idx, s_row = sem("i_place_ready"), sem("i_row_ready")
        s_scat = [sem(f"i_rows_scattered{u}") for u in range(4)]
        with ExitStack() as scope:
            def sc(name, shape, dt=F32):
                return scope.enter_context(nc.sbuf_tensor(name, shape, dt))
            index, row = sc("i_index", [P, 4], U32), sc("i_row", [P, 4, ROWW])
            block = scope.enter_context(nc.Block())

            @block.scalar
            def _(act):
                def assemble(t, u):
                    if not early(t, 4):
                        act.wait_ge(s_scat[u], landed(t, u, 4) - 16)
                    act.copy(row[:, u, 0:C], acc[:, bass.ds(t * ACCW, C)]).then_inc(s_row, 1)
                    act.copy(row[:, u, C:ROWW].unsqueeze(2), picks[:, :, bass.ds(t, 1)]).then_inc(s_row, 1)
                    act.copy(index[:, u:u + 1], place[:, bass.ds(t, 1)]).then_inc(s_row, 1)
                pipeline(act, TILES, 4, [(0, assemble)])

            @block.gpsimd
            def _(pool):
                def scatter(t, u):
                    fence(pool, s_row, 3 * t + 3)
                    pool.indirect_dma_start(out=sorted_dram, in_=row[:, u, :], in_offset=None,
                                            out_offset=bass.IndirectOffsetOnAxis(ap=index[:, u:u + 1], axis=0)
                                            ).then_inc(s_scat[u], 16)
                pipeline(pool, TILES, 4, [(0, scatter)])
                for u in range(4):
                    pool.wait_ge(s_scat[u], 16 * len(range(u, TILES, 4)))

        s_t, s_tc, s_ptc, s_b, s_bc = (sem("j_transposed"), sem("j_rows_t_copied"), sem("j_pick_t_copied"), sem("j_b2_ready"),
                                       sem("j_b2_kept"))
        s_load = [sem(f"j_rows_landed{u}") for u in range(4)]
        rows_t, total = q_tab, acc
        picks_t = hsc("h_picks_t", [EXPERTS, TILES * P], BF16)
        with ExitStack() as scope:
            def sc(name, shape, dt=F32):
                return scope.enter_context(nc.sbuf_tensor(name, shape, dt))
            row, pick_t = sc("j_row", [P, 4, ROWW]), sc("j_pick_t", [EXPERTS, 2, P])
            block = scope.enter_context(nc.Block())

            @block.sync
            def _(sp):
                ordered = sorted_dram.rearrange("(t p) c -> p t c", p=P)

                def load(t, u):
                    if not early(t, 4):
                        sp.wait_ge(s_t, t - 3)
                    sp.dma_start(row[:, u:u + 1, :], ordered[:, bass.ds(t, 1), :]).then_inc(s_load[u], 16)
                pipeline(sp, TILES, 4, [(0, load)])

            @block.tensor
            def _(pe):
                def turn_rows(t, u):
                    pe.wait_ge(s_load[u], landed(t, u, 4))
                    if not early(t, 2):
                        pe.wait_ge(s_tc, t - 1)
                        pe.wait_ge(s_ptc, 2 * (t - 1))
                    for k in range(KC):
                        pe.transpose(bank[u % 2][:, k * P:(k + 1) * P], row[:, u, k * P:(k + 1) * P], ident[:])
                    pe.transpose(bank[u % 2][0:EXPERTS, C:C + P], row[:, u, C:ROWW], ident[:]).then_inc(s_t, 1)

                def offset(t, u):
                    pe.wait_ge(s_ptc, 2 * t + 2)
                    if not early(t, 2):
                        pe.wait_ge(s_bc, t - 1)
                    pe.matmul(bank[2 + u % 2][:, 0:C], pick_t[:, u % 2, :], w["moe_b2"][:], start=True, stop=True
                              ).then_inc(s_b, 1)
                pipeline(pe, TILES, 4, [(0, turn_rows), (1, offset)])

            @block.scalar
            def _(act):
                def copy_t(t, u):
                    act.wait_ge(s_t, t + 1)
                    act.copy(rows_t[:, bass.ds(t * C, C)], bank[u % 2][:, 0:C]).then_inc(s_tc, 1)
                    if not early(t, 2):
                        act.wait_ge(s_b, t - 1)
                    act.copy(pick_t[:, u % 2, :], bank[u % 2][0:EXPERTS, C:C + P]).then_inc(s_ptc, 1)
                    act.copy(picks_t[:, bass.ds(t * P, P)], bank[u % 2][0:EXPERTS, C:C + P]).then_inc(s_ptc, 1)
                pipeline(act, TILES, 4, [(0, copy_t)])
                act.wait_ge(s_tc, TILES)
                act.wait_ge(s_ptc, 2 * TILES)

            @block.vector
            def _(dve):
                def keep(t, u):
                    dve.wait_ge(s_b, t + 1)
                    dve.tensor_copy(total[:, bass.ds(t * C, C)], bank[2 + u % 2][:, 0:C]).then_inc(s_bc, 1)
                pipeline(dve, TILES, 4, [(1, keep)])
                dve.wait_ge(s_bc, TILES)

        s_w1, s_hid, s_relu, s_eo, s_add = (sem("k_w1_copied"), sem("k_hidden_ready"), sem("k_relu_ready"), sem("k_out_ready"),
                                            sem("k_added"))
        with ExitStack() as scope:
            def sc(name, shape, dt=F32):
                return scope.enter_context(nc.sbuf_tensor(name, shape, dt))
            w1, b1 = sc("k_w1", [P, 4, KC, P]), sc("k_b1", [P, 4])
            w2, mask = sc("k_w2", [P, 4, C]), sc("k_mask", [EXPERTS, 4, P], BF16)
            hidden = sc("k_hidden", [P, 4, P])
            COPIES = 4
            block = scope.enter_context(nc.Block())

            def pair_of(engine, s):
                return nc.values_load_multi_w_load_instructions(walk[0:1, bass.ds(2 * s, 1)], engines=(engine,), min_val=0,
                                                                max_val=EPAIRS - 1)[1][0]

            def tile_of(engine, s):
                return nc.values_load_multi_w_load_instructions(walk[0:1, bass.ds(2 * s + 1, 1)], engines=(engine,),
                                                                min_val=0, max_val=TILES - 1)[1][0]

            @block.scalar
            def _(act):
                def fetch(s, u):
                    pair = pair_of(mybir.EngineType.Activation, s)
                    if not early(s, 4):
                        act.wait_ge(s_eo, s - 3)
                    act.copy(w1[:, u, :, :], w["moe_w1"][:, :, bass.ds(pair * P, P)]).then_inc(s_w1, 1)
                    act.copy(b1[:, u:u + 1], w["moe_b1"][:, bass.ds(pair, 1)]).then_inc(s_w1, 1)
                    act.copy(mask[:, u, :], moe_mask[:, bass.ds(pair * P, P)]).then_inc(s_w1, 1)
                    act.copy(w2[:, u, :], w["moe_w2"][:].rearrange("p m c -> p (m c)")[:, bass.ds(pair * C, C)]
                             ).then_inc(s_w1, 1)

                def relu(s, u):
                    act.wait_ge(s_hid, s + 1)
                    act.wait_ge(s_w1, COPIES * (s + 1))
                    if not early(s, 4):
                        act.wait_ge(s_eo, s - 3)
                    act.activation(hidden[:, u, :], bank[u % 2][:, 0:P], ACT.Relu, bias=b1[:, u:u + 1]).then_inc(s_relu, 1)
                pipeline(act, MOE_RUN, 4, [(0, fetch), (2, relu)])

            @block.tensor
            def _(pe):
                def hide(s, u):
                    tile = tile_of(mybir.EngineType.PE, s)
                    pe.wait_ge(s_w1, COPIES * (s + 1))
                    if not early(s, 2):
                        pe.wait_ge(s_relu, s - 1)
                    for k in range(KC):
                        pe.matmul(bank[u % 2][:, 0:P], w1[:, u, k, :], rows_t[:, bass.ds(tile * C + k * P, P)],
                                  start=(k == 0), stop=False)
                    pe.matmul(bank[u % 2][:, 0:P], mask[:, u, :], picks_t[:, bass.ds(tile * P, P)],
                              start=False, stop=True).then_inc(s_hid, 1)

                def put_out(s, u):
                    pe.wait_ge(s_relu, s + 1)
                    if not early(s, 2):
                        pe.wait_ge(s_add, s - 1)
                    pe.matmul(bank[2 + u % 2][:, 0:C], hidden[:, u, :], w2[:, u, :],
                              start=True, stop=True).then_inc(s_eo, 1)
                pipeline(pe, MOE_RUN, 4, [(3, put_out), (1, hide)])

            @block.vector
            def _(dve):
                def add(s, u):
                    tile = tile_of(mybir.EngineType.DVE, s)
                    dve.wait_ge(s_eo, s + 1)
                    if not early(s, 1):
                        dve.wait_ge(s_add, s)
                    row = total[:, bass.ds(tile * C, C)]
                    dve.tensor_tensor(row, row, bank[2 + u % 2][:, 0:C], ALU.add).then_inc(s_add, 1)
                pipeline(dve, MOE_RUN, 4, [(3, add)])
                dve.wait_ge(s_add, MOE_RUN)

        s_out, s_idx, s_done = sem("l_outputs_stored"), sem("l_place_ready"), sem("l_rows_done")
        s_land = [sem(f"l_outputs_landed{u}") for u in range(4)]
        s_store = [sem(f"l_rows_stored{u}") for u in range(4)]
        with ExitStack() as scope:
            def sc(name, shape, dt=F32):
                return scope.enter_context(nc.sbuf_tensor(name, shape, dt))
            index, got, res = sc("l_index", [P, 4], U32), sc("l_got", [P, 4, C]), sc("l_res", [P, 4, C])
            block = scope.enter_context(nc.Block())

            @block.sync
            def _(sp):
                sp.dma_start(out_dram.rearrange("(t p) c -> p t c", p=P),
                             total[:, 0:TILES * C].rearrange("p (t c) -> p t c", c=C)).then_inc(s_out, 16)

                def store(t, u):
                    sp.wait_ge(s_done, t + 1)
                    sp.dma_start(out_rows[:, bass.ds(t, 1), :], res[:, u:u + 1, :]).then_inc(s_store[u], 16)
                pipeline(sp, TILES, 4, [(0, store)])
                for u in range(4):
                    sp.wait_ge(s_store[u], 16 * len(range(u, TILES, 4)))

            @block.scalar
            def _(act):
                def fetch_index(t, u):
                    if not early(t, 4):
                        fence(act, s_land[u], landed(t, u, 4) - 16)
                    act.copy(index[:, u:u + 1], place[:, bass.ds(t, 1)]).then_inc(s_idx, 1)
                pipeline(act, TILES, 4, [(0, fetch_index)])

            @block.gpsimd
            def _(pool):
                pool.wait_ge(s_out, 16)

                def gather(t, u):
                    if not early(t, 4):
                        pool.wait_ge(s_done, t - 3)
                    fence(pool, s_idx, t + 1)
                    pool.indirect_dma_start(out=got[:, u, :], out_offset=None, in_=out_dram,
                                            in_offset=bass.IndirectOffsetOnAxis(ap=index[:, u:u + 1], axis=0)
                                            ).then_inc(s_land[u], 16)
                pipeline(pool, TILES, 4, [(0, gather)])

            @block.vector
            def _(dve):
                def finish(t, u):
                    dve.wait_ge(s_land[u], landed(t, u, 4))
                    if not early(t, 4):
                        dve.wait_ge(s_store[u], landed(t, u, 4) - 16)
                    dve.scalar_tensor_tensor(out=res[:, u, :], in0=got[:, u, :], scalar=0.0,
                                             in1=x[:, bass.ds(t, 1), :].rearrange("p a c -> p (a c)"),
                                             op0=ALU.max, op1=ALU.add).then_inc(s_done, 1)
                pipeline(dve, TILES, 4, [(0, finish)])
        hs.close()


OUT_SHAPE = (ROWS, C)


def kernel(**inputs):
    import ml_dtypes
    import concourse.bacc as bacc
    from concourse.bass_utils import run_bass_kernel_spmd

    g = {k: np.asarray(v) for k, v in inputs.items()}

    def by_channel(m):
        return m.reshape(-1, P, m.shape[1]).transpose(1, 0, 2)

    pad = STEP_TABLE * P - EDGES
    src = np.pad(g["src"].astype(np.int32), (0, pad)).reshape(STEP_TABLE, P)
    dst = np.pad(g["dst"].astype(np.int32), (0, pad), constant_values=PAD_DST).reshape(STEP_TABLE, P)
    moe_w1 = g["L1_ffn_W1"].transpose(1, 0, 2).reshape(C, EXPERTS * HID)
    mask = np.where(np.arange(EXPERTS * HID)[None] // HID == np.arange(EXPERTS)[:, None], 0.0, -1e30)
    arrays = {
        "x": np.pad(g["x"], ((0, ROWS - NODES), (0, 0))),
        "edge_rows": np.concatenate([src, dst], axis=1),
        "l0_w1t": by_channel(g["L0_gnn_W1"].T), "l0_w2t": by_channel(g["L0_gnn_W2"].T),
        "l0_fx": by_channel(g["L0_ffn_W_fx"]),
        "w_xt": g["L0_ffn_W_x"].T.reshape(H0, D0, C).transpose(1, 0, 2),
        "b_x": g["L0_ffn_b_x"].reshape(H0, D0).T,
        "w_slice": g["L0_ffn_W_slice"], "w_q": g["L0_ffn_W_q"], "w_k": g["L0_ffn_W_k"], "w_v": g["L0_ffn_W_v"],
        "b_fx_row": g["L0_ffn_b_fx"][None],
        "l0_slice_out": g["L0_ffn_W_out"].reshape(H0, D0, C).transpose(1, 0, 2),
        "l1_qt": by_channel(g["L1_gnn_Wq"].T),
        "l1_kvt": by_channel(np.concatenate([g["L1_gnn_Wk"].T, g["L1_gnn_Wv"].T], axis=1)),
        "l1_pt": by_channel(g["L1_gnn_Wp"].T),
        "l1_w1t": by_channel(g["L1_gnn_W1"].T), "l1_w2t": by_channel(g["L1_gnn_W2"].T),
        "l1_b1": g["L1_gnn_b1"].reshape(MC, P).T,
        "ln_g": g["L1_gnn_ln_g"].reshape(KC, P).T, "ln_b": g["L1_gnn_ln_b"].reshape(KC, P).T,
        "router_t": by_channel(g["L1_ffn_router_w"].T),
        "moe_w1": by_channel(moe_w1), "moe_b1": g["L1_ffn_b1"].reshape(EC, P).T,
        "moe_w2": by_channel(g["L1_ffn_W2"].reshape(EXPERTS * HID, C)), "moe_b2": g["L1_ffn_b2"],
        "moe_mask": mask.astype(ml_dtypes.bfloat16),
        "b1": g["L0_gnn_b1"][None], "b2": g["L0_gnn_b2"][None], "b_slice": g["L0_ffn_b_slice"][None],
        "b_out": g["L0_ffn_b_out"][None], "bq": g["L1_gnn_bq"][None],
        "bkv": np.concatenate([g["L1_gnn_bk"], g["L1_gnn_bv"]])[None],
        "bp": g["L1_gnn_bp"][None], "b2m": g["L1_gnn_b2"][None], "router_b": g["L1_ffn_router_b"][None],
        "temperature": g["L0_ffn_temperature"].reshape(1, H0),
    }
    arrays = {k: np.ascontiguousarray(v) for k, v in arrays.items()}
    nc = bacc.Bacc("TRN2", target_bir_lowering=False, num_devices=1)
    aps = {k: nc.dram_tensor("in_" + k, v.shape, mybir.dt.from_np(v.dtype), kind="ExternalInput").ap()
           for k, v in arrays.items()}
    out = nc.dram_tensor("out_rows", OUT_SHAPE, F32, kind="ExternalOutput").ap()
    build(nc, aps, out)
    r = run_bass_kernel_spmd(nc, [{"in_" + k: v for k, v in arrays.items()}], core_ids=[0])
    return r.results[0]["out_rows"][:NODES]
```
